# Optimizing a Trainium2 kernel written in Bass

```python
import numpy as np
import jax
import jax.numpy as jnp

def _softmax(x, axis=-1):
    return jax.nn.softmax(x, axis=axis)

def _gelu(x):
    return jax.nn.gelu(x, approximate=True)

def _silu(x):
    return jax.nn.silu(x)

def _sigmoid(x):
    return jax.nn.sigmoid(x)

def _layernorm(x, axis=-1, eps=1e-05):
    m = jnp.mean(x, axis=axis, keepdims=True)
    v = jnp.var(x, axis=axis, keepdims=True)
    return (x - m) / jnp.sqrt(v + eps)

def _scatter_add(tgt, idx, src, axis=0):
    return tgt.at[idx].add(src)

def _segment_sum(src, seg, n):
    return jax.ops.segment_sum(src, seg, n)
kernel_name = 'mk_cond_seq_d2_seqx_r4_09f540'

def setup_inputs(seed: int=0):
    np.random.seed(seed)
    _w = jnp.asarray

    def _rec_inputs():
        import jax
        import jax.numpy as jnp
        _rk = jax.random.key(seed)
        x = 7.22e-05 + 1 * jax.random.normal(jax.random.fold_in(_rk, 1), (16, 256, 512), jnp.float32)
        _lenS = 256 - jax.random.randint(jax.random.fold_in(_rk, 7), (16,), 0, max(1, 256 // 4) + 1, jnp.int32)
        _lenS2 = 256 - jax.random.randint(jax.random.fold_in(_rk, 8), (16,), 0, max(1, 256 // 4) + 1, jnp.int32)
        cond_2048 = 0.0061147 + 1.02565 * jax.random.normal(jax.random.fold_in(_rk, 11), (16, 512), jnp.float32)
        pos_BxS = jnp.broadcast_to(jnp.arange(256, dtype=jnp.int32), (16, 256))
        return (x, cond_2048, pos_BxS)
    x, cond_2048, pos_BxS = _rec_inputs()

    def _L0_cond_setup():
        import jax, jax.numpy as jnp
        import numpy as np
        D_MODEL = 512
        N_HEADS = 16
        N_KV_HEADS = 4
        HEAD_DIM = D_MODEL // N_HEADS
        N_GROUPS = N_HEADS // N_KV_HEADS
        BLOCK_SIZE = 128
        WINDOW = 64
        GLOBAL_EVERY = 64
        LATENT = 128
        ROPE_THETA = 10000.0
        LN_EPS = 1e-05

        def _rope_tables(T, dtype):
            freqs = 1.0 / ROPE_THETA ** (jnp.arange(0, HEAD_DIM, 2, dtype=jnp.float32) / HEAD_DIM)
            emb = jnp.arange(T, dtype=jnp.float32)[:, None] * freqs[None, :]
            cos = jnp.concatenate([jnp.cos(emb), jnp.cos(emb)], axis=-1).astype(dtype)
            sin = jnp.concatenate([jnp.sin(emb), jnp.sin(emb)], axis=-1).astype(dtype)
            return (cos, sin)

        def _rotate_half(x):
            h = x.shape[-1] // 2
            return jnp.concatenate([-x[..., h:], x[..., :h]], axis=-1)

        def _sparse_mask(T):
            idx = jnp.arange(T)
            blk = idx // BLOCK_SIZE
            future_block = blk[None, :] > blk[:, None]
            outside_window = jnp.abs(idx[None, :] - idx[:, None]) > WINDOW
            global_visible = jnp.broadcast_to((idx % GLOBAL_EVERY == 0)[None, :], (T, T))
            return outside_window & ~global_visible | future_block
        key = jax.random.key(seed)
        ks = jax.random.split(key, 9)
        B, T = (2, 512)
        s = 0.02
        return {'x': jax.random.normal(ks[0], (B, T, D_MODEL), jnp.float32), 't_emb': jax.random.normal(ks[1], (B, D_MODEL), jnp.float32), 'W_ada': jax.random.normal(ks[2], (2 * D_MODEL, D_MODEL), jnp.float32) * s, 'b_ada': jnp.zeros((2 * D_MODEL,), jnp.float32), 'Wq': jax.random.normal(ks[3], (N_HEADS * HEAD_DIM, D_MODEL), jnp.float32) * s, 'Wkd': jax.random.normal(ks[4], (LATENT, D_MODEL), jnp.float32) * s, 'Wku': jax.random.normal(ks[5], (N_KV_HEADS * HEAD_DIM, LATENT), jnp.float32) * s, 'Wvu': jax.random.normal(ks[6], (N_KV_HEADS * HEAD_DIM, LATENT), jnp.float32) * s, 'Wo': jax.random.normal(ks[7], (D_MODEL, N_HEADS * HEAD_DIM), jnp.float32) * s}
    _L0_cond_all = _L0_cond_setup()
    _L0_cond_in = {k: v for k, v in _L0_cond_all.items() if k in ('W_ada', 'b_ada', 'Wq', 'Wkd', 'Wku', 'Wvu', 'Wo')}
    del _L0_cond_all

    def _L1_cond_setup():
        import jax, jax.numpy as jnp
        import numpy as np
        HIDDEN, NQ, NKV, HD, INTER = (512, 8, 1, 64, 2048)
        B, S = (4, 512)
        EPS = 1e-06
        ROPE_BASE = 10000.0

        def ada_rms(x, t, w, tw):
            n = x * jax.lax.rsqrt(jnp.mean(jnp.square(x), axis=-1, keepdims=True) + EPS)
            scale = t @ tw.T
            return n * (w * (1.0 + scale))[:, None, :]

        def apply_rope(x, pos_ids):
            half = HD // 2
            inv_freq = 1.0 / ROPE_BASE ** (jnp.arange(0, HD, 2, dtype=jnp.float32) / HD)
            ang = pos_ids.astype(jnp.float32)[:, :, None] * inv_freq
            cos = jnp.concatenate([jnp.cos(ang), jnp.cos(ang)], axis=-1)[:, None]
            sin = jnp.concatenate([jnp.sin(ang), jnp.sin(ang)], axis=-1)[:, None]
            x1, x2 = (x[..., :half], x[..., half:])
            rot = jnp.concatenate([-x2, x1], axis=-1)
            return x * cos + rot * sin
        key = jax.random.key(seed)
        ks = jax.random.split(key, 12)
        f32 = jnp.float32
        inp = {'x': jax.random.normal(ks[0], (B, S, HIDDEN), f32), 'pos_ids': jnp.broadcast_to(jnp.arange(S, dtype=jnp.int32), (B, S)), 'time_emb': jax.random.normal(ks[1], (B, HIDDEN), f32), 'ln1_w': jnp.ones((HIDDEN,), f32), 'ln1_tw': jax.random.normal(ks[2], (HIDDEN, HIDDEN), f32) * 0.02, 'ln2_w': jnp.ones((HIDDEN,), f32), 'ln2_tw': jax.random.normal(ks[3], (HIDDEN, HIDDEN), f32) * 0.02, 'Wq': jax.random.normal(ks[4], (NQ * HD, HIDDEN), f32) * 0.02, 'Wk': jax.random.normal(ks[5], (NKV * HD, HIDDEN), f32) * 0.02, 'Wv': jax.random.normal(ks[6], (NKV * HD, HIDDEN), f32) * 0.02, 'Wo': jax.random.normal(ks[7], (HIDDEN, NQ * HD), f32) * 0.02, 'Wg': jax.random.normal(ks[8], (INTER, HIDDEN), f32) * 0.02, 'Wu': jax.random.normal(ks[9], (INTER, HIDDEN), f32) * 0.02, 'Wd': jax.random.normal(ks[10], (HIDDEN, INTER), f32) * 0.02}
        return inp
    _L1_cond_all = _L1_cond_setup()
    _L1_cond_in = {k: v for k, v in _L1_cond_all.items() if k in ('ln1_w', 'ln1_tw', 'ln2_w', 'ln2_tw', 'Wq', 'Wk', 'Wv', 'Wo', 'Wg', 'Wu', 'Wd')}
    del _L1_cond_all
    return {'x': x, 'cond_2048': cond_2048, 'pos_BxS': pos_BxS, 'L0_cond_W_ada': _L0_cond_in['W_ada'], 'L0_cond_b_ada': _L0_cond_in['b_ada'], 'L0_cond_Wq': _L0_cond_in['Wq'], 'L0_cond_Wkd': _L0_cond_in['Wkd'], 'L0_cond_Wku': _L0_cond_in['Wku'], 'L0_cond_Wvu': _L0_cond_in['Wvu'], 'L0_cond_Wo': _L0_cond_in['Wo'], 'L1_cond_ln1_w': _L1_cond_in['ln1_w'], 'L1_cond_ln1_tw': _L1_cond_in['ln1_tw'], 'L1_cond_ln2_w': _L1_cond_in['ln2_w'], 'L1_cond_ln2_tw': _L1_cond_in['ln2_tw'], 'L1_cond_Wq': _L1_cond_in['Wq'], 'L1_cond_Wk': _L1_cond_in['Wk'], 'L1_cond_Wv': _L1_cond_in['Wv'], 'L1_cond_Wo': _L1_cond_in['Wo'], 'L1_cond_Wg': _L1_cond_in['Wg'], 'L1_cond_Wu': _L1_cond_in['Wu'], 'L1_cond_Wd': _L1_cond_in['Wd']}

def reference(x, cond_2048, pos_BxS, L0_cond_W_ada, L0_cond_b_ada, L0_cond_Wq, L0_cond_Wkd, L0_cond_Wku, L0_cond_Wvu, L0_cond_Wo, L1_cond_ln1_w, L1_cond_ln1_tw, L1_cond_ln2_w, L1_cond_ln2_tw, L1_cond_Wq, L1_cond_Wk, L1_cond_Wv, L1_cond_Wo, L1_cond_Wg, L1_cond_Wu, L1_cond_Wd):
    import jax
    import jax.numpy as jnp

    def _L0_cond_ref(x, t_emb, W_ada, b_ada, Wq, Wkd, Wku, Wvu, Wo):
        import jax, jax.numpy as jnp
        import numpy as np
        D_MODEL = 512
        N_HEADS = 16
        N_KV_HEADS = 4
        HEAD_DIM = D_MODEL // N_HEADS
        N_GROUPS = N_HEADS // N_KV_HEADS
        BLOCK_SIZE = 128
        WINDOW = 64
        GLOBAL_EVERY = 64
        LATENT = 128
        ROPE_THETA = 10000.0
        LN_EPS = 1e-05

        def _rope_tables(T, dtype):
            freqs = 1.0 / ROPE_THETA ** (jnp.arange(0, HEAD_DIM, 2, dtype=jnp.float32) / HEAD_DIM)
            emb = jnp.arange(T, dtype=jnp.float32)[:, None] * freqs[None, :]
            cos = jnp.concatenate([jnp.cos(emb), jnp.cos(emb)], axis=-1).astype(dtype)
            sin = jnp.concatenate([jnp.sin(emb), jnp.sin(emb)], axis=-1).astype(dtype)
            return (cos, sin)

        def _rotate_half(x):
            h = x.shape[-1] // 2
            return jnp.concatenate([-x[..., h:], x[..., :h]], axis=-1)

        def _sparse_mask(T):
            idx = jnp.arange(T)
            blk = idx // BLOCK_SIZE
            future_block = blk[None, :] > blk[:, None]
            outside_window = jnp.abs(idx[None, :] - idx[:, None]) > WINDOW
            global_visible = jnp.broadcast_to((idx % GLOBAL_EVERY == 0)[None, :], (T, T))
            return outside_window & ~global_visible | future_block
        B, T, C = x.shape
        proj = t_emb @ W_ada.T + b_ada
        scale, shift = (proj[:, :C], proj[:, C:])
        mu = jnp.mean(x, axis=-1, keepdims=True)
        var = jnp.mean(jnp.square(x - mu), axis=-1, keepdims=True)
        h = (x - mu) * jax.lax.rsqrt(var + LN_EPS)
        h = h * (1.0 + scale[:, None, :]) + shift[:, None, :]
        q = (h @ Wq.T).reshape(B, T, N_HEADS, HEAD_DIM).transpose(0, 2, 1, 3)
        c_kv = h @ Wkd.T
        k = (c_kv @ Wku.T).reshape(B, T, N_KV_HEADS, HEAD_DIM).transpose(0, 2, 1, 3)
        v = (c_kv @ Wvu.T).reshape(B, T, N_KV_HEADS, HEAD_DIM).transpose(0, 2, 1, 3)
        cos, sin = _rope_tables(T, x.dtype)
        cos, sin = (cos[None, None], sin[None, None])
        q = q * cos + _rotate_half(q) * sin
        k = k * cos + _rotate_half(k) * sin
        k_exp = jnp.repeat(k, N_GROUPS, axis=1)
        v_exp = jnp.repeat(v, N_GROUPS, axis=1)
        mask = _sparse_mask(T)
        scores = jnp.einsum('bhtd,bhsd->bhts', q, k_exp) / jnp.sqrt(jnp.asarray(HEAD_DIM, x.dtype))
        scores = jnp.where(mask[None, None], jnp.asarray(-jnp.inf, x.dtype), scores)
        attn = jax.nn.softmax(scores, axis=-1)
        y = jnp.einsum('bhts,bhsd->bhtd', attn, v_exp)
        out = y.transpose(0, 2, 1, 3).reshape(B, T, C) @ Wo.T
        return x + out

    def _L1_cond_ref(x, pos_ids, time_emb, ln1_w, ln1_tw, ln2_w, ln2_tw, Wq, Wk, Wv, Wo, Wg, Wu, Wd):
        import jax, jax.numpy as jnp
        import numpy as np
        HIDDEN, NQ, NKV, HD, INTER = (512, 8, 1, 64, 2048)
        B, S = (4, 512)
        EPS = 1e-06
        ROPE_BASE = 10000.0

        def ada_rms(x, t, w, tw):
            n = x * jax.lax.rsqrt(jnp.mean(jnp.square(x), axis=-1, keepdims=True) + EPS)
            scale = t @ tw.T
            return n * (w * (1.0 + scale))[:, None, :]

        def apply_rope(x, pos_ids):
            half = HD // 2
            inv_freq = 1.0 / ROPE_BASE ** (jnp.arange(0, HD, 2, dtype=jnp.float32) / HD)
            ang = pos_ids.astype(jnp.float32)[:, :, None] * inv_freq
            cos = jnp.concatenate([jnp.cos(ang), jnp.cos(ang)], axis=-1)[:, None]
            sin = jnp.concatenate([jnp.sin(ang), jnp.sin(ang)], axis=-1)[:, None]
            x1, x2 = (x[..., :half], x[..., half:])
            rot = jnp.concatenate([-x2, x1], axis=-1)
            return x * cos + rot * sin
        b, s, _ = x.shape
        g = NQ // NKV
        res = x
        h = ada_rms(x, time_emb, ln1_w, ln1_tw)
        q = (h @ Wq.T).reshape(b, s, NQ, HD).transpose(0, 2, 1, 3)
        k = (h @ Wk.T).reshape(b, s, NKV, HD).transpose(0, 2, 1, 3)
        v = (h @ Wv.T).reshape(b, s, NKV, HD).transpose(0, 2, 1, 3)
        q = apply_rope(q, pos_ids)
        k = apply_rope(k, pos_ids)
        qg = q.reshape(b, NKV, g, s, HD)
        scores = jnp.einsum('bkgsd,bktd->bkgst', qg, k) / jnp.sqrt(jnp.float32(HD))
        attn = jax.nn.softmax(scores, axis=-1)
        ctx = jnp.einsum('bkgst,bktd->bkgsd', attn, v)
        ctx = ctx.reshape(b, NQ, s, HD).transpose(0, 2, 1, 3).reshape(b, s, NQ * HD)
        x = res + ctx @ Wo.T
        res = x
        h = ada_rms(x, time_emb, ln2_w, ln2_tw)
        mlp = jax.nn.silu(h @ Wg.T) * (h @ Wu.T) @ Wd.T
        return res + mlp
    x = _L0_cond_ref(x, cond_2048, L0_cond_W_ada, L0_cond_b_ada, L0_cond_Wq, L0_cond_Wkd, L0_cond_Wku, L0_cond_Wvu, L0_cond_Wo)
    x = _L1_cond_ref(x, pos_BxS, cond_2048, L1_cond_ln1_w, L1_cond_ln1_tw, L1_cond_ln2_w, L1_cond_ln2_tw, L1_cond_Wq, L1_cond_Wk, L1_cond_Wv, L1_cond_Wo, L1_cond_Wg, L1_cond_Wu, L1_cond_Wd)
    return x

_drawn_inputs = setup_inputs


def setup_inputs(seed=0):
    import zlib

    import numpy as np

    out = dict(_drawn_inputs(seed))
    spreads = {'L0_cond_b_ada': (0.0, 0.8), 'L1_cond_ln1_w': (1.0, 0.6), 'L1_cond_ln2_w': (1.0, 0.6)}
    factors = {'L0_cond_Wq': 8.0,
     'L0_cond_Wku': 8.0,
     'L1_cond_ln1_tw': 8.0,
     'L1_cond_Wq': 8.0,
     'L1_cond_Wk': 8.0,
     'L1_cond_Wv': 3.531,
     'L1_cond_Wo': 3.527,
     'L1_cond_ln2_tw': 8.0,
     'L1_cond_Wg': 6.418,
     'L1_cond_Wu': 6.269,
     'L1_cond_Wd': 6.262}
    for name, (base, spread) in spreads.items():
        noise = np.random.default_rng([zlib.crc32(name.encode()), seed]).standard_normal(out[name].shape)
        drawn = base * np.exp(spread * noise) if base else spread * noise
        out[name] = jnp.asarray(drawn.astype(out[name].dtype))
    for name, factor in factors.items():
        out[name] = (out[name] * factor).astype(out[name].dtype)
    return out
```

```python
from contextlib import ExitStack

import numpy as np

import concourse.bass as bass
from concourse import mybir

ALU = mybir.AluOpType
ACT = mybir.ActivationFunctionType
AX = mybir.AxisListType
F32 = mybir.dt.float32
F16 = mybir.dt.float16
I32 = mybir.dt.int32

P = 128
SEQS, TOK, D = 16, 256, 512
TILES = TOK // P
CH = D // P
FF = 2048
FCH = FF // P
PAIRS = FCH // 2
H0, KV0, HD0 = 16, 4, 32
H1, HD1 = 8, 64
LAT = 128
WINDOW, GLOBAL = 64, 64
LN_EPS, RMS_EPS = 1e-5, 1e-6
WS = 64.0
HS = 1.0 / 16.0
NEG = 1.0e30
K_OWN, K_NEAR = P, WINDOW + 1
K_TWO = K_OWN + K_NEAR
TAB = 3 * HD1 // 2
ROUND = 1.5 * 2.0 ** 23
TWO_PI_1, TWO_PI_2 = 6.28125, 0.00193500518798828125
TWO_PI_3 = float(2 * np.pi - TWO_PI_1 - TWO_PI_2)
PI_IN = 3.1415925

UNITS0, UNITS1 = 12, 8
UNITS = UNITS0 + UNITS1
S_READ = ([("lat_low", 1, 1), ("rope_terms", 6, 1), ("near_low", 1, 1)]
          + [("terms_made", UNITS, u + 1) for u in range(UNITS0)]
          + [("mid_ready", 4, 1), ("mid_ready", 4, 2), ("rope_terms", 6, 4)]
          + [("terms_made", UNITS, UNITS0 + u + 1) for u in range(UNITS1)]
          + [("mid_ready", 4, 3), ("mid_ready", 4, 4)])
S_USES = len(S_READ)
S_LAT, S_KV, S_NEAR, S_UNIT0 = range(4)
S_OUT0 = S_UNIT0 + UNITS0
S_KV1 = S_OUT0 + TILES
S_UNIT1 = S_KV1 + 1
S_OUT1 = S_UNIT1 + UNITS1
T_FILL0, T_K0, T_Q0, T_UNIT0 = 0, 2, 3, 7
T_K1 = T_UNIT0 + UNITS0 + 4
T_Q1, T_UNIT1 = T_K1 + 1, T_K1 + 3
T_FILL = [T_FILL0, T_K1 - 4, T_K1 - 2, T_UNIT1 + UNITS1, T_UNIT1 + UNITS1 + 2]
T_USES = T_FILL[4] + 2
HI_FILL = [0, 2 + UNITS0, 4 + UNITS0, 6 + UNITS, 8 + UNITS]
HI_UNIT = [2, 6 + UNITS0]
HI_USES = 10 + UNITS


def count(n, per, k):
    i, off = n
    return off * per + k if i is None else i * per + (off * per + k)


def need(eng, sem, value):
    if isinstance(value, int) and value <= 0:
        return
    eng.wait_ge(sem, value)


def need_apart(eng, sem, value, met):
    if isinstance(value, int):
        need(eng, sem, value)
        return
    value = eng.to_reg(value)
    eng.wait_ge(*met)
    eng.wait_ge(sem, value)


def index(n):
    i, off = n
    return off if i is None else i + off


def before(n, use, uses):
    return (n, use - 2) if use >= 2 else ((n[0], n[1] - 1), use - 2 + uses)


def unit_heads(layer, u):
    if layer == 0:
        group, kind = divmod(u, 3)
        if kind == 0:
            return [(4 * group + j, 0, j * P, P) for j in range(4)]
        return [(4 * group + 2 * (kind - 1) + j, 1, 2 * j * P, K_TWO) for j in range(2)]
    pair, t = divmod(u, TILES)
    return [(2 * pair + j, t, j * TOK, TOK) for j in range(2)]


def build(nc, x, cond_t, pos_t, w_ada_t, b_ada_t, wq0_t, wkd_t, wku_t, wvu_t, wo0_t, ln1_w, tw1_t,
          ln2_w, tw2_t, wq1_t, wk1_t, wv1_t, wo1_t, wg_t, wu_t, wd_t, mask_c, rope0_c, freq_c, rope1,
          out):
    with ExitStack() as ctx:
        def sb(name, shape, dt=F32):
            return ctx.enter_context(nc.sbuf_tensor(name, shape, dt))

        def sem(name):
            return ctx.enter_context(nc.semaphore(name))

        def weight(name, chunks, cols):
            return (sb(name + "_hi", [P, chunks, cols], F16), sb(name + "_lo", [P, chunks, cols], F16))

        wkd = weight("wkd", CH, LAT)
        wkv0 = weight("wkv0", 1, 2 * KV0 * HD0)
        wq0 = weight("wq0", CH, D)
        wo0 = weight("wo0", CH, D)
        wkv1 = weight("wkv1", CH, 2 * HD1)
        wq1 = weight("wq1", CH, D)
        wo1 = weight("wo1", CH, D)
        wg = weight("wg", CH, FF)
        wu = weight("wu", CH, FF)
        wd = weight("wd", FCH, D)

        x_in = sb("x_in", [P, TILES, D])
        x_mid = sb("x_mid", [P, TILES, D])
        x_res = sb("x_res", [P, TILES, D])
        work = sb("work", [P, TILES, D])
        act_t = (sb("act_hi", [P, CH, TOK], F16), sb("act_lo", [P, CH, TOK], F16))
        mlp_t = (sb("mlp_hi", [P, CH, TOK], F16), sb("mlp_lo", [P, CH, TOK], F16))
        lat = (sb("lat_hi", [P, WINDOW + TOK], F16), sb("lat_lo", [P, WINDOW + TOK], F16))
        stack = sb("stack", [P, 2048], F16)
        q_t = sb("q_t", [P, H0, TOK], F16)
        k0_t = sb("k0_t", [P, KV0, P + WINDOW + P], F16)
        v0 = (sb("v0_hi", [P, 3, P], F16), sb("v0_lo", [P, 3, P], F16))
        k1_t = k0_t[:].rearrange("p g k -> p (g k)")[:, 0:2 * TOK].rearrange("p (a k) -> p a k", a=2)
        v1 = tuple(v[:, 0, :].rearrange("p (t d) -> p t d", t=TILES) for v in v0)
        prob = sb("prob", [P, 2, 512])
        prob_t = (sb("prob_hi", [P, 2, 512], F16), sb("prob_lo", [P, 2, 512], F16))
        low = sb("low", [P, 2, 4])
        sums0 = sb("sums0", [P, TILES, H0])
        sums1 = sb("sums1", [P, TILES, H1])
        inv = sb("inv", [P, TILES, H0])
        silu = sb("silu", [P, 512])
        inner = sb("inner", [P, 512])
        inner_t = sb("inner_t", [P, 2, FCH, TOK], F16)
        mask = sb("mask", [P, K_TWO])
        rope0 = sb("rope0", [P, 2, TILES, 2, HD0])
        rope1_sb = sb("rope1_sb", [P, TILES, TAB])
        ident = sb("ident", [P, P])
        ident16 = sb("ident16", [P, P], F16)
        bn = sb("bn", [P, TILES, 6])
        moments = sb("moments", [P, TILES, 2])
        squares = sb("squares", [P, TILES])
        shifted = sb("shifted", [P, TILES])
        rstd = sb("rstd", [P, TILES])
        minus_half = sb("minus_half", [P, TILES])
        gain0 = sb("gain0", [P, CH, SEQS])
        bias0 = sb("bias0", [P, CH, SEQS])
        gain1 = sb("gain1", [P, CH, SEQS])
        gain2 = sb("gain2", [P, CH, SEQS])
        b_ada = sb("b_ada", [P, 2 * CH])
        ln_w = sb("ln_w", [P, 2, CH])
        cond = silu[:, 0:CH * SEQS].rearrange("p (c s) -> p c s", c=CH)
        freq = silu[:, 64:64 + HD1 // 2]
        posf = silu[:, 128:128 + SEQS * TILES]
        pos = silu[:, 192:192 + SEQS * TILES].bitcast(I32)

        def bank(name):
            return ctx.enter_context(nc.psum_tensor(name, [P, 512], F32))

        score = [bank("score0"), bank("score1")]
        trans = [bank("trans0"), bank("trans1")]
        ybank = [bank("y0"), bank("y1")]
        gbank, ubank = bank("gate"), bank("up")

        stage = inner_t[:].rearrange("p a c t -> p (a c t)").bitcast(F32).rearrange(
            "p (s n) -> p s n", s=2)
        normed = stack[:].bitcast(F32)
        k_stack0 = stack[:, 0:1024].rearrange("p (g a d) -> p g a d", a=4, d=HD0)
        q_stack0 = stack[:].rearrange("p (h a d) -> p h a d", a=4, d=HD0)
        k_stack1 = stack[:, 0:512].rearrange("p (t a d) -> p t a d", a=4, d=HD1)
        q_stack1 = [stack[:, at:at + 1024].rearrange("p (h a d) -> p h a d", a=2, d=HD1)
                    for at in (1024, 0)]
        turns = work[:].rearrange("p t d -> p (t d)")
        reduced = x_mid[:].rearrange("p t d -> p (t d)")
        early = q_t[:].rearrange("p h t -> p (h t)").bitcast(F32)
        angle, table = early[:, 0:512], early[:, 512:2048]

        raw_in = [sem("raw_in0"), sem("raw_in1")]
        cond_in, const_in, pos_in = sem("cond_in"), sem("const_in"), sem("pos_in")
        raw_high, raw_split, cond_used = sem("raw_high"), sem("raw_split"), sem("cond_used")
        gains_made, ident_zero, ident_made = sem("gains_made"), sem("ident_zero"), sem("ident_made")
        half_made, prob_clear = sem("half_made"), sem("prob_clear")
        angle_step, angle_ready, sines, table_made, table_out = (
            sem("angle_step"), sem("angle_ready"), sem("sines"), sem("table_made"), sem("table_out"))
        x_arrived, rope_arrived, res_copied, out_stored = (
            sem("x_arrived"), sem("rope_arrived"), sem("res_copied"), sem("out_stored"))
        bn_raw, ln_stat, square_sum, eps_added, rstd_ready = (
            sem("bn_raw"), sem("ln_stat"), sem("square_sum"), sem("eps_added"), sem("rstd_ready"))
        work_ready, t_full, t_free, hi_done, norm_high = (
            sem("work_ready"), sem("t_full"), sem("t_free"), sem("hi_done"), sem("norm_high"))
        s_full, lat_low, near_low, terms_made = (
            sem("s_full"), sem("lat_low"), sem("near_low"), sem("terms_made"))
        y_full, weighted = sem("y_full"), sem("weighted")
        lat_high, v_high = sem("lat_high"), sem("v_high")
        rope_terms, rope_sum, stack_high, stack_low, stack_ready = (
            sem("rope_terms"), sem("rope_sum"), sem("stack_high"), sem("stack_low"),
            sem("stack_ready"))
        low_ready, pv_done, inv_ready = sem("low_ready"), sem("pv_done"), sem("inv_ready")
        mid_ready = sem("mid_ready")
        g_full, u_full, silu_done, inner_ready, inner_high, inner_low, d_full, d_read = (
            sem("g_full"), sem("u_full"), sem("silu_done"), sem("inner_ready"), sem("inner_high"),
            sem("inner_low"), sem("d_full"), sem("d_read"))

        def wide(ap):
            return ap.rearrange("(c p) n -> p c n", p=P)

        loads = []
        for part in range(2):
            loads.append([(wide(w_ada_t)[:, :, part * D:(part + 1) * D], CH, D, 0)])
        loads.append([(wide(tw1_t), CH, D, 0)])
        loads.append([(wide(tw2_t), CH, D, 0)])
        raw = len(loads)
        splits = []

        def split(parts, target):
            loads.append(parts)
            splits.append(target)

        n_lat = CH * LAT
        split([(wide(wkd_t), CH, LAT, 0)], [(wkd, 0, n_lat)])
        split([(wku_t, 1, P, 0), (wvu_t, 1, P, P)], [(wkv0, 0, 2 * P)])
        split([(wide(wq0_t), CH, D, 0)], [(wq0, 0, CH * D)])
        split([(wide(wo0_t), CH, D, 0)], [(wo0, 0, CH * D)])
        split([(wide(wk1_t), CH, HD1, 0), (wide(wv1_t), CH, HD1, CH * HD1)], None)
        split([(wide(wq1_t), CH, D, 0)], [(wq1, 0, CH * D)])
        split([(wide(wo1_t), CH, D, 0)], [(wo1, 0, CH * D)])
        for w, w_t in ((wg, wg_t), (wu, wu_t)):
            for c in range(CH):
                split([(w_t[c * P:(c + 1) * P, :], 1, FF, 0)], [(w, c * FF, FF)])
        for c in range(CH):
            split([(wide(wd_t[c * D:(c + 1) * D, :]), CH, D, 0)], [(wd, c * CH * D, CH * D)])

        landed = []
        got = [0, 0]
        for m, parts in enumerate(loads):
            got[m % 2] += 16 * len(parts)
            landed.append((raw_in[m % 2], got[m % 2]))

        def split_views(m, half):
            target = splits[m - raw]
            slot = stage[:, m % 2, :]
            if target is None:
                n = CH * HD1
                return [(slot[:, j * n:(j + 1) * n].rearrange("p (c k) -> p c k", c=CH),
                         wkv1[half][:, :, j * HD1:(j + 1) * HD1]) for j in range(2)]
            (w, at, n), = target
            return [(slot[:, 0:n], w[half][:].rearrange("p c n -> p (c n)")[:, at:at + n])]

        rope_tab = rope1.rearrange("(s t) p n -> s p t n", t=TILES)
        x_dram = x.rearrange("s (t p) d -> s p t d", p=P)
        out_dram = out.rearrange("s (t p) d -> s p t d", p=P)

        block = ctx.enter_context(nc.Block())

        @block.sync
        def _(sp):
            sp.dma_start(cond, cond_t.rearrange("(c p) s -> p c s", p=P)).then_inc(cond_in, 16)
            sp.dma_start(b_ada[:], b_ada_t).then_inc(cond_in, 16)
            sp.dma_start(ln_w[:, 0, :], ln1_w).then_inc(cond_in, 16)
            sp.dma_start(ln_w[:, 1, :], ln2_w).then_inc(cond_in, 16)
            sp.dma_start(pos, pos_t).then_inc(pos_in, 16)
            sp.dma_start(freq, freq_c).then_inc(pos_in, 16)
            for m, parts in enumerate(loads):
                if 2 <= m < raw + 2:
                    sp.wait_ge(cond_used, m - 1)
                elif m >= raw + 2:
                    sp.wait_ge(raw_split, m - raw - 1)
                for src, chunks, cols, at in parts:
                    dst = stage[:, m % 2, at:at + chunks * cols]
                    if chunks > 1:
                        dst = dst.rearrange("p (c n) -> p c n", c=chunks)
                    sp.dma_start(dst, src).then_inc(raw_in[m % 2], 16)
                if m == 1:
                    sp.dma_start(x_in[:], x_dram[0]).then_inc(x_arrived, 16)
                    sp.dma_start(mask[:], mask_c).then_inc(const_in, 16)
                    sp.dma_start(rope0[:].rearrange("p a t c d -> p (a t c d)"), rope0_c).then_inc(
                        const_in, 16)

            def ahead(n):
                need_apart(sp, mid_ready, count(n, 4, 2), (cond_used, 1))
                sp.dma_start(x_in[:], x_dram[index((n[0], n[1] + 1))]).then_inc(x_arrived, 16)
                need_apart(sp, rope_sum, count(n, 6, 6), (cond_used, 1))
                sp.dma_start(rope1_sb[:], rope_tab[index((n[0], n[1] + 1))]).then_inc(
                    rope_arrived, 16)

            def residual(n):
                need(sp, mid_ready, count(n, 4, 4))
                sp.dma_start(x_res[:], x_mid[:]).then_inc(res_copied, 16)

            def store(n):
                for t in range(TILES):
                    need_apart(sp, d_read, count(n, TILES, TILES + t + 1), (cond_used, 1))
                    sp.dma_start(out_dram[index(n)][:, t, :], x_res[:, t, :]).then_inc(
                        out_stored, 16)
                need_apart(sp, out_stored, count(n, 16 * TILES, 16 * TILES), (cond_used, 1))

            sp.wait_ge(table_out, 32)
            sp.dma_start(rope1_sb[:], rope_tab[0]).then_inc(rope_arrived, 16)
            ahead((None, 0))
            with sp.Fori(0, SEQS - 2) as i:
                residual((i, 0))
                store((i, 0))
                ahead((i, 1))
            residual((None, SEQS - 2))
            store((None, SEQS - 2))
            residual((None, SEQS - 1))
            store((None, SEQS - 1))

        @block.gpsimd
        def _(pool):
            pool.memset(ident[:], 0.0).then_inc(ident_zero, 1)
            pool.memset(minus_half[:], -0.5).then_inc(half_made, 1)
            pool.memset(prob[:], 0.0).then_inc(prob_clear, 1)
            pool.wait_ge(ident_zero, 1)
            pool.affine_select(out=ident[:], in_=ident[:], compare_op=ALU.not_equal, fill=1.0,
                               base=0, pattern=[[-1, P]], channel_multiplier=1).then_inc(
                                   ident_made, 1)
            pool.wait_ge(ident_made, 1)
            pool.tensor_copy(ident16[:], ident[:]).then_inc(ident_made, 1)
            pool.wait_ge(half_made, 1)

            def root(n, k):
                if k == 0:
                    need_apart(pool, ln_stat, count(n, 2, 2), (half_made, 1))
                    pool.tensor_scalar(shifted[:], moments[:, :, 1], LN_EPS, 1.0, ALU.add,
                                       ALU.mult).then_inc(eps_added, 1)
                else:
                    need_apart(pool, square_sum, count(n, 4, 2 * k), (half_made, 1))
                    pool.tensor_scalar(shifted[:], squares[:], 1.0 / D, RMS_EPS, ALU.mult,
                                       ALU.add).then_inc(eps_added, 1)
                need(pool, eps_added, count(n, 3, k + 1))
                pool.tensor_tensor(rstd[:], shifted[:], minus_half[:], ALU.pow).then_inc(
                    rstd_ready, 1)

            def inner_lows(n):
                for p in range(PAIRS):
                    need(pool, inner_high, count(n, PAIRS, p + 1))
                    pair = inner_t[:, :, 2 * p:2 * p + 2, :].rearrange("p a c t -> p a (c t)")
                    pool.tensor_tensor(pair[:, 1, :], inner[:], pair[:, 0, :],
                                       ALU.subtract).then_inc(inner_low, 1)

            def roots(n):
                for k in range(3):
                    root(n, k)

            roots((None, 0))
            with pool.Fori(0, SEQS - 1) as i:
                inner_lows((i, 0))
                roots((i, 1))
            inner_lows((None, SEQS - 1))

        @block.scalar
        def _(act):
            def fill(n, f):
                for b in range(2):
                    use = T_FILL[f] + b
                    need(act, t_full, count(n, T_USES, use + 1))
                    for c in (2 * b, 2 * b + 1):
                        src = trans[use % 2][:, (c % 2) * TOK:(c % 2 + 1) * TOK]
                        at = index(n)
                        if f == 0:
                            ins = act.activation(
                                normed[:, c * TOK:(c + 1) * TOK], src, ACT.Identity, scale=gain0[:, c, bass.ds(at, 1)],
                                bias=bias0[:, c, bass.ds(at, 1)])
                        elif f in (1, 3):
                            if c % 2 == 0:
                                act.activation(act_t[0][:, c:c + 2, :].rearrange("p c t -> p (c t)"),
                                               trans[use % 2][:], ACT.Copy).then_inc(hi_done, 1)
                            continue
                        else:
                            g, to = (gain1, act_t) if f == 2 else (gain2, mlp_t)
                            ins = act.activation(to[0][:, c, :], src, ACT.Copy,
                                                 scale=g[:, c, bass.ds(at, 1)])
                        if c % 2 == 1:
                            ins.then_inc(hi_done, 1)

            def exps(n, layer, u):
                base = 0 if layer == 0 else UNITS0
                need(act, low_ready, count(n, UNITS, base + u + 1))
                t_unit = T_UNIT0 if layer == 0 else T_UNIT1
                if u >= 2:
                    need(act, t_full, count(n, T_USES, t_unit + u - 1))
                bank_ = score[((S_UNIT0 if layer == 0 else S_UNIT1) + u) % 2]
                slot = prob[:, u % 2, :]
                for j, (h, t, at, wid) in enumerate(unit_heads(layer, u)):
                    sums = (sums0 if layer == 0 else sums1)[:, t, h:h + 1]
                    ins = act.activation(slot[:, at:at + wid], bank_[:, at:at + wid], ACT.Exp,
                                         bias=low[:, u % 2, j:j + 1], scale=-1.0, accum_out=sums)
                ins.then_inc(terms_made, 1)

            def prob_highs(n, layer, u):
                t_unit = T_UNIT0 if layer == 0 else T_UNIT1
                base = 0 if layer == 0 else UNITS0
                need(act, t_full, count(n, T_USES, t_unit + u + 1))
                need(act, pv_done, count(n, UNITS, base + u - 1))
                act.activation(prob_t[0][:, u % 2, :], trans[(t_unit + u) % 2][:],
                               ACT.Copy).then_inc(hi_done, 1)

            def units(n, layer):
                total = UNITS0 if layer == 0 else UNITS1
                exps(n, layer, 0)
                for u in range(total):
                    if u + 1 < total:
                        exps(n, layer, u + 1)
                    prob_highs(n, layer, u)

            def attention(n):
                fill(n, 0)
                need(act, s_full, count(n, S_USES, S_LAT + 1))
                src = score[S_LAT % 2]
                act.activation(lat[0][:, WINDOW:], src[:, 0:TOK], ACT.Copy, scale=1.0 / WS)
                act.activation(lat[0][:, 0:WINDOW], src[:, P - WINDOW:P], ACT.Copy,
                               scale=1.0 / WS).then_inc(lat_high, 1)
                need(act, s_full, count(n, S_USES, S_KV + 1))
                kv = score[S_KV % 2][:].rearrange("p (t n) -> p t n", t=TILES)
                act.activation(v0[0][:, 0:TILES, :], kv[:, :, P:2 * P], ACT.Copy,
                               scale=1.0 / WS).then_inc(v_high, 1)
                need(act, s_full, count(n, S_USES, S_NEAR + 1))
                act.activation(v0[0][0:K_NEAR, 2, :], score[S_NEAR % 2][0:K_NEAR, 0:P], ACT.Copy,
                               scale=1.0 / WS).then_inc(v_high, 1)
                need(act, rope_sum, count(n, 6, 1))
                act.activation(k_stack0[:, :, 0, :], work[:, 0, 0:2 * P].rearrange(
                    "p (g d) -> p g d", d=HD0), ACT.Copy).then_inc(stack_high, 1)
                for t in range(TILES):
                    need(act, rope_sum, count(n, 6, 2 + t))
                    need(act, t_full, count(n, T_USES, T_Q0 + 2 * t))
                    act.activation(q_stack0[:, :, 0, :], work[:, 0, :].rearrange(
                        "p (h d) -> p h d", d=HD0), ACT.Copy).then_inc(stack_high, 1)
                units(n, 0)
                fill(n, 1)
                square(n, 0)
                fill(n, 2)
                need(act, s_full, count(n, S_USES, S_KV1 + 1))
                kv = score[S_KV1 % 2][:, 0:TILES * P].rearrange("p (t n) -> p t n", t=TILES)
                act.activation(v1[0], kv[:, :, HD1:P], ACT.Copy, scale=1.0 / WS).then_inc(
                    v_high, 1)
                need(act, rope_sum, count(n, 6, 4))
                act.activation(k_stack1[:, :, 0, :], work[:, 0, 0:P].rearrange(
                    "p (t d) -> p t d", t=TILES), ACT.Copy).then_inc(stack_high, 1)
                for t in range(TILES):
                    need(act, rope_sum, count(n, 6, 5 + t))
                    if t == 1:
                        need(act, t_full, count(n, T_USES, T_K1 + 1))
                    act.activation(q_stack1[t][:, :, 0, :], work[:, 0, :].rearrange(
                        "p (h d) -> p h d", d=HD1), ACT.Copy,
                        scale=-float(HD1) ** -0.5).then_inc(stack_high, 1)
                units(n, 1)
                fill(n, 3)
                square(n, 1)
                fill(n, 4)

            def square(n, k):
                for t in range(TILES):
                    need(act, mid_ready, count(n, 4, 2 * k + t + 1))
                    act.activation(normed[:, t * D:(t + 1) * D], x_mid[:, t, :], ACT.Square,
                                   accum_out=squares[:, t:t + 1]).then_inc(square_sum, 1)

            def mlp(n):
                for p in range(PAIRS):
                    need(act, g_full, count(n, PAIRS, p + 1))
                    if p > 0:
                        need(act, inner_ready, count(n, PAIRS, p))
                    act.activation(silu[:], gbank[:], ACT.Silu, scale=1.0 / WS).then_inc(
                        silu_done, 1)
                    need(act, inner_ready, count(n, PAIRS, p + 1))
                    act.activation(inner_t[:, 0, 2 * p:2 * p + 2, :].rearrange("p c t -> p (c t)"),
                                   inner[:], ACT.Copy).then_inc(inner_high, 1)

            for half in range(2):
                act.wait_ge(angle_ready, half + 1)
                act.activation(reduced, reduced, ACT.Sin).then_inc(sines, 1)
                act.wait_ge(table_made, half + 1)
                tiles = SEQS * TILES // 2
                act.dma_start(
                    rope1[half * tiles:(half + 1) * tiles].rearrange("t p n -> p t n"),
                    table.rearrange("p (t n) -> p t n", t=tiles)).then_inc(table_out, 16)
            for m in range(raw, len(loads)):
                act.wait_ge(*landed[m])
                views = split_views(m, 0)
                for v, (src, dst) in enumerate(views):
                    ins = act.activation(dst, src, ACT.Copy, scale=WS)
                ins.then_inc(raw_high, 1)
            act.wait_ge(gains_made, 4 * CH)
            act.wait_ge(prob_clear, 1)
            attention((None, 0))
            with act.Fori(0, SEQS - 1) as i:
                mlp((i, 0))
                attention((i, 1))
            mlp((None, SEQS - 1))

        @block.vector
        def _(dve):
            def halves_low(n, f):
                for b in range(2):
                    need(dve, hi_done, count(n, HI_USES, HI_FILL[f] + b + 1))
                    if f == 0:
                        hi = act_t[0][:, 2 * b:2 * b + 2, :].rearrange("p c t -> p (c t)")
                        lo = act_t[1][:, 2 * b:2 * b + 2, :].rearrange("p c t -> p (c t)")
                        value = normed[:, b * 512:(b + 1) * 512]
                        dve.tensor_copy(hi, value).then_inc(norm_high, 1)
                        need(dve, norm_high, count(n, 2, b + 1))
                        dve.tensor_tensor(lo, value, hi, ALU.subtract).then_inc(
                            t_free, 1)
                    elif f in (1, 3):
                        hi = act_t[0][:, 2 * b:2 * b + 2, :].rearrange("p c t -> p (c t)")
                        lo = act_t[1][:, 2 * b:2 * b + 2, :].rearrange("p c t -> p (c t)")
                        dve.tensor_tensor(lo, trans[(T_FILL[f] + b) % 2][:], hi,
                                          ALU.subtract).then_inc(t_free, 1)
                    else:
                        g, to = (gain1, act_t) if f == 2 else (gain2, mlp_t)
                        for c in (2 * b, 2 * b + 1):
                            src = trans[(T_FILL[f] + b) % 2][:, (c % 2) * TOK:(c % 2 + 1) * TOK]
                            ins = dve.scalar_tensor_tensor(
                                to[1][:, c, :], src, g[:, c, bass.ds(index(n), 1)], to[0][:, c, :],
                                ALU.mult, ALU.subtract)
                        ins.then_inc(t_free, 1)

            def lows(n, layer, u):
                use = (S_UNIT0 if layer == 0 else S_UNIT1) + u
                need_apart(dve, s_full, count(n, S_USES, use + 1), (const_in, 32))
                bank_ = score[use % 2]
                if layer == 0:
                    for j, (h, t, at, wid) in enumerate(unit_heads(0, u)):
                        view = bank_[:, at:at + wid]
                        ins = dve.tensor_tensor_reduce(
                            out=view, in0=view, in1=mask[:, 0:wid], scale=1.0, scalar=3.0e38,
                            op0=ALU.add, op1=ALU.min, accum_out=low[:, u % 2, j:j + 1])
                else:
                    ins = dve.tensor_reduce(low[:, u % 2, 0:2], bank_[:].rearrange(
                        "p (h k) -> p h k", h=2), AX.X, ALU.min)
                ins.then_inc(low_ready, 1)

            def prob_lows(n, layer, u):
                t_unit = T_UNIT0 if layer == 0 else T_UNIT1
                need(dve, hi_done, count(n, HI_USES, HI_UNIT[layer] + u + 1))
                dve.tensor_tensor(prob_t[1][:, u % 2, :], trans[(t_unit + u) % 2][:],
                                  prob_t[0][:, u % 2, :], ALU.subtract).then_inc(t_free, 1)

            def units(n, layer):
                total = UNITS0 if layer == 0 else UNITS1
                lows(n, layer, 0)
                lows(n, layer, 1)
                for u in range(total):
                    prob_lows(n, layer, u)
                    if u + 2 < total:
                        lows(n, layer, u + 2)

            def normalise(n, layer):
                sums, hd, heads = (sums0, HD0, H0) if layer == 0 else (sums1, HD1, H1)
                for t in range(TILES):
                    done = (UNITS0 - 2, UNITS0, UNITS - 1, UNITS)[2 * layer + t]
                    need(dve, pv_done, count(n, UNITS, done))
                    dve.reciprocal(inv[:, t, 0:heads], sums[:, t, :]).then_inc(inv_ready, 1)
                    need(dve, inv_ready, count(n, 4, 2 * layer + t + 1))
                    dve.tensor_tensor(
                        work[:, t, :].rearrange("p (h d) -> p h d", d=hd),
                        ybank[t][:].rearrange("p (h d) -> p h d", d=hd),
                        inv[:, t, 0:heads].unsqueeze(2).broadcast_to([P, heads, hd]),
                        ALU.mult).then_inc(weighted, 1)

            def add(n, layer):
                use = S_OUT0 if layer == 0 else S_OUT1
                if layer == 0:
                    need(dve, res_copied, count((n[0], n[1] - 1), 16, 16))
                for t in range(TILES):
                    need(dve, s_full, count(n, S_USES, use + t + 1))
                    src = x_in if layer == 0 else x_mid
                    dve.scalar_tensor_tensor(x_mid[:, t, :], score[(use + t) % 2][:], 1.0 / WS,
                                             src[:, t, :], ALU.mult, ALU.add).then_inc(mid_ready, 1)

            def rotate0(n, ps, q_or_k, t, heads, dst, swap, done):
                view = ps.rearrange("p (h two d) -> p h two d", two=2, d=HD0 // 2)
                for c, (src, to) in enumerate(((view, dst), (view[:, :, ::-1, :], swap))):
                    table = rope0[:, q_or_k, t, c, :].rearrange("p (two d) -> p two d", two=2)
                    ins = dve.tensor_tensor(
                        to.rearrange("p (h two d) -> p h two d", two=2, d=HD0 // 2), src,
                        table.unsqueeze(1).broadcast_to([P, heads, 2, HD0 // 2]), ALU.mult)
                if done is not None:
                    ins.then_inc(done, 1)

            def rotate1(n, ps, t, heads, dst, swap, done):
                half = HD1 // 2
                view = ps.rearrange("p (h two d) -> p h two d", two=2, d=half)
                cos = rope1_sb[:, t, 0:half].unsqueeze(1).unsqueeze(1).broadcast_to(
                    [P, heads, 2, half])
                sin = rope1_sb[:, t, half:].rearrange("p (two d) -> p two d", two=2).unsqueeze(
                    1).broadcast_to([P, heads, 2, half])
                for src, to, table in ((view, dst, cos), (view[:, :, ::-1, :], swap, sin)):
                    ins = dve.tensor_tensor(
                        to.rearrange("p (h two d) -> p h two d", two=2, d=half), src, table,
                        ALU.mult)
                if done is not None:
                    ins.then_inc(done, 1)

            def rope_add(n, k, size):
                need(dve, rope_terms, count(n, 6, k + 1))
                dve.tensor_tensor(work[:, 0, 0:size], work[:, 0, 0:size], work[:, 1, 0:size],
                                  ALU.add).then_inc(rope_sum, 1)
                need(dve, stack_high, count(n, 6, k + 1))

            def layer0(n):
                need(dve, x_arrived, count(n, 16, 16))
                for t in range(TILES):
                    dve.bn_stats(bn[:, t, :], x_in[:, t, :]).then_inc(bn_raw, 1)
                for t in range(TILES):
                    need_apart(dve, bn_raw, count(n, 2, t + 1), (const_in, 32))
                    dve.bn_aggr(moments[:, t, :], bn[:, t, :]).then_inc(ln_stat, 1)
                need(dve, rstd_ready, count(n, 3, 1))
                for t in range(TILES):
                    dve.tensor_scalar(work[:, t, :], x_in[:, t, :], moments[:, t, 0:1],
                                      rstd[:, t:t + 1], ALU.subtract, ALU.mult).then_inc(
                                          work_ready, 1)
                halves_low(n, 0)
                need(dve, lat_high, count(n, 1, 1))
                src = score[S_LAT % 2]
                dve.scalar_tensor_tensor(lat[1][:, WINDOW:], src[:, 0:TOK], 1.0 / WS,
                                         lat[0][:, WINDOW:], ALU.mult, ALU.subtract)
                dve.scalar_tensor_tensor(lat[1][:, 0:WINDOW], src[:, P - WINDOW:P], 1.0 / WS,
                                         lat[0][:, 0:WINDOW], ALU.mult,
                                         ALU.subtract).then_inc(lat_low, 1)
                need(dve, v_high, count(n, 3, 1))
                kv = score[S_KV % 2][:].rearrange("p (t n) -> p t n", t=TILES)
                dve.scalar_tensor_tensor(v0[1][:, 0:TILES, :], kv[:, :, P:2 * P], 1.0 / WS,
                                         v0[0][:, 0:TILES, :], ALU.mult, ALU.subtract)
                for t in range(TILES):
                    rotate0(n, kv[:, t, 0:P], 1, t, KV0, work[:, 0, t * P:(t + 1) * P],
                            work[:, 1, t * P:(t + 1) * P],
                            None if t == 0 else rope_terms)
                need(dve, v_high, count(n, 3, 2))
                dve.scalar_tensor_tensor(v0[1][0:K_NEAR, 2, :], score[S_NEAR % 2][0:K_NEAR, 0:P],
                                         1.0 / WS, v0[0][0:K_NEAR, 2, :], ALU.mult,
                                         ALU.subtract).then_inc(near_low, 1)
                rope_add(n, 0, 2 * P)
                dve.tensor_copy(k_stack0[:, :, 2, :], k_stack0[:, :, 0, :])
                dve.tensor_tensor(k_stack0[:, :, 1, :], work[:, 0, 0:2 * P].rearrange(
                    "p (g d) -> p g d", d=HD0), k_stack0[:, :, 0, :], ALU.subtract).then_inc(
                        stack_low, 1)
                need(dve, stack_low, count(n, 4, 1))
                dve.tensor_copy(k_stack0[:, :, 3, :], k_stack0[:, :, 1, :]).then_inc(stack_ready, 1)
                for t in range(TILES):
                    need(dve, y_full, count(n, 4, t + 1))
                    rotate0(n, ybank[t][:], 0, t, H0, work[:, 0, :], work[:, 1, :], rope_terms)
                    rope_add(n, 1 + t, D)
                    dve.tensor_copy(q_stack0[:, :, 1, :], q_stack0[:, :, 0, :])
                    dve.tensor_tensor(q_stack0[:, :, 2, :], work[:, 0, :].rearrange(
                        "p (h d) -> p h d", d=HD0), q_stack0[:, :, 0, :], ALU.subtract).then_inc(
                            stack_low, 1)
                    need(dve, stack_low, count(n, 4, 2 + t))
                    dve.tensor_copy(q_stack0[:, :, 3, :], q_stack0[:, :, 2, :]).then_inc(
                        stack_ready, 1)
                    if t == 0:
                        keys0(n)
                    for b in range(2):
                        use = T_Q0 + 2 * t + b
                        need(dve, t_full, count(n, T_USES, use + 1))
                        dve.tensor_copy(
                            q_t[:, 8 * b:8 * b + 8, t * P:(t + 1) * P],
                            trans[use % 2][:].bitcast(F16).rearrange("p (h q) -> p h q", h=8),
                        ).then_inc(t_free, 1)
                units(n, 0)
                normalise(n, 0)
                halves_low(n, 1)
                add(n, 0)

            def keys0(n):
                need(dve, t_full, count(n, T_USES, T_K0 + 1))
                kt = trans[T_K0 % 2][:].bitcast(F16).rearrange("p (t g k) -> p t g k", t=TILES,
                                                               g=KV0)
                dve.tensor_copy(k0_t[:, :, 0:P], kt[:, 1, :, :])
                dve.tensor_copy(k0_t[:, :, P:P + WINDOW], kt[:, 0, :, P - WINDOW:P])
                dve.tensor_copy(k0_t[:, :, P + WINDOW:], kt[:, 0, :, :]).then_inc(t_free, 1)

            def rms(n, k):
                need(dve, rstd_ready, count(n, 3, k + 1))
                for t in range(TILES):
                    dve.tensor_scalar(work[:, t, :], x_mid[:, t, :], rstd[:, t:t + 1], None,
                                      ALU.mult).then_inc(work_ready, 1)

            def layer1(n):
                rms(n, 1)
                halves_low(n, 2)
                need(dve, v_high, count(n, 3, 3))
                kv = score[S_KV1 % 2][:, 0:TILES * P].rearrange("p (t n) -> p t n", t=TILES)
                dve.scalar_tensor_tensor(v1[1], kv[:, :, HD1:P], 1.0 / WS, v1[0], ALU.mult,
                                         ALU.subtract)
                need(dve, rope_arrived, count(n, 16, 16))
                for t in range(TILES):
                    rotate1(n, kv[:, t, 0:HD1], t, 1, work[:, 0, t * HD1:(t + 1) * HD1],
                            work[:, 1, t * HD1:(t + 1) * HD1], None if t == 0 else rope_terms)
                rope_add(n, 3, P)
                dve.tensor_copy(k_stack1[:, :, 1, :], k_stack1[:, :, 0, :])
                dve.tensor_tensor(k_stack1[:, :, 2, :], work[:, 0, 0:P].rearrange(
                    "p (t d) -> p t d", t=TILES), k_stack1[:, :, 0, :], ALU.subtract).then_inc(
                        stack_low, 1)
                need(dve, stack_low, count(n, 4, 4))
                dve.tensor_copy(k_stack1[:, :, 3, :], k_stack1[:, :, 2, :]).then_inc(stack_ready, 1)
                for t in range(TILES):
                    need(dve, y_full, count(n, 4, 2 + t + 1))
                    rotate1(n, ybank[t][:], t, H1, work[:, 0, :], work[:, 1, :], rope_terms)
                    rope_add(n, 4 + t, D)
                    dve.scalar_tensor_tensor(
                        q_stack1[t][:, :, 1, :], work[:, 0, :].rearrange("p (h d) -> p h d", d=HD1),
                        -float(HD1) ** -0.5, q_stack1[t][:, :, 0, :], ALU.mult,
                        ALU.subtract).then_inc(stack_ready, 1)
                    if t == 0:
                        need(dve, t_full, count(n, T_USES, T_K1 + 1))
                        dve.tensor_copy(
                            k1_t.rearrange("p a (t k) -> p a t k", t=TILES),
                            trans[T_K1 % 2][:].bitcast(F16)[:, 0:4 * P].rearrange(
                                "p (t a k) -> p a t k", t=TILES, a=2)).then_inc(t_free, 1)
                    use = T_Q1 + t
                    need(dve, t_full, count(n, T_USES, use + 1))
                    dve.tensor_copy(
                        q_t[:, 0:H1, t * P:(t + 1) * P],
                        trans[use % 2][:].bitcast(F16).rearrange("p (h q) -> p h q", h=H1),
                    ).then_inc(t_free, 1)
                units(n, 1)
                normalise(n, 1)
                halves_low(n, 3)
                add(n, 1)
                rms(n, 2)
                halves_low(n, 4)

            def mlp(n):
                for p in range(PAIRS):
                    need(dve, u_full, count(n, PAIRS, p + 1))
                    need(dve, silu_done, count(n, PAIRS, p + 1))
                    if p > 0:
                        need(dve, inner_high, count(n, PAIRS, p))
                        need(dve, inner_low, count(n, PAIRS, p))
                    dve.scalar_tensor_tensor(inner[:], ubank[:], HS / WS, silu[:], ALU.mult,
                                             ALU.mult).then_inc(inner_ready, 1)
                need(dve, res_copied, count(n, 16, 16))
                for t in range(TILES):
                    need(dve, d_full, count(n, TILES, t + 1))
                    dve.scalar_tensor_tensor(x_res[:, t, :], (gbank, ubank)[t][:],
                                             1.0 / (WS * HS), x_res[:, t, :], ALU.mult,
                                             ALU.add).then_inc(d_read, 1)

            steps = [0]

            def step(ins):
                steps[0] += 1
                ins.then_inc(angle_step, 1)
                dve.wait_ge(angle_step, steps[0])

            tiles = SEQS * TILES // 2
            dve.wait_ge(pos_in, 32)
            step(dve.tensor_copy(posf, pos))
            for half in range(2):
                step(dve.tensor_tensor(
                    angle.rearrange("p (t f) -> p t f", t=tiles),
                    posf[:, half * tiles:(half + 1) * tiles].unsqueeze(2).broadcast_to(
                        [P, tiles, HD1 // 2]),
                    freq.unsqueeze(1).broadcast_to([P, tiles, HD1 // 2]), ALU.mult))
                for c in range(2):
                    t_c = turns[:, c * 512:(c + 1) * 512]
                    r_c = reduced[:, c * 512:(c + 1) * 512]
                    step(dve.tensor_scalar(t_c, angle, 1.0 / (2 * np.pi), 0.25 * (1 - c), ALU.mult,
                                           ALU.add))
                    step(dve.tensor_scalar(t_c, t_c, ROUND, None, ALU.add))
                    step(dve.tensor_scalar(t_c, t_c, -ROUND, None, ALU.add))
                    step(dve.scalar_tensor_tensor(r_c, t_c, -TWO_PI_1, angle, ALU.mult, ALU.add))
                    step(dve.scalar_tensor_tensor(r_c, t_c, -TWO_PI_2, r_c, ALU.mult, ALU.add))
                    step(dve.scalar_tensor_tensor(r_c, t_c, -TWO_PI_3, r_c, ALU.mult, ALU.add))
                    if c == 0:
                        step(dve.tensor_scalar(r_c, r_c, float(np.pi / 2), None, ALU.add))
                dve.tensor_scalar(reduced, reduced, PI_IN, -PI_IN, ALU.min, ALU.max).then_inc(
                    angle_ready, 1)
                dve.wait_ge(sines, half + 1)
                if half == 1:
                    dve.wait_ge(table_out, 16)
                tab = table.rearrange("p (t n) -> p t n", t=tiles)
                f = HD1 // 2
                for at, c, sign in ((0, 0, 1.0), (f, 1, -1.0), (2 * f, 1, 1.0)):
                    ins = dve.tensor_scalar(
                        tab[:, :, at:at + f],
                        reduced[:, c * 512:(c + 1) * 512].rearrange("p (t f) -> p t f", t=tiles),
                        sign / WS, None, ALU.mult)
                ins.then_inc(table_made, 1)
            dve.wait_ge(cond_used, raw)
            dve.wait_ge(cond_in, 64)
            mod = ybank[0][:, 0:4 * CH * SEQS].rearrange("p (m s) -> p m s", s=SEQS)
            for c in range(CH):
                dve.tensor_scalar(gain0[:, c, :], mod[:, c, :], b_ada[:, c:c + 1], 1.0, ALU.add,
                                  ALU.add).then_inc(gains_made, 1)
                dve.tensor_scalar(bias0[:, c, :], mod[:, CH + c, :], b_ada[:, CH + c:CH + c + 1],
                                  None, ALU.add).then_inc(gains_made, 1)
                dve.tensor_scalar(gain1[:, c, :], mod[:, 2 * CH + c, :], 1.0, ln_w[:, 0, c:c + 1],
                                  ALU.add, ALU.mult).then_inc(gains_made, 1)
                dve.tensor_scalar(gain2[:, c, :], mod[:, 3 * CH + c, :], 1.0, ln_w[:, 1, c:c + 1],
                                  ALU.add, ALU.mult).then_inc(gains_made, 1)
            for m in range(raw, len(loads)):
                dve.wait_ge(raw_high, m - raw + 1)
                for (src, dst), (_, hi) in zip(split_views(m, 1), split_views(m, 0)):
                    ins = dve.scalar_tensor_tensor(dst, src, WS, hi, ALU.mult, ALU.subtract)
                ins.then_inc(raw_split, 1)
            dve.wait_ge(const_in, 32)
            dve.wait_ge(gains_made, 4 * CH)
            dve.wait_ge(table_out, 32)
            dve.sem_inc(d_read, TILES)
            layer0((None, 0))
            layer1((None, 0))
            with dve.Fori(0, SEQS - 1) as i:
                mlp((i, 0))
                layer0((i, 1))
                layer1((i, 1))
            mlp((None, SEQS - 1))

        @block.tensor
        def _(pe):
            def product(out_ap, left, right, start=True, stop=True):
                pe.matmul(out_ap, left[0], right[0], start=start, stop=False)
                pe.matmul(out_ap, left[0], right[1], start=False, stop=False)
                return pe.matmul(out_ap, left[1], right[0], start=False, stop=stop)

            def cut(pair, *at):
                return pair[0][at], pair[1][at]

            def events():
                return {"lat_low": lat_low, "rope_terms": rope_terms, "near_low": near_low,
                        "terms_made": terms_made, "mid_ready": mid_ready}

            def score_bank(n, use):
                m, last = before(n, use, S_USES)
                name, per, k = S_READ[last]
                need(pe, events()[name], count(m, per, k))
                return score[use % 2]

            def trans_bank(n, use):
                m, last = before(n, use, T_USES)
                need(pe, t_free, count(m, T_USES, last + 1))
                return trans[use % 2]

            def fill(n, f):
                for b in range(2):
                    bank_ = trans_bank(n, T_FILL[f] + b)
                    for t in range(TILES):
                        if b == 0:
                            if f in (1, 3):
                                need(pe, weighted, count(n, 4, f - 1 + t + 1))
                            else:
                                need(pe, work_ready, count(n, 6, f + t + 1))
                        for c in (2 * b, 2 * b + 1):
                            ins = pe.transpose(bank_[:, (c % 2) * TOK + t * P:][:, 0:P],
                                               work[:, t, c * P:(c + 1) * P], ident[:])
                    ins.then_inc(t_full, 1)

            def token_major(out_ap, src, t, w, cols):
                for c in range(CH):
                    ins = product(out_ap, cut(src, slice(None), c, slice(t * P, (t + 1) * P)),
                                  cut(w, slice(None), c, slice(0, cols)), c == 0, c == CH - 1)
                return ins

            def queries(n, layer, t, w):
                if layer == 0:
                    need(pe, weighted, count((n[0], n[1] - 1), 4, 2 + t + 1))
                else:
                    need(pe, weighted, count(n, 4, t + 1))
                token_major(ybank[t][:], act_t, t, w, D).then_inc(y_full, 1)

            def stacks(n, use, first, views):
                bank_ = trans_bank(n, use)[:].bitcast(F16)
                need(pe, stack_ready, count(n, 6, first))
                for m, view in enumerate(views):
                    ins = pe.transpose(bank_[:, m * P:(m + 1) * P], view, ident16[:])
                ins.then_inc(t_full, 1)

            def unit_scores(n, layer, u):
                bank_ = score_bank(n, (S_UNIT0 if layer == 0 else S_UNIT1) + u)
                for h, t, at, wid in unit_heads(layer, u):
                    q = q_t[:, h, t * P:(t + 1) * P]
                    if layer == 0:
                        first = 0 if t else P + WINDOW
                        ins = pe.matmul(bank_[:, at:at + wid], q,
                                        k0_t[:, h // (H0 // KV0), first:first + wid], start=True,
                                        stop=True)
                    else:
                        pe.matmul(bank_[:, at:at + wid], q, k1_t[:, 0, :], start=True, stop=False)
                        ins = pe.matmul(bank_[:, at:at + wid], q, k1_t[:, 1, :], start=False,
                                        stop=True)
                ins.then_inc(s_full, 1)

            def unit_transposes(n, layer, u):
                need(pe, terms_made, count(n, UNITS, layer * UNITS0 + u + 1))
                bank_ = trans_bank(n, (T_UNIT0 if layer == 0 else T_UNIT1) + u)
                for b in range(4):
                    ins = pe.transpose(bank_[:, b * P:(b + 1) * P],
                                       prob[:, u % 2, b * P:(b + 1) * P], ident[:])
                ins.then_inc(t_full, 1)

            def unit_values(n, layer, u):
                need(pe, t_free, count(n, T_USES, (T_UNIT0 if layer == 0 else T_UNIT1) + u + 1))
                for h, t, at, wid in unit_heads(layer, u):
                    if layer == 0:
                        if h == 0:
                            need(pe, rope_terms, count(n, 6, 1 + t + 1))
                        g = h // (H0 // KV0)
                        out_ap = ybank[t][:, h * HD0:(h + 1) * HD0]
                        blocks = [(at, P, 0)] if t == 0 else [(at, P, 1), (at + P, K_NEAR, 2)]
                        for m, (col, rows, tile) in enumerate(blocks):
                            ins = product(
                                out_ap, cut(prob_t, slice(0, rows), u % 2, slice(col, col + P)),
                                cut(v0, slice(0, rows), tile, slice(g * HD0, (g + 1) * HD0)),
                                m == 0, m == len(blocks) - 1)
                    else:
                        if h == 0:
                            need(pe, rope_terms, count(n, 6, 4 + t + 1))
                        out_ap = ybank[t][:, h * HD1:(h + 1) * HD1]
                        for m in range(TILES):
                            ins = product(
                                out_ap,
                                cut(prob_t, slice(None), u % 2, slice(at + m * P, at + m * P + P)),
                                cut(v1, slice(None), m, slice(None)), m == 0, m == TILES - 1)
                ins.then_inc(pv_done, 1)

            def units(n, layer):
                total = UNITS0 if layer == 0 else UNITS1
                unit_scores(n, layer, 0)
                unit_scores(n, layer, 1)
                for u in range(total):
                    unit_transposes(n, layer, u)
                    if u + 2 < total:
                        unit_scores(n, layer, u + 2)
                    if u > 0:
                        unit_values(n, layer, u - 1)
                unit_values(n, layer, total - 1)

            def project(n, layer, w):
                for t in range(TILES):
                    bank_ = score_bank(n, (S_OUT0 if layer == 0 else S_OUT1) + t)
                    if t == 0:
                        need(pe, t_free, count(n, T_USES, T_FILL[1 if layer == 0 else 3] + 2))
                    token_major(bank_[:], act_t, t, w, D).then_inc(s_full, 1)

            def layer0(n):
                fill(n, 0)
                bank_ = score_bank(n, S_LAT)
                for c in range(CH):
                    if c % 2 == 0:
                        need(pe, t_free, count(n, T_USES, T_FILL[0] + c // 2 + 1))
                    ins = product(bank_[:, 0:TOK], cut(wkd, slice(None), c, slice(None)),
                                  cut(act_t, slice(None), c, slice(None)), c == 0, c == CH - 1)
                ins.then_inc(s_full, 1)
                queries(n, 0, 0, wq0)
                bank_ = score_bank(n, S_KV)
                need(pe, lat_low, count(n, 1, 1))
                for t in range(TILES):
                    ins = product(bank_[:, t * TOK:(t + 1) * TOK],
                                  cut(lat, slice(None), slice(WINDOW + t * P, WINDOW + t * P + P)),
                                  cut(wkv0, slice(None), 0, slice(None)))
                ins.then_inc(s_full, 1)
                bank_ = score_bank(n, S_NEAR)
                product(bank_[0:K_NEAR, 0:P], cut(lat, slice(None), slice(0, K_NEAR)),
                        cut(wkv0, slice(None), 0, slice(P, 2 * P))).then_inc(s_full, 1)
                queries(n, 0, 1, wq0)
                stacks(n, T_K0, 1, [stack[:, m * P:(m + 1) * P] for m in range(TILES * KV0)])
                for t in range(TILES):
                    for b in range(2):
                        stacks(n, T_Q0 + 2 * t + b, 2 + t,
                               [stack[:, h * P:(h + 1) * P] for h in range(8 * b, 8 * b + 8)])
                need(pe, t_free, count(n, T_USES, T_Q0 + 4))
                units(n, 0)
                fill(n, 1)
                project(n, 0, wo0)

            def layer1(n):
                fill(n, 2)
                bank_ = score_bank(n, S_KV1)
                need(pe, t_free, count(n, T_USES, T_FILL[2] + 2))
                for t in range(TILES):
                    ins = token_major(bank_[:, t * P:(t + 1) * P], act_t, t, wkv1, P)
                ins.then_inc(s_full, 1)
                for t in range(TILES):
                    queries(n, 1, t, wq1)
                stacks(n, T_K1, 4, [stack[:, m * P:(m + 1) * P] for m in range(2 * TILES)])
                for t, at in enumerate((1024, 0)):
                    stacks(n, T_Q1 + t, 5 + t,
                           [stack[:, at + h * P:at + (h + 1) * P] for h in range(H1)])
                need(pe, t_free, count(n, T_USES, T_Q1 + 2))
                units(n, 1)
                fill(n, 3)
                project(n, 1, wo1)
                fill(n, 4)

            def mlp(n):
                need(pe, t_free, count(n, T_USES, T_USES))
                for p in range(PAIRS):
                    for w, bank_, full, read in ((wg, gbank, g_full, silu_done),
                                                 (wu, ubank, u_full, inner_ready)):
                        if p > 0:
                            need(pe, read, count(n, PAIRS, p))
                        else:
                            need(pe, d_read, count(n, TILES, 1 if w is wg else 2))
                        for m in range(2):
                            f = 2 * p + m
                            for c in range(CH):
                                ins = product(bank_[:, m * TOK:(m + 1) * TOK],
                                              cut(w, slice(None), c, slice(f * P, (f + 1) * P)),
                                              cut(mlp_t, slice(None), c, slice(None)), c == 0,
                                              c == CH - 1)
                        ins.then_inc(full, 1)
                for t in range(TILES):
                    if t == 0:
                        need(pe, silu_done, count(n, PAIRS, PAIRS))
                    else:
                        need(pe, inner_ready, count(n, PAIRS, PAIRS))
                    for f in range(FCH):
                        if t == 0 and f % 2 == 0:
                            need(pe, inner_high, count(n, PAIRS, f // 2 + 1))
                            need(pe, inner_low, count(n, PAIRS, f // 2 + 1))
                        cols = slice(t * P, (t + 1) * P)
                        ins = product((gbank, ubank)[t][:],
                                      (inner_t[:, 0, f, cols], inner_t[:, 1, f, cols]),
                                      cut(wd, slice(None), f, slice(None)), f == 0, f == FCH - 1)
                    ins.then_inc(d_full, 1)

            pe.wait_ge(cond_in, 64)
            mod = ybank[0][:, 0:4 * CH * SEQS].rearrange("p (m s) -> p m s", s=SEQS)
            for m in range(raw):
                pe.wait_ge(*landed[m])
                slot = stage[:, m % 2, :].rearrange("p (c n) -> p c n", c=CH)
                for j in range(CH):
                    for c in range(CH):
                        ins = pe.matmul(mod[:, m * CH + j, :], slot[:, c, j * P:(j + 1) * P],
                                        cond[:, c, :], start=c == 0, stop=c == CH - 1)
                ins.then_inc(cond_used, 1)
            pe.wait_ge(ident_made, 2)
            pe.wait_ge(gains_made, 4 * CH)
            pe.wait_ge(raw_split, len(loads) - raw)
            layer0((None, 0))
            layer1((None, 0))
            with pe.Fori(0, SEQS - 1) as i:
                mlp((i, 0))
                layer0((i, 1))
                layer1((i, 1))
            mlp((None, SEQS - 1))


def key_mask():
    q = np.arange(P)[:, None]
    own = np.arange(P)[None, :]
    own_ok = (np.abs(q - own) <= WINDOW) | (own % GLOBAL == 0)
    near = np.arange(P - WINDOW, P)[None, :]
    near_ok = (q + P - near <= WINDOW) | (near % GLOBAL == 0)
    ok = np.concatenate([own_ok, near_ok, np.ones((P, 1), bool)], axis=1)
    return np.where(ok, 0.0, NEG).astype(np.float32)


def frequencies(width):
    f = np.float32(1.0) / np.float32(10000.0) ** (np.arange(0, width, 2, dtype=np.float32)
                                                  / np.float32(width))
    return f.astype(np.float32)


def rope_table0():
    angle = np.arange(TOK, dtype=np.float32)[:, None] * frequencies(HD0)[None, :]
    cos, sin = np.cos(angle.astype(np.float64)), np.sin(angle.astype(np.float64))
    one = np.stack([np.concatenate([cos, cos], 1), np.concatenate([-sin, sin], 1)], 1)
    both = np.stack([one * (-(HD0 ** -0.5) / WS), one / WS])
    both = both.reshape(2, TILES, P, 2, HD0).transpose(2, 0, 1, 3, 4)
    return np.ascontiguousarray(both.reshape(P, -1).astype(np.float32))


def kernel(**inputs):
    import concourse.bacc as bacc
    from concourse.bass_utils import run_bass_kernel_spmd

    def get(name):
        return np.asarray(inputs[name])

    def turned(name):
        return np.ascontiguousarray(get(name).T)

    def by_feature(v):
        return np.ascontiguousarray(v.reshape(-1, P).T)

    arrays = {
        "x": np.ascontiguousarray(get("x")),
        "cond_t": turned("cond_2048"),
        "pos_t": np.ascontiguousarray(get("pos_BxS").reshape(SEQS * TILES, P).T),
        "w_ada_t": turned("L0_cond_W_ada"), "b_ada_t": by_feature(get("L0_cond_b_ada")),
        "wq0_t": turned("L0_cond_Wq"), "wkd_t": turned("L0_cond_Wkd"),
        "wku_t": turned("L0_cond_Wku"), "wvu_t": turned("L0_cond_Wvu"),
        "wo0_t": turned("L0_cond_Wo"),
        "ln1_w": by_feature(get("L1_cond_ln1_w")), "tw1_t": turned("L1_cond_ln1_tw"),
        "ln2_w": by_feature(get("L1_cond_ln2_w")), "tw2_t": turned("L1_cond_ln2_tw"),
        "wq1_t": turned("L1_cond_Wq"), "wk1_t": turned("L1_cond_Wk"),
        "wv1_t": turned("L1_cond_Wv"), "wo1_t": turned("L1_cond_Wo"),
        "wg_t": turned("L1_cond_Wg"), "wu_t": turned("L1_cond_Wu"), "wd_t": turned("L1_cond_Wd"),
        "mask_c": key_mask(), "rope0_c": rope_table0(),
        "freq_c": np.ascontiguousarray(np.broadcast_to(frequencies(HD1), (P, HD1 // 2))),
    }
    nc = bacc.Bacc("TRN2", target_bir_lowering=False, num_devices=1)
    args = {name: nc.dram_tensor(name + "_dram", a.shape, mybir.dt.from_np(a.dtype),
                                 kind="ExternalInput").ap() for name, a in arrays.items()}
    args["rope1"] = nc.dram_tensor("rope1_dram", (SEQS * TILES, P, TAB), F32, kind="Internal").ap()
    args["out"] = nc.dram_tensor("out_dram", (SEQS, TOK, D), F32, kind="ExternalOutput").ap()
    build(nc, **args)
    result = run_bass_kernel_spmd(nc, [{name + "_dram": a for name, a in arrays.items()}],
                                  core_ids=[0])
    return result.results[0]["out_dram"]
```

```python
from contextlib import ExitStack

import numpy as np

import concourse.bass as bass
from concourse import mybir

ALU = mybir.AluOpType
ACT = mybir.ActivationFunctionType
AX = mybir.AxisListType
F32 = mybir.dt.float32
F16 = mybir.dt.float16
I32 = mybir.dt.int32

P = 128
SEQS, TOK, D = 16, 256, 512
TILES = TOK // P
CH = D // P
FF = 2048
FCH = FF // P
PAIRS = FCH // 2
H0, KV0, HD0 = 16, 4, 32
H1, HD1 = 8, 64
LAT = 128
WINDOW, GLOBAL = 64, 64
LN_EPS, RMS_EPS = 1e-5, 1e-6
WS = 64.0
HS = 1.0 / 16.0
NEG = 1.0e30
K_OWN, K_NEAR = P, WINDOW + 1
K_TWO = K_OWN + K_NEAR
ROWS0 = 3 * HD0
TAB = 3 * HD1 // 2
ROUND = 1.5 * 2.0 ** 23
TWO_PI_1, TWO_PI_2 = 6.28125, 0.00193500518798828125
TWO_PI_3 = float(2 * np.pi - TWO_PI_1 - TWO_PI_2)
PI_IN = 3.1415925

UNITS0, UNITS1 = 12, 8
UNITS = UNITS0 + UNITS1
S_READ = ([("lat_low", 1, 1), ("rope_terms", 6, 1), ("near_low", 1, 1)]
          + [("terms_made", UNITS, u + 1) for u in range(UNITS0)]
          + [("mid_ready", 4, 1), ("mid_ready", 4, 2), ("rope_terms", 6, 4)]
          + [("terms_made", UNITS, UNITS0 + u + 1) for u in range(UNITS1)]
          + [("mid_ready", 4, 3), ("mid_ready", 4, 4)])
S_USES = len(S_READ)
S_LAT, S_KV, S_NEAR, S_UNIT0 = range(4)
S_OUT0 = S_UNIT0 + UNITS0
S_KV1 = S_OUT0 + TILES
S_UNIT1 = S_KV1 + 1
S_OUT1 = S_UNIT1 + UNITS1
T_FILL0, T_K0, T_Q0, T_UNIT0 = 0, 2, 3, 7
T_K1 = T_UNIT0 + UNITS0 + 4
T_Q1, T_UNIT1 = T_K1 + 1, T_K1 + 3
T_FILL = [T_FILL0, T_K1 - 4, T_K1 - 2, T_UNIT1 + UNITS1, T_UNIT1 + UNITS1 + 2]
T_USES = T_FILL[4] + 2
HI_FILL = [0, 2 + UNITS0, 4 + UNITS0, 6 + UNITS, 8 + UNITS]
HI_UNIT = [2, 6 + UNITS0]
HI_USES = 10 + UNITS


PARTS = 4 * PAIRS + TILES * PAIRS
PLAN = ([("fill0", 3), ("latent", 2), ("query0", 0), ("kv", 0), ("query1", 0), ("keys", 1),
         ("stack0", 2), ("stack1", 2), ("scores0", 1)]
        + [(f"unit0_{u}", 0 if u in (4, 8) else 1) for u in range(UNITS0)]
        + [("fill1", 2), ("out0", 2), ("fill2", 2), ("kv1", 2), ("query2", 0), ("query3", 0),
           ("keys1", 1), ("stack2", 2), ("stack3", 1), ("scores1", 1)]
        + [(f"unit1_{u}", 0 if u == 4 else 1) for u in range(UNITS1)]
        + [("fill3", 2), ("out1", 1), ("fill4", 2)])
BEFORE = {name: sum(parts for _, parts in PLAN[:m + 1]) for m, (name, _) in enumerate(PLAN)}
BEFORE["end"] = PARTS
PREVIOUS = dict(zip([name for name, _ in PLAN] + ["end"], [None] + [name for name, _ in PLAN]))


def parts_at(step):
    return range(BEFORE.get(PREVIOUS[step], 0), BEFORE[step])


def pairs_at(step, done):
    return [p for p in range(PAIRS)
            if 4 * p + done - 1 in parts_at(step)]


def tiles_at(step):
    return [t for t in range(TILES) if 4 * PAIRS + (t + 1) * PAIRS - 1 in parts_at(step)]


def count(n, per, k):
    i, off = n
    return off * per + k if i is None else i * per + (off * per + k)


def need(eng, sem, value):
    if isinstance(value, int) and value <= 0:
        return
    eng.wait_ge(sem, value)


def need_apart(eng, sem, value, met):
    if isinstance(value, int):
        need(eng, sem, value)
        return
    value = eng.to_reg(value)
    eng.wait_ge(*met)
    eng.wait_ge(sem, value)


def index(n):
    i, off = n
    return off if i is None else i + off


def before(n, use, uses):
    return (n, use - 2) if use >= 2 else ((n[0], n[1] - 1), use - 2 + uses)


def unit_heads(layer, u):
    if layer == 0:
        group, kind = divmod(u, 3)
        if kind == 0:
            return [(4 * group + j, 0, j * P, P) for j in range(4)]
        return [(4 * group + 2 * (kind - 1) + j, 1, 2 * j * P, K_TWO) for j in range(2)]
    pair, t = divmod(u, TILES)
    return [(2 * pair + j, t, j * TOK, TOK) for j in range(2)]


def build(nc, x, cond_t, pos_t, w_ada_t, b_ada_t, wq0_t, wkd_t, wku_t, wvu_t, wo0_t, ln1_w, tw1_t,
          ln2_w, tw2_t, wq1_t, wk1_t, wv1_t, wo1_t, wg_t, wu_t, wd_t, mask_c, rope0_c, freq_c, rope1,
          out):
    with ExitStack() as ctx:
        def sb(name, shape, dt=F32):
            return ctx.enter_context(nc.sbuf_tensor(name, shape, dt))

        def sem(name):
            return ctx.enter_context(nc.semaphore(name))

        def weight(name, chunks, cols):
            return (sb(name + "_hi", [P, chunks, cols], F16), sb(name + "_lo", [P, chunks, cols], F16))

        wkd = weight("wkd", CH, LAT)
        wkv0 = weight("wkv0", 1, 2 * KV0 * HD0)
        wq0 = weight("wq0", CH, D)
        wo0 = weight("wo0", CH, D)
        wkv1 = weight("wkv1", CH, 2 * HD1)
        wq1 = weight("wq1", CH, D)
        wo1 = weight("wo1", CH, D)
        wg = weight("wg", CH, FF)
        wu = weight("wu", CH, FF)
        wd = weight("wd", FCH, D)

        x_in = sb("x_in", [P, TILES, D])
        x_mid = sb("x_mid", [P, TILES, D])
        x_res = sb("x_res", [P, TILES, D])
        work = sb("work", [P, TILES, D])
        act_t = (sb("act_hi", [P, CH, TOK], F16), sb("act_lo", [P, CH, TOK], F16))
        mlp_t = (sb("mlp_hi", [P, CH, TOK], F16), sb("mlp_lo", [P, CH, TOK], F16))
        lat = (sb("lat_hi", [P, WINDOW + TOK], F16), sb("lat_lo", [P, WINDOW + TOK], F16))
        stack = sb("stack", [P, 2048], F16)
        q_t = sb("q_t", [P, H0, TOK], F16)
        k_t = sb("k_t", [P, KV0, P + WINDOW + P], F16)
        k0_t = k_t[0:ROWS0]
        v0 = (sb("v0_hi", [P, 3, P], F16), sb("v0_lo", [P, 3, P], F16))
        k1_t = k_t[:].rearrange("p g k -> p (g k)")[:, 0:2 * TOK].rearrange("p (a k) -> p a k", a=2)
        v1 = tuple(v[:, 0, :].rearrange("p (t d) -> p t d", t=TILES) for v in v0)
        prob = sb("prob", [P, 2, 512])
        prob_t = (sb("prob_hi", [P, 2, 512], F16), sb("prob_lo", [P, 2, 512], F16))
        low = sb("low", [P, 2, 4])
        sums0 = sb("sums0", [P, TILES, H0])
        sums1 = sb("sums1", [P, TILES, H1])
        inv = sb("inv", [P, TILES, H0])
        silu = sb("silu", [P, 512])
        inner = sb("inner", [P, 512])
        inner_t = sb("inner_t", [P, 2, FCH, TOK], F16)
        mask = sb("mask", [P, K_TWO])
        rope0 = sb("rope0", [P, 2, TILES, 2, HD0])
        rope1_sb = sb("rope1_sb", [P, TILES, TAB])
        ident = sb("ident", [P, P])
        ident16 = sb("ident16", [P, P], F16)
        bn = sb("bn", [P, TILES, 6])
        moments = sb("moments", [P, TILES, 2])
        squares = sb("squares", [P, TILES])
        shifted = sb("shifted", [P, TILES])
        rstd = sb("rstd", [P, TILES])
        minus_half = sb("minus_half", [P, TILES])
        gain0 = sb("gain0", [P, CH, SEQS])
        bias0 = sb("bias0", [P, CH, SEQS])
        gain1 = sb("gain1", [P, CH, SEQS])
        gain2 = sb("gain2", [P, CH, SEQS])
        b_ada = sb("b_ada", [P, 2 * CH])
        ln_w = sb("ln_w", [P, 2, CH])
        cond = silu[:, 0:CH * SEQS].rearrange("p (c s) -> p c s", c=CH)
        freq = silu[:, 64:64 + HD1 // 2]
        posf = silu[:, 128:128 + SEQS * TILES]
        pos = silu[:, 192:192 + SEQS * TILES].bitcast(I32)

        def bank(name):
            return ctx.enter_context(nc.psum_tensor(name, [P, 512], F32))

        score = [bank("score0"), bank("score1")]
        trans = [bank("trans0"), bank("trans1")]
        ybank = [bank("y0"), bank("y1")]
        gbank, ubank = bank("gate"), bank("up")

        stage = inner_t[:].rearrange("p a c t -> p (a c t)").bitcast(F32).rearrange(
            "p (s n) -> p s n", s=2)
        normed = stack[:].bitcast(F32)
        k_stack0 = stack[:, 0:2 * KV0 * ROWS0].rearrange("p (g a d) -> p g a d", a=3, d=HD0)
        q_stack0 = stack[:, 0:H0 * ROWS0].rearrange("p (h a d) -> p h a d", a=3, d=HD0)
        k_stack1 = stack[:, 0:512].rearrange("p (t a d) -> p t a d", a=4, d=HD1)
        q_stack1 = [stack[:, at:at + 1024].rearrange("p (h a d) -> p h a d", a=2, d=HD1)
                    for at in (1024, 0)]
        turns = work[:].rearrange("p t d -> p (t d)")
        reduced = x_mid[:].rearrange("p t d -> p (t d)")
        early = q_t[:].rearrange("p h t -> p (h t)").bitcast(F32)
        angle, table = early[:, 0:512], early[:, 512:2048]

        raw_in = [sem("raw_in0"), sem("raw_in1")]
        cond_in, const_in, pos_in = sem("cond_in"), sem("const_in"), sem("pos_in")
        raw_high, raw_split, cond_used = sem("raw_high"), sem("raw_split"), sem("cond_used")
        gains_made, ident_zero, ident_made = sem("gains_made"), sem("ident_zero"), sem("ident_made")
        half_made, prob_clear = sem("half_made"), sem("prob_clear")
        angle_step, angle_ready, sines, table_made, table_out = (
            sem("angle_step"), sem("angle_ready"), sem("sines"), sem("table_made"), sem("table_out"))
        x_arrived, rope_arrived, res_copied, out_stored = (
            sem("x_arrived"), sem("rope_arrived"), sem("res_copied"), sem("out_stored"))
        bn_raw, ln_stat, square_sum, eps_added, rstd_ready = (
            sem("bn_raw"), sem("ln_stat"), sem("square_sum"), sem("eps_added"), sem("rstd_ready"))
        work_ready, t_full, t_free, hi_done, norm_high = (
            sem("work_ready"), sem("t_full"), sem("t_free"), sem("hi_done"), sem("norm_high"))
        s_full, lat_low, near_low, terms_made = (
            sem("s_full"), sem("lat_low"), sem("near_low"), sem("terms_made"))
        y_full, weighted = sem("y_full"), sem("weighted")
        lat_high, v_high = sem("lat_high"), sem("v_high")
        rope_terms, rope_sum, stack_high, stack_again, stack_low = (
            sem("rope_terms"), sem("rope_sum"), sem("stack_high"), sem("stack_again"),
            sem("stack_low"))
        low_ready, pv_done, inv_ready = sem("low_ready"), sem("pv_done"), sem("inv_ready")
        mid_ready = sem("mid_ready")
        g_full, u_full, tanh_done, gated, inner_ready, inner_high, inner_low, d_full, d_read = (
            sem("g_full"), sem("u_full"), sem("tanh_done"), sem("gated"), sem("inner_ready"),
            sem("inner_high"), sem("inner_low"), sem("d_full"), sem("d_read"))

        def wide(ap):
            return ap.rearrange("(c p) n -> p c n", p=P)

        loads = []
        for part in range(2):
            loads.append([(wide(w_ada_t)[:, :, part * D:(part + 1) * D], CH, D, 0)])
        loads.append([(wide(tw1_t), CH, D, 0)])
        loads.append([(wide(tw2_t), CH, D, 0)])
        raw = len(loads)
        splits = []

        def split(parts, target):
            loads.append(parts)
            splits.append(target)

        n_lat = CH * LAT
        split([(wide(wkd_t), CH, LAT, 0)], [(wkd, 0, n_lat)])
        split([(wku_t, 1, P, 0), (wvu_t, 1, P, P)], [(wkv0, 0, 2 * P)])
        split([(wide(wq0_t), CH, D, 0)], [(wq0, 0, CH * D)])
        split([(wide(wo0_t), CH, D, 0)], [(wo0, 0, CH * D)])
        split([(wide(wk1_t), CH, HD1, 0), (wide(wv1_t), CH, HD1, CH * HD1)], None)
        split([(wide(wq1_t), CH, D, 0)], [(wq1, 0, CH * D)])
        split([(wide(wo1_t), CH, D, 0)], [(wo1, 0, CH * D)])
        for w, w_t in ((wg, wg_t), (wu, wu_t)):
            for c in range(CH):
                split([(w_t[c * P:(c + 1) * P, :], 1, FF, 0)], [(w, c * FF, FF)])
        for c in range(CH):
            split([(wide(wd_t[c * D:(c + 1) * D, :]), CH, D, 0)], [(wd, c * CH * D, CH * D)])

        landed = []
        got = [0, 0]
        for m, parts in enumerate(loads):
            got[m % 2] += 16 * len(parts)
            landed.append((raw_in[m % 2], got[m % 2]))

        def split_views(m, half):
            target = splits[m - raw]
            slot = stage[:, m % 2, :]
            if target is None:
                n = CH * HD1
                return [(slot[:, j * n:(j + 1) * n].rearrange("p (c k) -> p c k", c=CH),
                         wkv1[half][:, :, j * HD1:(j + 1) * HD1]) for j in range(2)]
            (w, at, n), = target
            return [(slot[:, 0:n], w[half][:].rearrange("p c n -> p (c n)")[:, at:at + n])]

        rope_tab = rope1.rearrange("(s t) p n -> s p t n", t=TILES)
        x_dram = x.rearrange("s (t p) d -> s p t d", p=P)
        out_dram = out.rearrange("s (t p) d -> s p t d", p=P)

        block = ctx.enter_context(nc.Block())

        @block.sync
        def _(sp):
            sp.dma_start(cond, cond_t.rearrange("(c p) s -> p c s", p=P)).then_inc(cond_in, 16)
            sp.dma_start(b_ada[:], b_ada_t).then_inc(cond_in, 16)
            sp.dma_start(ln_w[:, 0, :], ln1_w).then_inc(cond_in, 16)
            sp.dma_start(ln_w[:, 1, :], ln2_w).then_inc(cond_in, 16)
            sp.dma_start(pos, pos_t).then_inc(pos_in, 16)
            sp.dma_start(freq, freq_c).then_inc(pos_in, 16)
            for m, parts in enumerate(loads):
                if 2 <= m < raw + 2:
                    sp.wait_ge(cond_used, m - 1)
                elif m >= raw + 2:
                    sp.wait_ge(raw_split, m - raw - 1)
                for src, chunks, cols, at in parts:
                    dst = stage[:, m % 2, at:at + chunks * cols]
                    if chunks > 1:
                        dst = dst.rearrange("p (c n) -> p c n", c=chunks)
                    sp.dma_start(dst, src).then_inc(raw_in[m % 2], 16)
                if m == 1:
                    sp.dma_start(x_in[:], x_dram[0]).then_inc(x_arrived, 16)
                    sp.dma_start(mask[:], mask_c).then_inc(const_in, 16)
                    sp.dma_start(rope0[:].rearrange("p a t c d -> p (a t c d)"), rope0_c).then_inc(
                        const_in, 16)

            def ahead(n):
                need_apart(sp, mid_ready, count(n, 4, 2), (cond_used, 1))
                sp.dma_start(x_in[:], x_dram[index((n[0], n[1] + 1))]).then_inc(x_arrived, 16)
                need_apart(sp, rope_sum, count(n, 6, 6), (cond_used, 1))
                sp.dma_start(rope1_sb[:], rope_tab[index((n[0], n[1] + 1))]).then_inc(
                    rope_arrived, 16)

            def residual(n):
                need(sp, mid_ready, count(n, 4, 4))
                sp.dma_start(x_res[:], x_mid[:]).then_inc(res_copied, 16)

            def store(n):
                for t in range(TILES):
                    need_apart(sp, d_read, count(n, TILES, TILES + t + 1), (cond_used, 1))
                    sp.dma_start(out_dram[index(n)][:, t, :], x_res[:, t, :]).then_inc(
                        out_stored, 16)
                need_apart(sp, out_stored, count(n, 16 * TILES, 16 * TILES), (cond_used, 1))

            sp.wait_ge(table_out, 32)
            sp.dma_start(rope1_sb[:], rope_tab[0]).then_inc(rope_arrived, 16)
            ahead((None, 0))
            with sp.Fori(0, SEQS - 2) as i:
                residual((i, 0))
                ahead((i, 1))
                store((i, 0))
            residual((None, SEQS - 2))
            store((None, SEQS - 2))
            residual((None, SEQS - 1))
            store((None, SEQS - 1))

        @block.gpsimd
        def _(pool):
            pool.memset(ident[:], 0.0).then_inc(ident_zero, 1)
            pool.memset(minus_half[:], -0.5).then_inc(half_made, 1)
            pool.memset(prob[:], 0.0).then_inc(prob_clear, 1)
            pool.wait_ge(ident_zero, 1)
            pool.affine_select(out=ident[:], in_=ident[:], compare_op=ALU.not_equal, fill=1.0,
                               base=0, pattern=[[-1, P]], channel_multiplier=1).then_inc(
                                   ident_made, 1)
            pool.wait_ge(ident_made, 1)
            pool.tensor_copy(ident16[:], ident[:]).then_inc(ident_made, 1)
            pool.wait_ge(half_made, 1)

            def root(n, k):
                if k == 0:
                    need_apart(pool, ln_stat, count(n, 2, 2), (half_made, 1))
                    pool.tensor_scalar(shifted[:], moments[:, :, 1], LN_EPS, 1.0, ALU.add,
                                       ALU.mult).then_inc(eps_added, 1)
                else:
                    need_apart(pool, square_sum, count(n, 4, 2 * k), (half_made, 1))
                    pool.tensor_scalar(shifted[:], squares[:], 1.0 / D, RMS_EPS, ALU.mult,
                                       ALU.add).then_inc(eps_added, 1)
                need(pool, eps_added, count(n, 3, k + 1))
                pool.tensor_tensor(rstd[:], shifted[:], minus_half[:], ALU.pow).then_inc(
                    rstd_ready, 1)

            def inner_lows(n, pairs):
                for p in pairs:
                    need(pool, inner_high, count(n, PAIRS, p + 1))
                    pair = inner_t[:, :, 2 * p:2 * p + 2, :].rearrange("p a c t -> p a (c t)")
                    pool.tensor_tensor(pair[:, 1, :], inner[:], pair[:, 0, :],
                                       ALU.subtract).then_inc(inner_low, 1)

            def layers(n, mlp):
                for step, _ in PLAN:
                    if step in ("fill0", "fill2", "fill4"):
                        root(n, int(step[-1]) // 2)
                    if mlp is not None:
                        inner_lows(mlp, pairs_at(step, 4))

            layers((None, 0), None)
            with pool.Fori(0, SEQS - 1) as i:
                layers((i, 1), (i, 0))
            inner_lows((None, SEQS - 1), range(PAIRS))

        @block.scalar
        def _(act):
            def fill(n, f):
                for b in range(2):
                    use = T_FILL[f] + b
                    need(act, t_full, count(n, T_USES, use + 1))
                    for c in (2 * b, 2 * b + 1):
                        src = trans[use % 2][:, (c % 2) * TOK:(c % 2 + 1) * TOK]
                        at = index(n)
                        if f == 0:
                            ins = act.activation(
                                normed[:, c * TOK:(c + 1) * TOK], src, ACT.Identity, scale=gain0[:, c, bass.ds(at, 1)],
                                bias=bias0[:, c, bass.ds(at, 1)])
                        elif f in (1, 3):
                            if c % 2 == 0:
                                act.activation(act_t[0][:, c:c + 2, :].rearrange("p c t -> p (c t)"),
                                               trans[use % 2][:], ACT.Copy).then_inc(hi_done, 1)
                            continue
                        else:
                            g, to = (gain1, act_t) if f == 2 else (gain2, mlp_t)
                            ins = act.activation(to[0][:, c, :], src, ACT.Copy,
                                                 scale=g[:, c, bass.ds(at, 1)])
                        if c % 2 == 1:
                            ins.then_inc(hi_done, 1)

            def exps(n, layer, u):
                base = 0 if layer == 0 else UNITS0
                need(act, low_ready, count(n, UNITS, base + u + 1))
                t_unit = T_UNIT0 if layer == 0 else T_UNIT1
                if u >= 2:
                    need(act, t_full, count(n, T_USES, t_unit + u - 1))
                bank_ = score[((S_UNIT0 if layer == 0 else S_UNIT1) + u) % 2]
                slot = prob[:, u % 2, :]
                for j, (h, t, at, wid) in enumerate(unit_heads(layer, u)):
                    sums = (sums0 if layer == 0 else sums1)[:, t, h:h + 1]
                    ins = act.activation(slot[:, at:at + wid], bank_[:, at:at + wid], ACT.Exp,
                                         bias=low[:, u % 2, j:j + 1], scale=-1.0, accum_out=sums)
                ins.then_inc(terms_made, 1)

            def prob_highs(n, layer, u):
                t_unit = T_UNIT0 if layer == 0 else T_UNIT1
                base = 0 if layer == 0 else UNITS0
                need(act, t_full, count(n, T_USES, t_unit + u + 1))
                need(act, pv_done, count(n, UNITS, base + u - 1))
                act.activation(prob_t[0][:, u % 2, :], trans[(t_unit + u) % 2][:],
                               ACT.Copy).then_inc(hi_done, 1)

            def layers(n, mlp):
                def ahead(step):
                    if mlp is not None:
                        tanhs(mlp, pairs_at(step, 2))

                def behind(step):
                    if mlp is not None:
                        inner_highs(mlp, pairs_at(step, 4))

                def units(layer):
                    total = UNITS0 if layer == 0 else UNITS1
                    ahead(f"scores{layer}")
                    exps(n, layer, 0)
                    behind(f"scores{layer}")
                    for u in range(total):
                        if u + 1 < total:
                            exps(n, layer, u + 1)
                        ahead(f"unit{layer}_{u}")
                        prob_highs(n, layer, u)
                        behind(f"unit{layer}_{u}")

                def stack_high_half(step, k, used, dst, src, again=None, scale=1.0):
                    need(act, rope_sum, count(n, 6, k))
                    if used:
                        need(act, t_full, count(n, T_USES, used))
                    act.activation(dst, src, ACT.Copy, scale=scale).then_inc(stack_high, 1)
                    if again is not None:
                        need(act, stack_high, count(n, 6, k))
                        act.activation(again, dst, ACT.Copy).then_inc(stack_again, 1)
                    ahead(step)
                    behind(step)

                def from_stack(use, copies):
                    need(act, t_full, count(n, T_USES, use + 1))
                    for to, at in copies:
                        ins = act.activation(to, at, ACT.Copy)
                    ins.then_inc(t_free, 1)

                def whole_fill(f):
                    ahead(f"fill{f}")
                    fill(n, f)
                    behind(f"fill{f}")

                whole_fill(0)
                ahead("latent")
                need(act, s_full, count(n, S_USES, S_LAT + 1))
                src = score[S_LAT % 2]
                act.activation(lat[0][:, WINDOW:], src[:, 0:TOK], ACT.Copy, scale=1.0 / WS)
                act.activation(lat[0][:, 0:WINDOW], src[:, P - WINDOW:P], ACT.Copy,
                               scale=1.0 / WS).then_inc(lat_high, 1)
                behind("latent")
                ahead("query0")
                behind("query0")
                ahead("kv")
                need(act, s_full, count(n, S_USES, S_KV + 1))
                kv = score[S_KV % 2][:].rearrange("p (t n) -> p t n", t=TILES)
                act.activation(v0[0][:, 0:TILES, :], kv[:, :, P:2 * P], ACT.Copy,
                               scale=1.0 / WS).then_inc(v_high, 1)
                need(act, s_full, count(n, S_USES, S_NEAR + 1))
                act.activation(v0[0][0:K_NEAR, 2, :], score[S_NEAR % 2][0:K_NEAR, 0:P], ACT.Copy,
                               scale=1.0 / WS).then_inc(v_high, 1)
                behind("kv")
                ahead("query1")
                behind("query1")
                stack_high_half("keys", 1, 0, k_stack0[:, :, 0, :],
                                work[:, 0, 0:2 * P].rearrange("p (g d) -> p g d", d=HD0),
                                k_stack0[:, :, 2, :])
                keys = trans[T_K0 % 2][0:ROWS0].bitcast(F16).rearrange(
                    "p (t g k) -> p t g k", t=TILES, g=KV0)
                from_stack(T_K0, [(k0_t[:, :, 0:P], keys[:, 1]),
                                  (k0_t[:, :, P:P + WINDOW], keys[:, 0, :, P - WINDOW:P]),
                                  (k0_t[:, :, P + WINDOW:], keys[:, 0])])
                for t in range(TILES):
                    stack_high_half(f"stack{t}", 2 + t, T_Q0 + 2 * t, q_stack0[:, :, 0, :],
                                    work[:, 0, :].rearrange("p (h d) -> p h d", d=HD0),
                                    q_stack0[:, :, 1, :])
                    for b in range(2):
                        use = T_Q0 + 2 * t + b
                        from_stack(use, [(q_t[0:ROWS0, 8 * b:8 * b + 8, t * P:(t + 1) * P],
                                          trans[use % 2][0:ROWS0].bitcast(F16).rearrange(
                                              "p (h q) -> p h q", h=8))])
                units(0)
                whole_fill(1)
                ahead("out0")
                square(n, 0)
                behind("out0")
                whole_fill(2)
                ahead("kv1")
                need(act, s_full, count(n, S_USES, S_KV1 + 1))
                kv = score[S_KV1 % 2][:, 0:TILES * P].rearrange("p (t n) -> p t n", t=TILES)
                act.activation(v1[0], kv[:, :, HD1:P], ACT.Copy, scale=1.0 / WS).then_inc(
                    v_high, 1)
                behind("kv1")
                for step in ("query2", "query3"):
                    ahead(step)
                    behind(step)
                stack_high_half("keys1", 4, 0, k_stack1[:, :, 0, :],
                                work[:, 0, 0:P].rearrange("p (t d) -> p t d", t=TILES),
                                k_stack1[:, :, 1, :])
                from_stack(T_K1, [(k1_t.rearrange("p a (t k) -> p a t k", t=TILES),
                                   trans[T_K1 % 2][:].bitcast(F16)[:, 0:4 * P].rearrange(
                                       "p (t a k) -> p a t k", t=TILES, a=2))])
                for t in range(TILES):
                    stack_high_half(f"stack{2 + t}", 5 + t, (T_K1 + 1) * t,
                                    q_stack1[t][:, :, 0, :],
                                    work[:, 0, :].rearrange("p (h d) -> p h d", d=HD1),
                                    scale=-float(HD1) ** -0.5)
                    use = T_Q1 + t
                    from_stack(use, [(q_t[:, 0:H1, t * P:(t + 1) * P],
                                      trans[use % 2][:].bitcast(F16).rearrange(
                                          "p (h q) -> p h q", h=H1))])
                units(1)
                whole_fill(3)
                ahead("out1")
                square(n, 1)
                behind("out1")
                whole_fill(4)
                ahead("end")
                behind("end")

            def square(n, k):
                for t in range(TILES):
                    need(act, mid_ready, count(n, 4, 2 * k + t + 1))
                    act.activation(normed[:, t * D:(t + 1) * D], x_mid[:, t, :], ACT.Square,
                                   accum_out=squares[:, t:t + 1]).then_inc(square_sum, 1)

            def tanhs(n, pairs):
                for p in pairs:
                    need(act, g_full, count(n, PAIRS, p + 1))
                    if p > 0:
                        need(act, inner_ready, count(n, PAIRS, p))
                    act.activation(silu[:], gbank[:], ACT.Tanh, scale=0.5 / WS).then_inc(
                        tanh_done, 1)

            def inner_highs(n, pairs):
                for p in pairs:
                    need(act, inner_ready, count(n, PAIRS, p + 1))
                    act.activation(inner_t[:, 0, 2 * p:2 * p + 2, :].rearrange("p c t -> p (c t)"),
                                   inner[:], ACT.Copy).then_inc(inner_high, 1)

            for half in range(2):
                act.wait_ge(angle_ready, half + 1)
                act.activation(reduced, reduced, ACT.Sin).then_inc(sines, 1)
                act.wait_ge(table_made, half + 1)
                tiles = SEQS * TILES // 2
                act.dma_start(
                    rope1[half * tiles:(half + 1) * tiles].rearrange("t p n -> p t n"),
                    table.rearrange("p (t n) -> p t n", t=tiles)).then_inc(table_out, 16)
            for m in range(raw, len(loads)):
                act.wait_ge(*landed[m])
                views = split_views(m, 0)
                for v, (src, dst) in enumerate(views):
                    ins = act.activation(dst, src, ACT.Copy, scale=WS)
                ins.then_inc(raw_high, 1)
            act.wait_ge(gains_made, 4 * CH)
            act.wait_ge(prob_clear, 1)
            layers((None, 0), None)
            with act.Fori(0, SEQS - 1) as i:
                layers((i, 1), (i, 0))
            for p in range(PAIRS):
                tanhs((None, SEQS - 1), [p])
                inner_highs((None, SEQS - 1), [p])

        @block.vector
        def _(dve):
            def halves_low(n, f):
                for b in range(2):
                    need(dve, hi_done, count(n, HI_USES, HI_FILL[f] + b + 1))
                    if f == 0:
                        hi = act_t[0][:, 2 * b:2 * b + 2, :].rearrange("p c t -> p (c t)")
                        lo = act_t[1][:, 2 * b:2 * b + 2, :].rearrange("p c t -> p (c t)")
                        value = normed[:, b * 512:(b + 1) * 512]
                        dve.tensor_copy(hi, value).then_inc(norm_high, 1)
                        need(dve, norm_high, count(n, 2, b + 1))
                        dve.tensor_tensor(lo, value, hi, ALU.subtract).then_inc(
                            t_free, 1)
                    elif f in (1, 3):
                        hi = act_t[0][:, 2 * b:2 * b + 2, :].rearrange("p c t -> p (c t)")
                        lo = act_t[1][:, 2 * b:2 * b + 2, :].rearrange("p c t -> p (c t)")
                        dve.tensor_tensor(lo, trans[(T_FILL[f] + b) % 2][:], hi,
                                          ALU.subtract).then_inc(t_free, 1)
                    else:
                        g, to = (gain1, act_t) if f == 2 else (gain2, mlp_t)
                        for c in (2 * b, 2 * b + 1):
                            src = trans[(T_FILL[f] + b) % 2][:, (c % 2) * TOK:(c % 2 + 1) * TOK]
                            ins = dve.scalar_tensor_tensor(
                                to[1][:, c, :], src, g[:, c, bass.ds(index(n), 1)], to[0][:, c, :],
                                ALU.mult, ALU.subtract)
                        ins.then_inc(t_free, 1)

            def lows(n, layer, u):
                use = (S_UNIT0 if layer == 0 else S_UNIT1) + u
                need_apart(dve, s_full, count(n, S_USES, use + 1), (const_in, 32))
                bank_ = score[use % 2]
                if layer == 0:
                    for j, (h, t, at, wid) in enumerate(unit_heads(0, u)):
                        view = bank_[:, at:at + wid]
                        ins = dve.tensor_tensor_reduce(
                            out=view, in0=view, in1=mask[:, 0:wid], scale=1.0, scalar=3.0e38,
                            op0=ALU.add, op1=ALU.min, accum_out=low[:, u % 2, j:j + 1])
                else:
                    ins = dve.tensor_reduce(low[:, u % 2, 0:2], bank_[:].rearrange(
                        "p (h k) -> p h k", h=2), AX.X, ALU.min)
                ins.then_inc(low_ready, 1)

            def prob_lows(n, layer, u):
                t_unit = T_UNIT0 if layer == 0 else T_UNIT1
                need(dve, hi_done, count(n, HI_USES, HI_UNIT[layer] + u + 1))
                dve.tensor_tensor(prob_t[1][:, u % 2, :], trans[(t_unit + u) % 2][:],
                                  prob_t[0][:, u % 2, :], ALU.subtract).then_inc(t_free, 1)

            def between(mlp, step):
                if mlp is not None:
                    gates(mlp, pairs_at(step, 2))
                    inners(mlp, pairs_at(step, 4))
                    sums(mlp, tiles_at(step))

            def units(n, mlp, layer):
                total = UNITS0 if layer == 0 else UNITS1
                between(mlp, f"scores{layer}")
                lows(n, layer, 0)
                lows(n, layer, 1)
                for u in range(total):
                    between(mlp, f"unit{layer}_{u}")
                    if u + 2 < total:
                        lows(n, layer, u + 2)
                    prob_lows(n, layer, u)

            def normalise(n, layer):
                sums, hd, heads = (sums0, HD0, H0) if layer == 0 else (sums1, HD1, H1)
                for t in range(TILES):
                    done = (UNITS0 - 2, UNITS0, UNITS - 1, UNITS)[2 * layer + t]
                    need(dve, pv_done, count(n, UNITS, done))
                    dve.reciprocal(inv[:, t, 0:heads], sums[:, t, :]).then_inc(inv_ready, 1)
                    need(dve, inv_ready, count(n, 4, 2 * layer + t + 1))
                    dve.tensor_tensor(
                        work[:, t, :].rearrange("p (h d) -> p h d", d=hd),
                        ybank[t][:].rearrange("p (h d) -> p h d", d=hd),
                        inv[:, t, 0:heads].unsqueeze(2).broadcast_to([P, heads, hd]),
                        ALU.mult).then_inc(weighted, 1)

            def add(n, layer):
                use = S_OUT0 if layer == 0 else S_OUT1
                if layer == 0:
                    need(dve, res_copied, count((n[0], n[1] - 1), 16, 16))
                for t in range(TILES):
                    need(dve, s_full, count(n, S_USES, use + t + 1))
                    src = x_in if layer == 0 else x_mid
                    dve.scalar_tensor_tensor(x_mid[:, t, :], score[(use + t) % 2][:], 1.0 / WS,
                                             src[:, t, :], ALU.mult, ALU.add).then_inc(mid_ready, 1)

            def rotate0(n, ps, q_or_k, t, heads, dst, swap, done):
                view = ps.rearrange("p (h two d) -> p h two d", two=2, d=HD0 // 2)
                for c, (src, to) in enumerate(((view, dst), (view[:, :, ::-1, :], swap))):
                    table = rope0[:, q_or_k, t, c, :].rearrange("p (two d) -> p two d", two=2)
                    ins = dve.tensor_tensor(
                        to.rearrange("p (h two d) -> p h two d", two=2, d=HD0 // 2), src,
                        table.unsqueeze(1).broadcast_to([P, heads, 2, HD0 // 2]), ALU.mult)
                if done is not None:
                    ins.then_inc(done, 1)

            def rotate1(n, ps, t, heads, dst, swap, done):
                half = HD1 // 2
                view = ps.rearrange("p (h two d) -> p h two d", two=2, d=half)
                cos = rope1_sb[:, t, 0:half].unsqueeze(1).unsqueeze(1).broadcast_to(
                    [P, heads, 2, half])
                sin = rope1_sb[:, t, half:].rearrange("p (two d) -> p two d", two=2).unsqueeze(
                    1).broadcast_to([P, heads, 2, half])
                for src, to, table in ((view, dst, cos), (view[:, :, ::-1, :], swap, sin)):
                    ins = dve.tensor_tensor(
                        to.rearrange("p (h two d) -> p h two d", two=2, d=half), src, table,
                        ALU.mult)
                if done is not None:
                    ins.then_inc(done, 1)

            def rope_add(n, k, size):
                need(dve, rope_terms, count(n, 6, k + 1))
                dve.tensor_tensor(work[:, 0, 0:size], work[:, 0, 0:size], work[:, 1, 0:size],
                                  ALU.add).then_inc(rope_sum, 1)
                need(dve, stack_high, count(n, 6, k + 1))

            def layer0(n, mlp):
                need(dve, x_arrived, count(n, 16, 16))
                for t in range(TILES):
                    dve.bn_stats(bn[:, t, :], x_in[:, t, :]).then_inc(bn_raw, 1)
                for t in range(TILES):
                    need_apart(dve, bn_raw, count(n, 2, t + 1), (const_in, 32))
                    dve.bn_aggr(moments[:, t, :], bn[:, t, :]).then_inc(ln_stat, 1)
                need(dve, rstd_ready, count(n, 3, 1))
                for t in range(TILES):
                    dve.tensor_scalar(work[:, t, :], x_in[:, t, :], moments[:, t, 0:1],
                                      rstd[:, t:t + 1], ALU.subtract, ALU.mult).then_inc(
                                          work_ready, 1)
                between(mlp, "fill0")
                halves_low(n, 0)
                between(mlp, "latent")
                need(dve, lat_high, count(n, 1, 1))
                src = score[S_LAT % 2]
                dve.scalar_tensor_tensor(lat[1][:, WINDOW:], src[:, 0:TOK], 1.0 / WS,
                                         lat[0][:, WINDOW:], ALU.mult, ALU.subtract)
                dve.scalar_tensor_tensor(lat[1][:, 0:WINDOW], src[:, P - WINDOW:P], 1.0 / WS,
                                         lat[0][:, 0:WINDOW], ALU.mult,
                                         ALU.subtract).then_inc(lat_low, 1)
                between(mlp, "query0")
                between(mlp, "kv")
                need(dve, v_high, count(n, 3, 1))
                kv = score[S_KV % 2][:].rearrange("p (t n) -> p t n", t=TILES)
                dve.scalar_tensor_tensor(v0[1][:, 0:TILES, :], kv[:, :, P:2 * P], 1.0 / WS,
                                         v0[0][:, 0:TILES, :], ALU.mult, ALU.subtract)
                for t in range(TILES):
                    rotate0(n, kv[:, t, 0:P], 1, t, KV0, work[:, 0, t * P:(t + 1) * P],
                            work[:, 1, t * P:(t + 1) * P],
                            None if t == 0 else rope_terms)
                need(dve, v_high, count(n, 3, 2))
                dve.scalar_tensor_tensor(v0[1][0:K_NEAR, 2, :], score[S_NEAR % 2][0:K_NEAR, 0:P],
                                         1.0 / WS, v0[0][0:K_NEAR, 2, :], ALU.mult,
                                         ALU.subtract).then_inc(near_low, 1)
                between(mlp, "query1")
                rope_add(n, 0, 2 * P)
                dve.tensor_tensor(k_stack0[:, :, 1, :], work[:, 0, 0:2 * P].rearrange(
                    "p (g d) -> p g d", d=HD0), k_stack0[:, :, 0, :], ALU.subtract).then_inc(
                        stack_low, 1)
                between(mlp, "keys")
                for t in range(TILES):
                    need(dve, y_full, count(n, 4, t + 1))
                    need(dve, stack_low, count(n, 6, 1 + t))
                    rotate0(n, ybank[t][:], 0, t, H0, work[:, 0, :], work[:, 1, :], rope_terms)
                    rope_add(n, 1 + t, D)
                    dve.tensor_tensor(q_stack0[:, :, 2, :], work[:, 0, :].rearrange(
                        "p (h d) -> p h d", d=HD0), q_stack0[:, :, 0, :], ALU.subtract).then_inc(
                            stack_low, 1)
                    between(mlp, f"stack{t}")
                units(n, mlp, 0)
                normalise(n, 0)
                between(mlp, "fill1")
                halves_low(n, 1)
                between(mlp, "out0")
                add(n, 0)

            def rms(n, k):
                need(dve, rstd_ready, count(n, 3, k + 1))
                for t in range(TILES):
                    dve.tensor_scalar(work[:, t, :], x_mid[:, t, :], rstd[:, t:t + 1], None,
                                      ALU.mult).then_inc(work_ready, 1)

            def layer1(n, mlp):
                rms(n, 1)
                between(mlp, "fill2")
                halves_low(n, 2)
                between(mlp, "kv1")
                need(dve, v_high, count(n, 3, 3))
                kv = score[S_KV1 % 2][:, 0:TILES * P].rearrange("p (t n) -> p t n", t=TILES)
                dve.scalar_tensor_tensor(v1[1], kv[:, :, HD1:P], 1.0 / WS, v1[0], ALU.mult,
                                         ALU.subtract)
                need(dve, rope_arrived, count(n, 16, 16))
                for t in range(TILES):
                    rotate1(n, kv[:, t, 0:HD1], t, 1, work[:, 0, t * HD1:(t + 1) * HD1],
                            work[:, 1, t * HD1:(t + 1) * HD1], None if t == 0 else rope_terms)
                for step in ("query2", "query3"):
                    between(mlp, step)
                rope_add(n, 3, P)
                for a in (2, 3):
                    ins = dve.tensor_tensor(k_stack1[:, :, a, :], work[:, 0, 0:P].rearrange(
                        "p (t d) -> p t d", t=TILES), k_stack1[:, :, 0, :], ALU.subtract)
                ins.then_inc(stack_low, 1)
                between(mlp, "keys1")
                for t in range(TILES):
                    need(dve, y_full, count(n, 4, 2 + t + 1))
                    need(dve, stack_low, count(n, 6, 4 + t))
                    rotate1(n, ybank[t][:], t, H1, work[:, 0, :], work[:, 1, :], rope_terms)
                    rope_add(n, 4 + t, D)
                    dve.scalar_tensor_tensor(
                        q_stack1[t][:, :, 1, :], work[:, 0, :].rearrange("p (h d) -> p h d", d=HD1),
                        -float(HD1) ** -0.5, q_stack1[t][:, :, 0, :], ALU.mult,
                        ALU.subtract).then_inc(stack_low, 1)
                    between(mlp, f"stack{2 + t}")
                units(n, mlp, 1)
                normalise(n, 1)
                between(mlp, "fill3")
                halves_low(n, 3)
                between(mlp, "out1")
                add(n, 1)
                rms(n, 2)
                between(mlp, "fill4")
                halves_low(n, 4)
                between(mlp, "end")

            def gates(n, pairs):
                for p in pairs:
                    need(dve, tanh_done, count(n, PAIRS, p + 1))
                    dve.scalar_tensor_tensor(silu[:], silu[:], 1.0, gbank[:], ALU.add,
                                             ALU.mult).then_inc(gated, 1)

            def inners(n, pairs):
                for p in pairs:
                    need(dve, u_full, count(n, PAIRS, p + 1))
                    need(dve, gated, count(n, PAIRS, p + 1))
                    if p > 0:
                        need(dve, inner_high, count(n, PAIRS, p))
                        need(dve, inner_low, count(n, PAIRS, p))
                    dve.scalar_tensor_tensor(inner[:], ubank[:], 0.5 * HS / (WS * WS), silu[:],
                                             ALU.mult, ALU.mult).then_inc(inner_ready, 1)

            def sums(n, tiles):
                for t in tiles:
                    need(dve, res_copied, count(n, 16, 16))
                    need(dve, d_full, count(n, TILES, t + 1))
                    dve.scalar_tensor_tensor(x_res[:, t, :], (gbank, ubank)[t][:],
                                             1.0 / (WS * HS), x_res[:, t, :], ALU.mult,
                                             ALU.add).then_inc(d_read, 1)

            steps = [0]

            def step(ins):
                steps[0] += 1
                ins.then_inc(angle_step, 1)
                dve.wait_ge(angle_step, steps[0])

            tiles = SEQS * TILES // 2
            dve.wait_ge(pos_in, 32)
            step(dve.tensor_copy(posf, pos))
            for half in range(2):
                step(dve.tensor_tensor(
                    angle.rearrange("p (t f) -> p t f", t=tiles),
                    posf[:, half * tiles:(half + 1) * tiles].unsqueeze(2).broadcast_to(
                        [P, tiles, HD1 // 2]),
                    freq.unsqueeze(1).broadcast_to([P, tiles, HD1 // 2]), ALU.mult))
                for c in range(2):
                    t_c = turns[:, c * 512:(c + 1) * 512]
                    r_c = reduced[:, c * 512:(c + 1) * 512]
                    step(dve.tensor_scalar(t_c, angle, 1.0 / (2 * np.pi), 0.25 * (1 - c), ALU.mult,
                                           ALU.add))
                    step(dve.tensor_scalar(t_c, t_c, ROUND, None, ALU.add))
                    step(dve.tensor_scalar(t_c, t_c, -ROUND, None, ALU.add))
                    step(dve.scalar_tensor_tensor(r_c, t_c, -TWO_PI_1, angle, ALU.mult, ALU.add))
                    step(dve.scalar_tensor_tensor(r_c, t_c, -TWO_PI_2, r_c, ALU.mult, ALU.add))
                    step(dve.scalar_tensor_tensor(r_c, t_c, -TWO_PI_3, r_c, ALU.mult, ALU.add))
                    if c == 0:
                        step(dve.tensor_scalar(r_c, r_c, float(np.pi / 2), None, ALU.add))
                dve.tensor_scalar(reduced, reduced, PI_IN, -PI_IN, ALU.min, ALU.max).then_inc(
                    angle_ready, 1)
                dve.wait_ge(sines, half + 1)
                if half == 1:
                    dve.wait_ge(table_out, 16)
                tab = table.rearrange("p (t n) -> p t n", t=tiles)
                f = HD1 // 2
                for at, c, sign in ((0, 0, 1.0), (f, 1, -1.0), (2 * f, 1, 1.0)):
                    ins = dve.tensor_scalar(
                        tab[:, :, at:at + f],
                        reduced[:, c * 512:(c + 1) * 512].rearrange("p (t f) -> p t f", t=tiles),
                        sign / WS, None, ALU.mult)
                ins.then_inc(table_made, 1)
            dve.wait_ge(cond_used, raw)
            dve.wait_ge(cond_in, 64)
            mod = ybank[0][:, 0:4 * CH * SEQS].rearrange("p (m s) -> p m s", s=SEQS)
            for c in range(CH):
                dve.tensor_scalar(gain0[:, c, :], mod[:, c, :], b_ada[:, c:c + 1], 1.0, ALU.add,
                                  ALU.add).then_inc(gains_made, 1)
                dve.tensor_scalar(bias0[:, c, :], mod[:, CH + c, :], b_ada[:, CH + c:CH + c + 1],
                                  None, ALU.add).then_inc(gains_made, 1)
                dve.tensor_scalar(gain1[:, c, :], mod[:, 2 * CH + c, :], 1.0, ln_w[:, 0, c:c + 1],
                                  ALU.add, ALU.mult).then_inc(gains_made, 1)
                dve.tensor_scalar(gain2[:, c, :], mod[:, 3 * CH + c, :], 1.0, ln_w[:, 1, c:c + 1],
                                  ALU.add, ALU.mult).then_inc(gains_made, 1)
            for m in range(raw, len(loads)):
                dve.wait_ge(raw_high, m - raw + 1)
                for (src, dst), (_, hi) in zip(split_views(m, 1), split_views(m, 0)):
                    ins = dve.scalar_tensor_tensor(dst, src, WS, hi, ALU.mult, ALU.subtract)
                ins.then_inc(raw_split, 1)
            dve.wait_ge(const_in, 32)
            dve.wait_ge(gains_made, 4 * CH)
            dve.wait_ge(table_out, 32)
            dve.sem_inc(d_read, TILES)
            layer0((None, 0), None)
            layer1((None, 0), None)
            with dve.Fori(0, SEQS - 1) as i:
                layer0((i, 1), (i, 0))
                layer1((i, 1), (i, 0))
            for p in range(PAIRS):
                gates((None, SEQS - 1), [p])
                inners((None, SEQS - 1), [p])
            sums((None, SEQS - 1), range(TILES))

        @block.tensor
        def _(pe):
            def product(out_ap, left, right, start=True, stop=True):
                pe.matmul(out_ap, left[0], right[0], start=start, stop=False)
                pe.matmul(out_ap, left[0], right[1], start=False, stop=False)
                return pe.matmul(out_ap, left[1], right[0], start=False, stop=stop)

            def cut(pair, *at):
                return pair[0][at], pair[1][at]

            def events():
                return {"lat_low": lat_low, "rope_terms": rope_terms, "near_low": near_low,
                        "terms_made": terms_made, "mid_ready": mid_ready}

            def score_bank(n, use):
                m, last = before(n, use, S_USES)
                name, per, k = S_READ[last]
                need(pe, events()[name], count(m, per, k))
                return score[use % 2]

            def trans_bank(n, use):
                m, last = before(n, use, T_USES)
                need(pe, t_free, count(m, T_USES, last + 1))
                return trans[use % 2]

            def fill(n, f):
                for b in range(2):
                    bank_ = trans_bank(n, T_FILL[f] + b)
                    for t in range(TILES):
                        if b == 0:
                            if f in (1, 3):
                                need(pe, weighted, count(n, 4, f - 1 + t + 1))
                            else:
                                need(pe, work_ready, count(n, 6, f + t + 1))
                        for c in (2 * b, 2 * b + 1):
                            ins = pe.transpose(bank_[:, (c % 2) * TOK + t * P:][:, 0:P],
                                               work[:, t, c * P:(c + 1) * P], ident[:])
                    ins.then_inc(t_full, 1)

            def token_major(out_ap, src, t, w, cols):
                for c in range(CH):
                    ins = product(out_ap, cut(src, slice(None), c, slice(t * P, (t + 1) * P)),
                                  cut(w, slice(None), c, slice(0, cols)), c == 0, c == CH - 1)
                return ins

            def queries(n, layer, t, w):
                if layer == 0:
                    need(pe, weighted, count((n[0], n[1] - 1), 4, 2 + t + 1))
                else:
                    need(pe, weighted, count(n, 4, t + 1))
                token_major(ybank[t][:], act_t, t, w, D).then_inc(y_full, 1)

            def stacks(n, use, k, again, rows, at, heads):
                bank_ = trans_bank(n, use)[0:rows].bitcast(F16)
                need(pe, stack_low, count(n, 6, k))
                if again:
                    need(pe, stack_again, count(n, 4, again))
                for m in range(heads):
                    ins = pe.transpose(bank_[:, m * P:(m + 1) * P],
                                       stack[:, at + m * rows:at + (m + 1) * rows], ident16[:])
                ins.then_inc(t_full, 1)

            def unit_scores(n, layer, u):
                bank_ = score_bank(n, (S_UNIT0 if layer == 0 else S_UNIT1) + u)
                for h, t, at, wid in unit_heads(layer, u):
                    q = q_t[0:(ROWS0, P)[layer], h, t * P:(t + 1) * P]
                    if layer == 0:
                        first = 0 if t else P + WINDOW
                        ins = pe.matmul(bank_[:, at:at + wid], q,
                                        k0_t[:, h // (H0 // KV0), first:first + wid], start=True,
                                        stop=True)
                    else:
                        pe.matmul(bank_[:, at:at + wid], q, k1_t[:, 0, :], start=True, stop=False)
                        ins = pe.matmul(bank_[:, at:at + wid], q, k1_t[:, 1, :], start=False,
                                        stop=True)
                ins.then_inc(s_full, 1)

            def unit_transposes(n, layer, u):
                need(pe, terms_made, count(n, UNITS, layer * UNITS0 + u + 1))
                bank_ = trans_bank(n, (T_UNIT0 if layer == 0 else T_UNIT1) + u)
                for b in range(4):
                    ins = pe.transpose(bank_[:, b * P:(b + 1) * P],
                                       prob[:, u % 2, b * P:(b + 1) * P], ident[:])
                ins.then_inc(t_full, 1)

            def unit_values(n, layer, u):
                need(pe, t_free, count(n, T_USES, (T_UNIT0 if layer == 0 else T_UNIT1) + u + 1))
                for h, t, at, wid in unit_heads(layer, u):
                    if layer == 0:
                        if h == 0:
                            need(pe, rope_terms, count(n, 6, 1 + t + 1))
                        g = h // (H0 // KV0)
                        out_ap = ybank[t][:, h * HD0:(h + 1) * HD0]
                        blocks = [(at, P, 0)] if t == 0 else [(at, P, 1), (at + P, K_NEAR, 2)]
                        for m, (col, rows, tile) in enumerate(blocks):
                            ins = product(
                                out_ap, cut(prob_t, slice(0, rows), u % 2, slice(col, col + P)),
                                cut(v0, slice(0, rows), tile, slice(g * HD0, (g + 1) * HD0)),
                                m == 0, m == len(blocks) - 1)
                    else:
                        if h == 0:
                            need(pe, rope_terms, count(n, 6, 4 + t + 1))
                        out_ap = ybank[t][:, h * HD1:(h + 1) * HD1]
                        for m in range(TILES):
                            ins = product(
                                out_ap,
                                cut(prob_t, slice(None), u % 2, slice(at + m * P, at + m * P + P)),
                                cut(v1, slice(None), m, slice(None)), m == 0, m == TILES - 1)
                ins.then_inc(pv_done, 1)

            def units(n, mlp, layer):
                total = UNITS0 if layer == 0 else UNITS1
                between(mlp, f"scores{layer}")
                unit_scores(n, layer, 0)
                unit_scores(n, layer, 1)
                for u in range(total):
                    between(mlp, f"unit{layer}_{u}")
                    if u + 2 < total:
                        unit_scores(n, layer, u + 2)
                    unit_transposes(n, layer, u)
                    if u > 0:
                        unit_values(n, layer, u - 1)
                unit_values(n, layer, total - 1)

            def project(n, layer, w):
                for t in range(TILES):
                    bank_ = score_bank(n, (S_OUT0 if layer == 0 else S_OUT1) + t)
                    if t == 0:
                        need(pe, t_free, count(n, T_USES, T_FILL[1 if layer == 0 else 3] + 2))
                    token_major(bank_[:], act_t, t, w, D).then_inc(s_full, 1)

            def layer0(n, mlp):
                between(mlp, "fill0")
                fill(n, 0)
                between(mlp, "latent")
                bank_ = score_bank(n, S_LAT)
                for c in range(CH):
                    if c % 2 == 0:
                        need(pe, t_free, count(n, T_USES, T_FILL[0] + c // 2 + 1))
                    ins = product(bank_[:, 0:TOK], cut(wkd, slice(None), c, slice(None)),
                                  cut(act_t, slice(None), c, slice(None)), c == 0, c == CH - 1)
                ins.then_inc(s_full, 1)
                between(mlp, "query0")
                queries(n, 0, 0, wq0)
                between(mlp, "kv")
                bank_ = score_bank(n, S_KV)
                need(pe, lat_low, count(n, 1, 1))
                for t in range(TILES):
                    ins = product(bank_[:, t * TOK:(t + 1) * TOK],
                                  cut(lat, slice(None), slice(WINDOW + t * P, WINDOW + t * P + P)),
                                  cut(wkv0, slice(None), 0, slice(None)))
                ins.then_inc(s_full, 1)
                bank_ = score_bank(n, S_NEAR)
                product(bank_[0:K_NEAR, 0:P], cut(lat, slice(None), slice(0, K_NEAR)),
                        cut(wkv0, slice(None), 0, slice(P, 2 * P))).then_inc(s_full, 1)
                between(mlp, "query1")
                queries(n, 0, 1, wq0)
                between(mlp, "keys")
                stacks(n, T_K0, 1, 1, ROWS0, 0, TILES * KV0)
                for t in range(TILES):
                    between(mlp, f"stack{t}")
                    for b in range(2):
                        stacks(n, T_Q0 + 2 * t + b, 2 + t, 2 + t, ROWS0, 8 * b * ROWS0, 8)
                need(pe, t_free, count(n, T_USES, T_Q0 + 4))
                units(n, mlp, 0)
                between(mlp, "fill1")
                fill(n, 1)
                between(mlp, "out0")
                project(n, 0, wo0)

            def layer1(n, mlp):
                between(mlp, "fill2")
                fill(n, 2)
                between(mlp, "kv1")
                bank_ = score_bank(n, S_KV1)
                need(pe, t_free, count(n, T_USES, T_FILL[2] + 2))
                for t in range(TILES):
                    ins = token_major(bank_[:, t * P:(t + 1) * P], act_t, t, wkv1, P)
                ins.then_inc(s_full, 1)
                for t in range(TILES):
                    between(mlp, f"query{2 + t}")
                    queries(n, 1, t, wq1)
                between(mlp, "keys1")
                stacks(n, T_K1, 4, 4, P, 0, 2 * TILES)
                for t, at in enumerate((1024, 0)):
                    between(mlp, f"stack{2 + t}")
                    stacks(n, T_Q1 + t, 5 + t, 0, P, at, H1)
                need(pe, t_free, count(n, T_USES, T_Q1 + 2))
                units(n, mlp, 1)
                between(mlp, "fill3")
                fill(n, 3)
                between(mlp, "out1")
                project(n, 1, wo1)
                between(mlp, "fill4")
                fill(n, 4)
                between(mlp, "end")

            def mlp_part(n, part):
                if part < 4 * PAIRS:
                    p, kind, m = part // 4, part // 2 % 2, part % 2
                    w, bank_, full, read = ((wg, gbank, g_full, gated),
                                            (wu, ubank, u_full, inner_ready))[kind]
                    if part == 0:
                        need(pe, t_free, count(n, T_USES, T_USES))
                    if m == 0:
                        if p > 0:
                            need(pe, read, count(n, PAIRS, p))
                        else:
                            need(pe, d_read, count(n, TILES, 1 + kind))
                    f = 2 * p + m
                    for c in range(CH):
                        ins = product(bank_[:, m * TOK:(m + 1) * TOK],
                                      cut(w, slice(None), c, slice(f * P, (f + 1) * P)),
                                      cut(mlp_t, slice(None), c, slice(None)), c == 0, c == CH - 1)
                    if m == 1:
                        ins.then_inc(full, 1)
                    return
                t, j = divmod(part - 4 * PAIRS, PAIRS)
                if t == 0:
                    if j == 0:
                        need(pe, gated, count(n, PAIRS, PAIRS))
                    need(pe, inner_high, count(n, PAIRS, j + 1))
                    need(pe, inner_low, count(n, PAIRS, j + 1))
                elif j == 0:
                    need(pe, inner_ready, count(n, PAIRS, PAIRS))
                cols = slice(t * P, (t + 1) * P)
                for f in (2 * j, 2 * j + 1):
                    ins = product((gbank, ubank)[t][:],
                                  (inner_t[:, 0, f, cols], inner_t[:, 1, f, cols]),
                                  cut(wd, slice(None), f, slice(None)), f == 0, f == FCH - 1)
                if j == PAIRS - 1:
                    ins.then_inc(d_full, 1)

            def between(mlp, step):
                if mlp is not None:
                    for part in parts_at(step):
                        mlp_part(mlp, part)

            pe.wait_ge(cond_in, 64)
            mod = ybank[0][:, 0:4 * CH * SEQS].rearrange("p (m s) -> p m s", s=SEQS)
            for m in range(raw):
                pe.wait_ge(*landed[m])
                slot = stage[:, m % 2, :].rearrange("p (c n) -> p c n", c=CH)
                for j in range(CH):
                    for c in range(CH):
                        ins = pe.matmul(mod[:, m * CH + j, :], slot[:, c, j * P:(j + 1) * P],
                                        cond[:, c, :], start=c == 0, stop=c == CH - 1)
                ins.then_inc(cond_used, 1)
            pe.wait_ge(ident_made, 2)
            pe.wait_ge(gains_made, 4 * CH)
            pe.wait_ge(raw_split, len(loads) - raw)
            layer0((None, 0), None)
            layer1((None, 0), None)
            with pe.Fori(0, SEQS - 1) as i:
                layer0((i, 1), (i, 0))
                layer1((i, 1), (i, 0))
            for part in range(PARTS):
                mlp_part((None, SEQS - 1), part)


def key_mask():
    q = np.arange(P)[:, None]
    own = np.arange(P)[None, :]
    own_ok = (np.abs(q - own) <= WINDOW) | (own % GLOBAL == 0)
    near = np.arange(P - WINDOW, P)[None, :]
    near_ok = (q + P - near <= WINDOW) | (near % GLOBAL == 0)
    ok = np.concatenate([own_ok, near_ok, np.ones((P, 1), bool)], axis=1)
    return np.where(ok, 0.0, NEG).astype(np.float32)


def frequencies(width):
    f = np.float32(1.0) / np.float32(10000.0) ** (np.arange(0, width, 2, dtype=np.float32)
                                                  / np.float32(width))
    return f.astype(np.float32)


def rope_table0():
    angle = np.arange(TOK, dtype=np.float32)[:, None] * frequencies(HD0)[None, :]
    cos, sin = np.cos(angle.astype(np.float64)), np.sin(angle.astype(np.float64))
    one = np.stack([np.concatenate([cos, cos], 1), np.concatenate([-sin, sin], 1)], 1)
    both = np.stack([one * (-(HD0 ** -0.5) / WS), one / WS])
    both = both.reshape(2, TILES, P, 2, HD0).transpose(2, 0, 1, 3, 4)
    return np.ascontiguousarray(both.reshape(P, -1).astype(np.float32))


def kernel(**inputs):
    import concourse.bacc as bacc
    from concourse.bass_utils import run_bass_kernel_spmd

    def get(name):
        return np.asarray(inputs[name])

    def turned(name):
        return np.ascontiguousarray(get(name).T)

    def by_feature(v):
        return np.ascontiguousarray(v.reshape(-1, P).T)

    arrays = {
        "x": np.ascontiguousarray(get("x")),
        "cond_t": turned("cond_2048"),
        "pos_t": np.ascontiguousarray(get("pos_BxS").reshape(SEQS * TILES, P).T),
        "w_ada_t": turned("L0_cond_W_ada"), "b_ada_t": by_feature(get("L0_cond_b_ada")),
        "wq0_t": turned("L0_cond_Wq"), "wkd_t": turned("L0_cond_Wkd"),
        "wku_t": turned("L0_cond_Wku"), "wvu_t": turned("L0_cond_Wvu"),
        "wo0_t": turned("L0_cond_Wo"),
        "ln1_w": by_feature(get("L1_cond_ln1_w")), "tw1_t": turned("L1_cond_ln1_tw"),
        "ln2_w": by_feature(get("L1_cond_ln2_w")), "tw2_t": turned("L1_cond_ln2_tw"),
        "wq1_t": turned("L1_cond_Wq"), "wk1_t": turned("L1_cond_Wk"),
        "wv1_t": turned("L1_cond_Wv"), "wo1_t": turned("L1_cond_Wo"),
        "wg_t": turned("L1_cond_Wg"), "wu_t": turned("L1_cond_Wu"), "wd_t": turned("L1_cond_Wd"),
        "mask_c": key_mask(), "rope0_c": rope_table0(),
        "freq_c": np.ascontiguousarray(np.broadcast_to(frequencies(HD1), (P, HD1 // 2))),
    }
    nc = bacc.Bacc("TRN2", target_bir_lowering=False, num_devices=1)
    args = {name: nc.dram_tensor(name + "_dram", a.shape, mybir.dt.from_np(a.dtype),
                                 kind="ExternalInput").ap() for name, a in arrays.items()}
    args["rope1"] = nc.dram_tensor("rope1_dram", (SEQS * TILES, P, TAB), F32, kind="Internal").ap()
    args["out"] = nc.dram_tensor("out_dram", (SEQS, TOK, D), F32, kind="ExternalOutput").ap()
    build(nc, **args)
    result = run_bass_kernel_spmd(nc, [{name + "_dram": a for name, a in arrays.items()}],
                                  core_ids=[0])
    return result.results[0]["out_dram"]
```

```python
from contextlib import ExitStack

import numpy as np

import concourse.bass as bass
from concourse import mybir

ALU = mybir.AluOpType
ACT = mybir.ActivationFunctionType
AX = mybir.AxisListType
F32 = mybir.dt.float32
F16 = mybir.dt.float16
I32 = mybir.dt.int32

P = 128
SEQS, TOK, D = 16, 256, 512
TILES = TOK // P
CH = D // P
FF = 2048
FCH = FF // P
PAIRS = FCH // 2
H0, KV0, HD0 = 16, 4, 32
H1, HD1 = 8, 64
LAT = 128
WINDOW, GLOBAL = 64, 64
LN_EPS, RMS_EPS = 1e-5, 1e-6
WS = 64.0
HS = 1.0 / 16.0
NEG = 1.0e30
K_OWN, K_NEAR = P, WINDOW + 1
K_TWO = K_OWN + K_NEAR
ROWS0 = 3 * HD0
TAB = 3 * HD1 // 2
ROUND = 1.5 * 2.0 ** 23
TWO_PI_1, TWO_PI_2 = 6.28125, 0.00193500518798828125
TWO_PI_3 = float(2 * np.pi - TWO_PI_1 - TWO_PI_2)
PI_IN = 3.1415925

UNITS0, UNITS1 = 12, 8
UNITS = UNITS0 + UNITS1
S_READ = ([("lat_low", 1, 1), ("rope_terms", 6, 1), ("near_low", 1, 1)]
          + [("terms_made", UNITS, u + 1) for u in range(UNITS0)]
          + [("mid_ready", 4, 1), ("mid_ready", 4, 2), ("rope_terms", 6, 4)]
          + [("terms_made", UNITS, UNITS0 + u + 1) for u in range(UNITS1)]
          + [("mid_ready", 4, 3), ("mid_ready", 4, 4)])
S_USES = len(S_READ)
S_LAT, S_KV, S_NEAR, S_UNIT0 = range(4)
S_OUT0 = S_UNIT0 + UNITS0
S_KV1 = S_OUT0 + TILES
S_UNIT1 = S_KV1 + 1
S_OUT1 = S_UNIT1 + UNITS1
T_FILL0, T_K0, T_Q0, T_UNIT0 = 0, 2, 3, 7
T_K1 = T_UNIT0 + UNITS0 + 4
T_Q1, T_UNIT1 = T_K1 + 1, T_K1 + 3
T_FILL = [T_FILL0, T_K1 - 4, T_K1 - 2, T_UNIT1 + UNITS1, T_UNIT1 + UNITS1 + 2]
T_USES = T_FILL[4] + 2
HI_FILL = [0, 2 + UNITS0, 4 + UNITS0, 6 + UNITS, 8 + UNITS]
HI_UNIT = [2, 6 + UNITS0]
HI_USES = 10 + UNITS


PARTS = 4 * PAIRS + TILES * PAIRS
PLAN = [("fill0", 2), ("latent", 2), ("query0", 0), ("kv", 0), ("query1", 1), ("keys", 0),
        ("stack0", 3), ("stack1", 3), ("scores0", 0), ("unit0_0", 1), ("unit0_1", 1),
        ("unit0_2", 0), ("unit0_3", 1), ("unit0_4", 1), ("unit0_5", 1), ("unit0_6", 1),
        ("unit0_7", 1), ("unit0_8", 1), ("unit0_9", 1), ("unit0_10", 1), ("unit0_11", 0),
        ("fill1", 1), ("out0", 2), ("fill2", 4), ("kv1", 2), ("query2", 0), ("query3", 0),
        ("keys1", 0), ("stack2", 3), ("stack3", 2), ("scores1", 1), ("unit1_0", 1),
        ("unit1_1", 1), ("unit1_2", 1), ("unit1_3", 0), ("unit1_4", 1), ("unit1_5", 0),
        ("unit1_6", 0), ("unit1_7", 0), ("fill3", 1), ("out1", 2), ("fill4", 3)]
BEFORE = {name: sum(parts for _, parts in PLAN[:m + 1]) for m, (name, _) in enumerate(PLAN)}
BEFORE["end"] = PARTS
PREVIOUS = dict(zip([name for name, _ in PLAN] + ["end"], [None] + [name for name, _ in PLAN]))


LN_STATS, LN_APPLY = "unit1_0", "unit1_2"

PIECE = 512
PIECES = [1, 1, 3, 3, 1, 3, 3] + 12 * [3]
POOLED = [k for k, pieces in enumerate(PIECES) if pieces > 1]
SPLITS = [("first", 2), ("fill0", 2), ("latent", 3), ("query0", 5), ("stack1", 4), ("scores0", 1),
          ("unit0_0", 1), ("unit0_4", 6), ("unit0_9", 3), ("unit0_10", 1), ("unit0_11", 2),
          ("fill1", 3), ("out0", 3), ("fill2", 2), ("kv1", 3), ("query2", 1), ("query3", 2),
          ("stack2", 1), ("stack3", 3), ("fill4", 1)]
PIECES_AT = {}
for name, pieces in SPLITS:
    done = sum(map(len, PIECES_AT.values()))
    PIECES_AT[name] = range(done, done + pieces)
PIECES_AT["end"] = range(sum(map(len, PIECES_AT.values())), sum(PIECES))
WEIGHTS_FOR = {"latent": 1, "kv": 2, "query0": 3, "out0": 4, "kv1": 5, "query2": 6, "out1": 7,
               "end": len(PIECES)}
CONDITION_AT, GAINS_AT = {"kv": 2, "stack0": 3}, "stack1"


def load_of(piece):
    return next(k for k in range(len(PIECES)) if piece < sum(PIECES[:k + 1]))


def parts_at(step):
    return range(BEFORE.get(PREVIOUS[step], 0), BEFORE[step])


def pairs_at(step, done):
    return [p for p in range(PAIRS) if 4 * p + done - 1 in parts_at(step)]


def tiles_at(step):
    return [t for t in range(TILES) if 4 * PAIRS + (t + 1) * PAIRS - 1 in parts_at(step)]


def count(n, per, k):
    i, off = n
    return off * per + k if i is None else i * per + (off * per + k)


def need(eng, sem, value):
    if isinstance(value, int) and value <= 0:
        return
    eng.wait_ge(sem, value)


def need_apart(eng, sem, value, met):
    if isinstance(value, int):
        need(eng, sem, value)
        return
    value = eng.to_reg(value)
    eng.wait_ge(*met)
    eng.wait_ge(sem, value)


def index(n):
    i, off = n
    return off if i is None else i + off


def before(n, use, uses):
    return (n, use - 2) if use >= 2 else ((n[0], n[1] - 1), use - 2 + uses)


def unit_heads(layer, u):
    if layer == 0:
        group, kind = divmod(u, 3)
        if kind == 0:
            return [(4 * group + j, 0, j * P, P) for j in range(4)]
        return [(4 * group + 2 * (kind - 1) + j, 1, 2 * j * P, K_TWO) for j in range(2)]
    pair, t = divmod(u, TILES)
    return [(2 * pair + j, t, j * TOK, TOK) for j in range(2)]


def build(nc, x, cond_t, pos_t, w_ada_t, b_ada_t, wq0_t, wkd_t, wku_t, wvu_t, wo0_t, ln1_w, tw1_t,
          ln2_w, tw2_t, wq1_t, wk1_t, wv1_t, wo1_t, wg_t, wu_t, wd_t, mask_c, rope0_c, freq_c,
          rope1, out):
    with ExitStack() as ctx:
        def sb(name, shape, dt=F32):
            return ctx.enter_context(nc.sbuf_tensor(name, shape, dt))

        def sem(name):
            return ctx.enter_context(nc.semaphore(name))

        def weight(name, chunks, cols):
            return tuple(sb(name + half, [P, chunks, cols], F16) for half in ("_hi", "_lo"))

        wkd = weight("wkd", CH, LAT)
        wkv0 = weight("wkv0", 1, 2 * KV0 * HD0)
        wq0 = weight("wq0", CH, D)
        wo0 = weight("wo0", CH, D)
        wkv1 = weight("wkv1", CH, 2 * HD1)
        wq1 = weight("wq1", CH, D)
        wo1 = weight("wo1", CH, D)
        wg = weight("wg", CH, FF)
        wu = weight("wu", CH, FF)
        wd = weight("wd", FCH, D)

        x_in = sb("x_in", [P, TILES, D])
        x_mid = sb("x_mid", [P, TILES, D])
        x_res = sb("x_res", [P, TILES, D])
        work = sb("work", [P, TILES, D])
        act_t = (sb("act_hi", [P, CH, TOK], F16), sb("act_lo", [P, CH, TOK], F16))
        mlp_t = (sb("mlp_hi", [P, CH, TOK], F16), sb("mlp_lo", [P, CH, TOK], F16))
        lat = (sb("lat_hi", [P, WINDOW + TOK], F16), sb("lat_lo", [P, WINDOW + TOK], F16))
        stack = sb("stack", [P, 2048], F16)
        q_t = sb("q_t", [P, H0, TOK], F16)
        k_t = sb("k_t", [P, KV0, P + WINDOW + P], F16)
        k0_t = k_t[0:ROWS0]
        v0 = (sb("v0_hi", [P, 3, P], F16), sb("v0_lo", [P, 3, P], F16))
        k1_t = k_t[:].rearrange("p g k -> p (g k)")[:, 0:2 * TOK].rearrange("p (a k) -> p a k", a=2)
        v1 = tuple(v[:, 0, :].rearrange("p (t d) -> p t d", t=TILES) for v in v0)
        prob = sb("prob", [P, 2, 512])
        prob_t = (sb("prob_hi", [P, 2, 512], F16), sb("prob_lo", [P, 2, 512], F16))
        low = sb("low", [P, 2, 4])
        sums0 = sb("sums0", [P, TILES, H0])
        sums1 = sb("sums1", [P, TILES, H1])
        inv = sb("inv", [P, TILES, H0])
        silu = sb("silu", [P, 512])
        inner = sb("inner", [P, 512])
        inner_t = sb("inner_t", [P, 2, FCH, TOK], F16)
        mask = sb("mask", [P, K_TWO])
        rope0 = sb("rope0", [P, 2, TILES, 2, HD0])
        rope1_sb = sb("rope1_sb", [P, TILES, TAB])
        ident = sb("ident", [P, P])
        ident16 = sb("ident16", [P, P], F16)
        bn = sb("bn", [P, TILES, 6])
        moments = sb("moments", [P, TILES, 2])
        squares = sb("squares", [P, TILES])
        ln_shifted, shifted = sb("ln_shifted", [P, TILES]), sb("shifted", [P, TILES])
        ln_rstd, rstd = sb("ln_rstd", [P, TILES]), sb("rstd", [P, TILES])
        minus_half = sb("minus_half", [P, TILES])
        gain0 = sb("gain0", [P, CH, SEQS])
        bias0 = sb("bias0", [P, CH, SEQS])
        gain1 = sb("gain1", [P, CH, SEQS])
        gain2 = sb("gain2", [P, CH, SEQS])
        b_ada = sb("b_ada", [P, 2 * CH])
        ln_w = sb("ln_w", [P, 2, CH])
        cond = silu[:, 0:CH * SEQS].rearrange("p (c s) -> p c s", c=CH)
        freq = silu[:, 64:64 + HD1 // 2]
        posf = silu[:, 128:128 + SEQS * TILES]
        pos = silu[:, 192:192 + SEQS * TILES].bitcast(I32)

        def bank(name):
            return ctx.enter_context(nc.psum_tensor(name, [P, 512], F32))

        score = [bank("score0"), bank("score1")]
        trans = [bank("trans0"), bank("trans1")]
        ybank = [bank("y0"), bank("y1")]
        gbank, ubank = bank("gate"), bank("up")
        mod = gbank[:, 0:4 * CH * SEQS].rearrange("p (m s) -> p m s", s=SEQS)

        stage = inner_t[:].rearrange("p a c t -> p (a c t)").bitcast(F32).rearrange(
            "p (s n) -> p s n", s=2)
        normed = stack[:].bitcast(F32).rearrange("p (t d) -> p t d", t=TILES)
        normed_t = work[:].rearrange("p t d -> p (t d)")
        k_stack0 = stack[:, 0:2 * KV0 * ROWS0].rearrange("p (g a d) -> p g a d", a=3, d=HD0)
        q_stack0 = stack[:, 0:H0 * ROWS0].rearrange("p (h a d) -> p h a d", a=3, d=HD0)
        k_stack1 = stack[:, 0:512].rearrange("p (t a d) -> p t a d", a=4, d=HD1)
        q_stack1 = [stack[:, at:at + 1024].rearrange("p (h a d) -> p h a d", a=2, d=HD1)
                    for at in (1024, 0)]
        turns = work[:].rearrange("p t d -> p (t d)")
        reduced = x_mid[:].rearrange("p t d -> p (t d)")
        free = q_t[:].rearrange("p h t -> p (h t)").bitcast(F32)
        angle, table = free[:, 0:512], free[:, 512:2048]
        dump = free[:, 0:TILES * D].rearrange("p (t d) -> p t d", t=TILES)

        raw_in = [sem("raw_in0"), sem("raw_in1")]
        cond_in, const_in, pos_in = sem("cond_in"), sem("const_in"), sem("pos_in")
        raw_high, raw_split, cond_used = sem("raw_high"), sem("raw_split"), sem("cond_used")
        pool_scaled, pool_split = sem("pool_scaled"), sem("pool_split")
        gains_made, ident_zero, ident_made = sem("gains_made"), sem("ident_zero"), sem("ident_made")
        half_made, prob_clear = sem("half_made"), sem("prob_clear")
        angle_step, angle_ready, sines, table_made, table_out = (
            sem("angle_step"), sem("angle_ready"), sem("sines"), sem("table_made"),
            sem("table_out"))
        x_arrived, rope_arrived, res_copied, out_stored = (
            sem("x_arrived"), sem("rope_arrived"), sem("res_copied"), sem("out_stored"))
        bn_raw, ln_stat, ln_eps_added, ln_rstd_ready, ln_ready = (
            sem("bn_raw"), sem("ln_stat"), sem("ln_eps_added"), sem("ln_rstd_ready"),
            sem("ln_ready"))
        square_sum, eps_added, rstd_ready = (
            sem("square_sum"), sem("eps_added"), sem("rstd_ready"))
        work_ready, t_full, t_free, hi_done, norm_high = (
            sem("work_ready"), sem("t_full"), sem("t_free"), sem("hi_done"), sem("norm_high"))
        s_full, lat_low, near_low, terms_made = (
            sem("s_full"), sem("lat_low"), sem("near_low"), sem("terms_made"))
        y_full, weighted = sem("y_full"), sem("weighted")
        lat_high, v_high = sem("lat_high"), sem("v_high")
        rope_terms, rope_sum, stack_high, stack_again, stack_low = (
            sem("rope_terms"), sem("rope_sum"), sem("stack_high"), sem("stack_again"),
            sem("stack_low"))
        low_ready, pv_done, inv_ready = sem("low_ready"), sem("pv_done"), sem("inv_ready")
        mid_ready = sem("mid_ready")
        g_full, u_full, tanh_done, gated, inner_ready, inner_high, inner_low, d_full, d_read = (
            sem("g_full"), sem("u_full"), sem("tanh_done"), sem("gated"), sem("inner_ready"),
            sem("inner_high"), sem("inner_low"), sem("d_full"), sem("d_read"))

        def wide(ap):
            return ap.rearrange("(c p) n -> p c n", p=P)

        loads, splits = [], []

        def raw_load(src):
            loads.append(([(src, CH, D, 0)], len(loads) - len(splits), False))

        def split(parts, target):
            loads.append((parts, len(splits), True))
            splits.append(target)

        for part in range(2):
            raw_load(wide(w_ada_t)[:, :, part * D:(part + 1) * D])
        split([(wide(wkd_t), CH, LAT, 0)], (wkd, 0, CH * LAT))
        split([(wku_t, 1, P, 0), (wvu_t, 1, P, P)], (wkv0, 0, 2 * P))
        split([(wide(wq0_t), CH, D, 0)], (wq0, 0, CH * D))
        split([(wide(wo0_t), CH, D, 0)], (wo0, 0, CH * D))
        split([(wide(wk1_t), CH, HD1, 0), (wide(wv1_t), CH, HD1, CH * HD1)], None)
        raw_load(wide(tw1_t))
        split([(wide(wq1_t), CH, D, 0)], (wq1, 0, CH * D))
        raw_load(wide(tw2_t))
        split([(wide(wo1_t), CH, D, 0)], (wo1, 0, CH * D))
        for w, w_t in ((wg, wg_t), (wu, wu_t)):
            for c in range(CH):
                split([(w_t[c * P:(c + 1) * P, :], 1, FF, 0)], (w, c * FF, FF))
        for c in range(CH):
            split([(wide(wd_t[c * D:(c + 1) * D, :]), CH, D, 0)], (wd, c * CH * D, CH * D))

        landed = []
        got = [0, 0]
        for m, (parts, _, _) in enumerate(loads):
            got[m % 2] += 16 * len(parts)
            landed.append((raw_in[m % 2], got[m % 2]))
        raws = [m for m, (_, _, is_split) in enumerate(loads) if not is_split]
        halved = [m for m, (_, _, is_split) in enumerate(loads) if is_split]

        def split_wait(eng, k):
            eng.wait_ge(raw_split, sum(PIECES[:k]))
            if POOLED[0] < k:
                eng.wait_ge(pool_split, sum(m < k for m in POOLED))

        def pooled_views(k):
            (hi, lo), at, n = splits[k]
            first = PIECES[k] * PIECE
            return stage[:, halved[k] % 2, first:n], *(
                w[:].rearrange("p c n -> p (c n)")[:, at + first:at + n] for w in (hi, lo))

        def split_views(piece, half):
            k = load_of(piece)
            slot = stage[:, halved[k] % 2, :]
            if splits[k] is None:
                n = CH * HD1
                return [(slot[:, j * n:(j + 1) * n].rearrange("p (c k) -> p c k", c=CH),
                         wkv1[half][:, :, j * HD1:(j + 1) * HD1]) for j in range(2)]
            w, at, n = splits[k]
            first = (piece - sum(PIECES[:k])) * PIECE
            last = min(first + PIECE, n)
            return [(slot[:, first:last],
                     w[half][:].rearrange("p c n -> p (c n)")[:, at + first:at + last])]

        rope_tab = rope1.rearrange("(s t) p n -> s p t n", t=TILES)
        x_dram = x.rearrange("s (t p) d -> s p t d", p=P)
        out_dram = out.rearrange("s (t p) d -> s p t d", p=P)

        block = ctx.enter_context(nc.Block())

        @block.sync
        def _(sp):
            sp.dma_start(cond, cond_t.rearrange("(c p) s -> p c s", p=P)).then_inc(cond_in, 16)
            sp.dma_start(b_ada[:], b_ada_t).then_inc(cond_in, 16)
            sp.dma_start(ln_w[:, 0, :], ln1_w).then_inc(cond_in, 16)
            sp.dma_start(ln_w[:, 1, :], ln2_w).then_inc(cond_in, 16)
            sp.dma_start(pos, pos_t).then_inc(pos_in, 16)
            sp.dma_start(freq, freq_c).then_inc(pos_in, 16)
            for m, (parts, k, is_split) in enumerate(loads):
                if m >= 2:
                    _, last, was_split = loads[m - 2]
                    if was_split:
                        split_wait(sp, last + 1)
                    else:
                        sp.wait_ge(cond_used, last + 1)
                for src, chunks, cols, at in parts:
                    dst = stage[:, m % 2, at:at + chunks * cols]
                    if chunks > 1:
                        dst = dst.rearrange("p (c n) -> p c n", c=chunks)
                    sp.dma_start(dst, src).then_inc(raw_in[m % 2], 16)
                if m == 1:
                    sp.dma_start(x_in[:], x_dram[0]).then_inc(x_arrived, 16)
                    sp.dma_start(mask[:], mask_c).then_inc(const_in, 16)
                    sp.dma_start(rope0[:].rearrange("p a t c d -> p (a t c d)"), rope0_c).then_inc(
                        const_in, 16)
                if is_split and k == 4:
                    sp.wait_ge(table_out, 32)
                    sp.dma_start(rope1_sb[:], rope_tab[0]).then_inc(rope_arrived, 16)

            def ahead(n, last=False):
                after = index((n[0], n[1] + (not last)))
                need_apart(sp, mid_ready, count(n, 4, 2), (cond_used, 1))
                sp.dma_start(x_in[:], x_dram[after]).then_inc(x_arrived, 16)
                if not last:
                    need_apart(sp, rope_sum, count(n, 6, 6), (cond_used, 1))
                    sp.dma_start(rope1_sb[:], rope_tab[after]).then_inc(rope_arrived, 16)

            def residual(n):
                need(sp, mid_ready, count(n, 4, 4))
                sp.dma_start(x_res[:], x_mid[:]).then_inc(res_copied, 16)

            def store(n):
                for t in range(TILES):
                    need_apart(sp, d_read, count(n, TILES, TILES + t + 1), (cond_used, 1))
                    sp.dma_start(out_dram[index(n)][:, t, :], x_res[:, t, :]).then_inc(
                        out_stored, 16)
                need_apart(sp, out_stored, count(n, 16 * TILES, 16 * TILES), (cond_used, 1))

            ahead((None, 0))
            with sp.Fori(0, SEQS - 2) as i:
                residual((i, 0))
                ahead((i, 1))
                store((i, 0))
            residual((None, SEQS - 2))
            ahead((None, SEQS - 1), last=True)
            store((None, SEQS - 2))
            residual((None, SEQS - 1))
            store((None, SEQS - 1))

        @block.gpsimd
        def _(pool):
            pool.memset(ident[:], 0.0).then_inc(ident_zero, 1)
            pool.memset(minus_half[:], -0.5).then_inc(half_made, 1)
            pool.memset(prob[:], 0.0).then_inc(prob_clear, 1)
            pool.wait_ge(ident_zero, 1)
            pool.affine_select(out=ident[:], in_=ident[:], compare_op=ALU.not_equal, fill=1.0,
                               base=0, pattern=[[-1, P]], channel_multiplier=1).then_inc(
                                   ident_made, 1)
            pool.wait_ge(ident_made, 1)
            pool.tensor_copy(ident16[:], ident[:]).then_inc(ident_made, 1)
            pool.wait_ge(half_made, 1)

            def ln_root(n):
                need_apart(pool, ln_stat, count(n, 2, 2), (half_made, 1))
                pool.tensor_scalar(ln_shifted[:], moments[:, :, 1], LN_EPS, 1.0, ALU.add,
                                   ALU.mult).then_inc(ln_eps_added, 1)
                need(pool, ln_eps_added, count(n, 1, 1))
                pool.tensor_tensor(ln_rstd[:], ln_shifted[:], minus_half[:], ALU.pow).then_inc(
                    ln_rstd_ready, 1)

            def root(n, k):
                need_apart(pool, square_sum, count(n, 4, 2 * k + 2), (half_made, 1))
                pool.tensor_scalar(shifted[:], squares[:], 1.0 / D, RMS_EPS, ALU.mult,
                                   ALU.add).then_inc(eps_added, 1)
                need(pool, eps_added, count(n, 2, k + 1))
                pool.tensor_tensor(rstd[:], shifted[:], minus_half[:], ALU.pow).then_inc(
                    rstd_ready, 1)

            def inner_lows(n, pairs):
                for p in pairs:
                    need(pool, inner_high, count(n, PAIRS, p + 1))
                    pair = inner_t[:, :, 2 * p:2 * p + 2, :].rearrange("p a c t -> p a (c t)")
                    pool.tensor_tensor(pair[:, 1, :], inner[:], pair[:, 0, :],
                                       ALU.subtract).then_inc(inner_low, 1)

            def layers(n, mlp):
                for step, _ in PLAN:
                    if step in ("fill2", "fill4"):
                        root(n, ("fill2", "fill4").index(step))
                    elif step == LN_STATS:
                        ln_root((n[0], n[1] + 1))
                    if mlp is not None:
                        inner_lows(mlp, pairs_at(step, 4))
                    else:
                        pieces(step)
                if mlp is None:
                    pieces("end")

            def pieces(step):
                for i, k in enumerate(POOLED):
                    if sum(PIECES[:k + 1]) - 1 in PIECES_AT.get(step, ()):
                        pool.wait_ge(*landed[halved[k]])
                        src, hi, lo = pooled_views(k)
                        pool.tensor_scalar(hi, src, WS, None, ALU.mult)
                        pool.tensor_scalar(src, src, WS, None, ALU.mult).then_inc(pool_scaled, 1)
                        pool.wait_ge(pool_scaled, i + 1)
                        pool.tensor_tensor(lo, src, hi, ALU.subtract).then_inc(pool_split, 1)

            ln_root((None, 0))
            layers((None, 0), None)
            with pool.Fori(0, SEQS - 1) as i:
                layers((i, 1), (i, 0))
            inner_lows((None, SEQS - 1), range(PAIRS))

        @block.scalar
        def _(act):
            def fill(n, f):
                for b in range(2):
                    use = T_FILL[f] + b
                    need(act, t_full, count(n, T_USES, use + 1))
                    for c in (2 * b, 2 * b + 1):
                        src = trans[use % 2][:, (c % 2) * TOK:(c % 2 + 1) * TOK]
                        at = index(n)
                        if f == 0:
                            ins = act.activation(
                                normed_t[:, c * TOK:(c + 1) * TOK], src, ACT.Identity,
                                scale=gain0[:, c, bass.ds(at, 1)],
                                bias=bias0[:, c, bass.ds(at, 1)])
                        elif f in (1, 3):
                            if c % 2 == 0:
                                both = act_t[0][:, c:c + 2, :].rearrange("p c t -> p (c t)")
                                act.activation(both, trans[use % 2][:], ACT.Copy).then_inc(
                                    hi_done, 1)
                            continue
                        else:
                            g, to = (gain1, act_t) if f == 2 else (gain2, mlp_t)
                            ins = act.activation(to[0][:, c, :], src, ACT.Copy,
                                                 scale=g[:, c, bass.ds(at, 1)])
                        if c % 2 == 1:
                            ins.then_inc(hi_done, 1)

            def exps(n, layer, u):
                base = 0 if layer == 0 else UNITS0
                need(act, low_ready, count(n, UNITS, base + u + 1))
                t_unit = T_UNIT0 if layer == 0 else T_UNIT1
                if u >= 2:
                    need(act, t_full, count(n, T_USES, t_unit + u - 1))
                bank_ = score[((S_UNIT0 if layer == 0 else S_UNIT1) + u) % 2]
                slot = prob[:, u % 2, :]
                for j, (h, t, at, wid) in enumerate(unit_heads(layer, u)):
                    sums = (sums0 if layer == 0 else sums1)[:, t, h:h + 1]
                    ins = act.activation(slot[:, at:at + wid], bank_[:, at:at + wid], ACT.Exp,
                                         bias=low[:, u % 2, j:j + 1], scale=-1.0, accum_out=sums)
                ins.then_inc(terms_made, 1)

            def prob_highs(n, layer, u):
                t_unit = T_UNIT0 if layer == 0 else T_UNIT1
                base = 0 if layer == 0 else UNITS0
                need(act, t_full, count(n, T_USES, t_unit + u + 1))
                need(act, pv_done, count(n, UNITS, base + u - 1))
                act.activation(prob_t[0][:, u % 2, :], trans[(t_unit + u) % 2][:],
                               ACT.Copy).then_inc(hi_done, 1)

            def layers(n, mlp):
                def ahead(step):
                    if mlp is not None:
                        tanhs(mlp, pairs_at(step, 2))
                    else:
                        weight_highs(step)
                        if step == "keys":
                            act.wait_ge(table_out, 32)
                        if step == "fill2":
                            act.wait_ge(gains_made, 4 * CH)

                def behind(step):
                    if mlp is not None:
                        inner_highs(mlp, pairs_at(step, 4))

                def units(layer):
                    total = UNITS0 if layer == 0 else UNITS1
                    ahead(f"scores{layer}")
                    exps(n, layer, 0)
                    behind(f"scores{layer}")
                    for u in range(total):
                        if u + 1 < total:
                            exps(n, layer, u + 1)
                        ahead(f"unit{layer}_{u}")
                        prob_highs(n, layer, u)
                        behind(f"unit{layer}_{u}")

                def stack_high_half(step, k, used, dst, src, again=None, scale=1.0):
                    need(act, rope_sum, count(n, 6, k))
                    if used:
                        need(act, t_full, count(n, T_USES, used))
                    act.activation(dst, src, ACT.Copy, scale=scale).then_inc(stack_high, 1)
                    if again is not None:
                        need(act, stack_high, count(n, 6, k))
                        act.activation(again, dst, ACT.Copy).then_inc(stack_again, 1)
                    ahead(step)
                    behind(step)

                def from_stack(use, copies):
                    need(act, t_full, count(n, T_USES, use + 1))
                    for to, at in copies:
                        ins = act.activation(to, at, ACT.Copy)
                    ins.then_inc(t_free, 1)

                def whole_fill(f):
                    ahead(f"fill{f}")
                    fill(n, f)
                    behind(f"fill{f}")

                whole_fill(0)
                ahead("latent")
                need(act, s_full, count(n, S_USES, S_LAT + 1))
                src = score[S_LAT % 2]
                act.activation(lat[0][:, WINDOW:], src[:, 0:TOK], ACT.Copy, scale=1.0 / WS)
                act.activation(lat[0][:, 0:WINDOW], src[:, P - WINDOW:P], ACT.Copy,
                               scale=1.0 / WS).then_inc(lat_high, 1)
                behind("latent")
                ahead("query0")
                behind("query0")
                ahead("kv")
                need(act, s_full, count(n, S_USES, S_KV + 1))
                kv = score[S_KV % 2][:].rearrange("p (t n) -> p t n", t=TILES)
                act.activation(v0[0][:, 0:TILES, :], kv[:, :, P:2 * P], ACT.Copy,
                               scale=1.0 / WS).then_inc(v_high, 1)
                need(act, s_full, count(n, S_USES, S_NEAR + 1))
                act.activation(v0[0][0:K_NEAR, 2, :], score[S_NEAR % 2][0:K_NEAR, 0:P], ACT.Copy,
                               scale=1.0 / WS).then_inc(v_high, 1)
                behind("kv")
                ahead("query1")
                behind("query1")
                stack_high_half("keys", 1, 0, k_stack0[:, :, 0, :],
                                work[:, 0, 0:2 * P].rearrange("p (g d) -> p g d", d=HD0),
                                k_stack0[:, :, 2, :])
                keys = trans[T_K0 % 2][0:ROWS0].bitcast(F16).rearrange(
                    "p (t g k) -> p t g k", t=TILES, g=KV0)
                from_stack(T_K0, [(k0_t[:, :, 0:P], keys[:, 1]),
                                  (k0_t[:, :, P:P + WINDOW], keys[:, 0, :, P - WINDOW:P]),
                                  (k0_t[:, :, P + WINDOW:], keys[:, 0])])
                for t in range(TILES):
                    stack_high_half(f"stack{t}", 2 + t, T_Q0 + 2 * t, q_stack0[:, :, 0, :],
                                    work[:, 0, :].rearrange("p (h d) -> p h d", d=HD0),
                                    q_stack0[:, :, 1, :])
                    for b in range(2):
                        use = T_Q0 + 2 * t + b
                        from_stack(use, [(q_t[0:ROWS0, 8 * b:8 * b + 8, t * P:(t + 1) * P],
                                          trans[use % 2][0:ROWS0].bitcast(F16).rearrange(
                                              "p (h q) -> p h q", h=8))])
                units(0)
                whole_fill(1)
                ahead("out0")
                square(n, 0)
                behind("out0")
                whole_fill(2)
                ahead("kv1")
                need(act, s_full, count(n, S_USES, S_KV1 + 1))
                kv = score[S_KV1 % 2][:, 0:TILES * P].rearrange("p (t n) -> p t n", t=TILES)
                act.activation(v1[0], kv[:, :, HD1:P], ACT.Copy, scale=1.0 / WS).then_inc(
                    v_high, 1)
                behind("kv1")
                for step in ("query2", "query3"):
                    ahead(step)
                    behind(step)
                stack_high_half("keys1", 4, 0, k_stack1[:, :, 0, :],
                                work[:, 0, 0:P].rearrange("p (t d) -> p t d", t=TILES),
                                k_stack1[:, :, 1, :])
                from_stack(T_K1, [(k1_t.rearrange("p a (t k) -> p a t k", t=TILES),
                                   trans[T_K1 % 2][:].bitcast(F16)[:, 0:4 * P].rearrange(
                                       "p (t a k) -> p a t k", t=TILES, a=2))])
                for t in range(TILES):
                    stack_high_half(f"stack{2 + t}", 5 + t, (T_K1 + 1) * t,
                                    q_stack1[t][:, :, 0, :],
                                    work[:, 0, :].rearrange("p (h d) -> p h d", d=HD1),
                                    scale=-float(HD1) ** -0.5)
                    use = T_Q1 + t
                    from_stack(use, [(q_t[:, 0:H1, t * P:(t + 1) * P],
                                      trans[use % 2][:].bitcast(F16).rearrange(
                                          "p (h q) -> p h q", h=H1))])
                units(1)
                whole_fill(3)
                ahead("out1")
                square(n, 1)
                behind("out1")
                whole_fill(4)
                ahead("end")
                behind("end")

            def square(n, k):
                for t in range(TILES):
                    need(act, mid_ready, count(n, 4, 2 * k + t + 1))
                    act.activation(dump[:, t, :], x_mid[:, t, :], ACT.Square,
                                   accum_out=squares[:, t:t + 1]).then_inc(square_sum, 1)

            def weight_highs(step):
                for piece in PIECES_AT.get(step, ()):
                    act.wait_ge(*landed[halved[load_of(piece)]])
                    for src, dst in split_views(piece, 0):
                        ins = act.activation(dst, src, ACT.Copy, scale=WS)
                    ins.then_inc(raw_high, 1)

            def tanhs(n, pairs):
                for p in pairs:
                    need(act, g_full, count(n, PAIRS, p + 1))
                    if p > 0:
                        need(act, inner_ready, count(n, PAIRS, p))
                    act.activation(silu[:], gbank[:], ACT.Tanh, scale=0.5 / WS).then_inc(
                        tanh_done, 1)

            def inner_highs(n, pairs):
                for p in pairs:
                    need(act, inner_ready, count(n, PAIRS, p + 1))
                    act.activation(inner_t[:, 0, 2 * p:2 * p + 2, :].rearrange("p c t -> p (c t)"),
                                   inner[:], ACT.Copy).then_inc(inner_high, 1)

            for half in range(2):
                if half == 1:
                    weight_highs("first")
                act.wait_ge(angle_ready, half + 1)
                act.activation(reduced, reduced, ACT.Sin).then_inc(sines, 1)
                act.wait_ge(table_made, half + 1)
                tiles = SEQS * TILES // 2
                act.dma_start(
                    rope1[half * tiles:(half + 1) * tiles].rearrange("t p n -> p t n"),
                    table.rearrange("p (t n) -> p t n", t=tiles)).then_inc(table_out, 16)
            act.wait_ge(gains_made, 2 * CH)
            act.wait_ge(prob_clear, 1)
            layers((None, 0), None)
            with act.Fori(0, SEQS - 1) as i:
                layers((i, 1), (i, 0))
            for p in range(PAIRS):
                tanhs((None, SEQS - 1), [p])
                inner_highs((None, SEQS - 1), [p])

        @block.vector
        def _(dve):
            def halves_low(n, f):
                for b in range(2):
                    need(dve, hi_done, count(n, HI_USES, HI_FILL[f] + b + 1))
                    if f == 0:
                        hi = act_t[0][:, 2 * b:2 * b + 2, :].rearrange("p c t -> p (c t)")
                        lo = act_t[1][:, 2 * b:2 * b + 2, :].rearrange("p c t -> p (c t)")
                        value = normed_t[:, b * 512:(b + 1) * 512]
                        dve.tensor_copy(hi, value).then_inc(norm_high, 1)
                        need(dve, norm_high, count(n, 2, b + 1))
                        dve.tensor_tensor(lo, value, hi, ALU.subtract).then_inc(
                            t_free, 1)
                    elif f in (1, 3):
                        hi = act_t[0][:, 2 * b:2 * b + 2, :].rearrange("p c t -> p (c t)")
                        lo = act_t[1][:, 2 * b:2 * b + 2, :].rearrange("p c t -> p (c t)")
                        dve.tensor_tensor(lo, trans[(T_FILL[f] + b) % 2][:], hi,
                                          ALU.subtract).then_inc(t_free, 1)
                    else:
                        g, to = (gain1, act_t) if f == 2 else (gain2, mlp_t)
                        for c in (2 * b, 2 * b + 1):
                            src = trans[(T_FILL[f] + b) % 2][:, (c % 2) * TOK:(c % 2 + 1) * TOK]
                            ins = dve.scalar_tensor_tensor(
                                to[1][:, c, :], src, g[:, c, bass.ds(index(n), 1)], to[0][:, c, :],
                                ALU.mult, ALU.subtract)
                        ins.then_inc(t_free, 1)

            def lows(n, layer, u):
                use = (S_UNIT0 if layer == 0 else S_UNIT1) + u
                need_apart(dve, s_full, count(n, S_USES, use + 1), (const_in, 32))
                bank_ = score[use % 2]
                if layer == 0:
                    for j, (h, t, at, wid) in enumerate(unit_heads(0, u)):
                        view = bank_[:, at:at + wid]
                        ins = dve.tensor_tensor_reduce(
                            out=view, in0=view, in1=mask[:, 0:wid], scale=1.0, scalar=3.0e38,
                            op0=ALU.add, op1=ALU.min, accum_out=low[:, u % 2, j:j + 1])
                else:
                    ins = dve.tensor_reduce(low[:, u % 2, 0:2], bank_[:].rearrange(
                        "p (h k) -> p h k", h=2), AX.X, ALU.min)
                ins.then_inc(low_ready, 1)

            def prob_lows(n, layer, u):
                t_unit = T_UNIT0 if layer == 0 else T_UNIT1
                need(dve, hi_done, count(n, HI_USES, HI_UNIT[layer] + u + 1))
                dve.tensor_tensor(prob_t[1][:, u % 2, :], trans[(t_unit + u) % 2][:],
                                  prob_t[0][:, u % 2, :], ALU.subtract).then_inc(t_free, 1)

            def between(mlp, step):
                if mlp is not None:
                    gates(mlp, pairs_at(step, 2))
                    inners(mlp, pairs_at(step, 4))
                    sums(mlp, tiles_at(step))
                else:
                    if step == GAINS_AT:
                        gains(1)
                    weight_lows(step)

            def units(n, mlp, layer):
                total = UNITS0 if layer == 0 else UNITS1
                between(mlp, f"scores{layer}")
                lows(n, layer, 0)
                lows(n, layer, 1)
                for u in range(total):
                    between(mlp, f"unit{layer}_{u}")
                    if f"unit{layer}_{u}" == LN_STATS:
                        ln_stats((n[0], n[1] + 1))
                    elif f"unit{layer}_{u}" == LN_APPLY:
                        ln_apply((n[0], n[1] + 1))
                    if u + 2 < total:
                        lows(n, layer, u + 2)
                    prob_lows(n, layer, u)

            def normalise(n, layer):
                sums, hd, heads = (sums0, HD0, H0) if layer == 0 else (sums1, HD1, H1)
                for t in range(TILES):
                    done = (UNITS0 - 2, UNITS0, UNITS - 1, UNITS)[2 * layer + t]
                    need(dve, pv_done, count(n, UNITS, done))
                    dve.reciprocal(inv[:, t, 0:heads], sums[:, t, :]).then_inc(inv_ready, 1)
                    need(dve, inv_ready, count(n, 4, 2 * layer + t + 1))
                    dve.tensor_tensor(
                        work[:, t, :].rearrange("p (h d) -> p h d", d=hd),
                        ybank[t][:].rearrange("p (h d) -> p h d", d=hd),
                        inv[:, t, 0:heads].unsqueeze(2).broadcast_to([P, heads, hd]),
                        ALU.mult).then_inc(weighted, 1)

            def add(n, layer):
                use = S_OUT0 if layer == 0 else S_OUT1
                if layer == 0:
                    need(dve, res_copied, count((n[0], n[1] - 1), 16, 16))
                for t in range(TILES):
                    need(dve, s_full, count(n, S_USES, use + t + 1))
                    src = x_in if layer == 0 else x_mid
                    dve.scalar_tensor_tensor(x_mid[:, t, :], score[(use + t) % 2][:], 1.0 / WS,
                                             src[:, t, :], ALU.mult, ALU.add).then_inc(mid_ready, 1)

            def rotate0(n, ps, q_or_k, t, heads, dst, swap, done):
                view = ps.rearrange("p (h two d) -> p h two d", two=2, d=HD0 // 2)
                for c, (src, to) in enumerate(((view, dst), (view[:, :, ::-1, :], swap))):
                    table = rope0[:, q_or_k, t, c, :].rearrange("p (two d) -> p two d", two=2)
                    ins = dve.tensor_tensor(
                        to.rearrange("p (h two d) -> p h two d", two=2, d=HD0 // 2), src,
                        table.unsqueeze(1).broadcast_to([P, heads, 2, HD0 // 2]), ALU.mult)
                if done is not None:
                    ins.then_inc(done, 1)

            def rotate1(n, ps, t, heads, dst, swap, done):
                half = HD1 // 2
                view = ps.rearrange("p (h two d) -> p h two d", two=2, d=half)
                cos = rope1_sb[:, t, 0:half].unsqueeze(1).unsqueeze(1).broadcast_to(
                    [P, heads, 2, half])
                sin = rope1_sb[:, t, half:].rearrange("p (two d) -> p two d", two=2).unsqueeze(
                    1).broadcast_to([P, heads, 2, half])
                for src, to, table in ((view, dst, cos), (view[:, :, ::-1, :], swap, sin)):
                    ins = dve.tensor_tensor(
                        to.rearrange("p (h two d) -> p h two d", two=2, d=half), src, table,
                        ALU.mult)
                if done is not None:
                    ins.then_inc(done, 1)

            def rope_add(n, k, size):
                need(dve, rope_terms, count(n, 6, k + 1))
                dve.tensor_tensor(work[:, 0, 0:size], work[:, 0, 0:size], work[:, 1, 0:size],
                                  ALU.add).then_inc(rope_sum, 1)
                need(dve, stack_high, count(n, 6, k + 1))

            def ln_stats(n):
                need(dve, x_arrived, count(n, 16, 16))
                for t in range(TILES):
                    dve.bn_stats(bn[:, t, :], x_in[:, t, :]).then_inc(bn_raw, 1)
                for t in range(TILES):
                    need_apart(dve, bn_raw, count(n, 2, t + 1), (const_in, 32))
                    dve.bn_aggr(moments[:, t, :], bn[:, t, :]).then_inc(ln_stat, 1)

            def ln_apply(n):
                need(dve, ln_rstd_ready, count(n, 1, 1))
                for t in range(TILES):
                    dve.tensor_scalar(normed[:, t, :], x_in[:, t, :], moments[:, t, 0:1],
                                      ln_rstd[:, t:t + 1], ALU.subtract, ALU.mult).then_inc(
                                          ln_ready, 1)

            def layer0(n, mlp):
                between(mlp, "fill0")
                halves_low(n, 0)
                between(mlp, "latent")
                need(dve, lat_high, count(n, 1, 1))
                src = score[S_LAT % 2]
                dve.scalar_tensor_tensor(lat[1][:, WINDOW:], src[:, 0:TOK], 1.0 / WS,
                                         lat[0][:, WINDOW:], ALU.mult, ALU.subtract)
                dve.scalar_tensor_tensor(lat[1][:, 0:WINDOW], src[:, P - WINDOW:P], 1.0 / WS,
                                         lat[0][:, 0:WINDOW], ALU.mult,
                                         ALU.subtract).then_inc(lat_low, 1)
                between(mlp, "query0")
                between(mlp, "kv")
                need(dve, v_high, count(n, 3, 1))
                kv = score[S_KV % 2][:].rearrange("p (t n) -> p t n", t=TILES)
                dve.scalar_tensor_tensor(v0[1][:, 0:TILES, :], kv[:, :, P:2 * P], 1.0 / WS,
                                         v0[0][:, 0:TILES, :], ALU.mult, ALU.subtract)
                for t in range(TILES):
                    rotate0(n, kv[:, t, 0:P], 1, t, KV0, work[:, 0, t * P:(t + 1) * P],
                            work[:, 1, t * P:(t + 1) * P],
                            None if t == 0 else rope_terms)
                need(dve, v_high, count(n, 3, 2))
                dve.scalar_tensor_tensor(v0[1][0:K_NEAR, 2, :], score[S_NEAR % 2][0:K_NEAR, 0:P],
                                         1.0 / WS, v0[0][0:K_NEAR, 2, :], ALU.mult,
                                         ALU.subtract).then_inc(near_low, 1)
                between(mlp, "query1")
                rope_add(n, 0, 2 * P)
                dve.tensor_tensor(k_stack0[:, :, 1, :], work[:, 0, 0:2 * P].rearrange(
                    "p (g d) -> p g d", d=HD0), k_stack0[:, :, 0, :], ALU.subtract).then_inc(
                        stack_low, 1)
                between(mlp, "keys")
                for t in range(TILES):
                    need(dve, y_full, count(n, 4, t + 1))
                    need(dve, stack_low, count(n, 6, 1 + t))
                    rotate0(n, ybank[t][:], 0, t, H0, work[:, 0, :], work[:, 1, :], rope_terms)
                    rope_add(n, 1 + t, D)
                    dve.tensor_tensor(q_stack0[:, :, 2, :], work[:, 0, :].rearrange(
                        "p (h d) -> p h d", d=HD0), q_stack0[:, :, 0, :], ALU.subtract).then_inc(
                            stack_low, 1)
                    between(mlp, f"stack{t}")
                units(n, mlp, 0)
                normalise(n, 0)
                between(mlp, "fill1")
                halves_low(n, 1)
                between(mlp, "out0")
                add(n, 0)

            def rms(n, k):
                need(dve, rstd_ready, count(n, 2, k))
                for t in range(TILES):
                    dve.tensor_scalar(work[:, t, :], x_mid[:, t, :], rstd[:, t:t + 1], None,
                                      ALU.mult).then_inc(work_ready, 1)

            def layer1(n, mlp):
                rms(n, 1)
                between(mlp, "fill2")
                halves_low(n, 2)
                between(mlp, "kv1")
                need(dve, v_high, count(n, 3, 3))
                kv = score[S_KV1 % 2][:, 0:TILES * P].rearrange("p (t n) -> p t n", t=TILES)
                dve.scalar_tensor_tensor(v1[1], kv[:, :, HD1:P], 1.0 / WS, v1[0], ALU.mult,
                                         ALU.subtract)
                need(dve, rope_arrived, count(n, 16, 16))
                for t in range(TILES):
                    rotate1(n, kv[:, t, 0:HD1], t, 1, work[:, 0, t * HD1:(t + 1) * HD1],
                            work[:, 1, t * HD1:(t + 1) * HD1], None if t == 0 else rope_terms)
                for step in ("query2", "query3"):
                    between(mlp, step)
                rope_add(n, 3, P)
                for a in (2, 3):
                    ins = dve.tensor_tensor(k_stack1[:, :, a, :], work[:, 0, 0:P].rearrange(
                        "p (t d) -> p t d", t=TILES), k_stack1[:, :, 0, :], ALU.subtract)
                ins.then_inc(stack_low, 1)
                between(mlp, "keys1")
                for t in range(TILES):
                    need(dve, y_full, count(n, 4, 2 + t + 1))
                    need(dve, stack_low, count(n, 6, 4 + t))
                    rotate1(n, ybank[t][:], t, H1, work[:, 0, :], work[:, 1, :], rope_terms)
                    rope_add(n, 4 + t, D)
                    dve.scalar_tensor_tensor(
                        q_stack1[t][:, :, 1, :], work[:, 0, :].rearrange("p (h d) -> p h d", d=HD1),
                        -float(HD1) ** -0.5, q_stack1[t][:, :, 0, :], ALU.mult,
                        ALU.subtract).then_inc(stack_low, 1)
                    between(mlp, f"stack{2 + t}")
                units(n, mlp, 1)
                normalise(n, 1)
                between(mlp, "fill3")
                halves_low(n, 3)
                between(mlp, "out1")
                add(n, 1)
                rms(n, 2)
                between(mlp, "fill4")
                halves_low(n, 4)
                between(mlp, "end")

            def gains(layer):
                dve.wait_ge(cond_used, 2 * layer + 2)
                dve.wait_ge(cond_in, 64)
                for c in range(CH):
                    for k in range(2):
                        src = mod[:, (2 * layer + k) * CH + c, :]
                        bias = b_ada[:, k * CH + c:k * CH + c + 1]
                        if layer == 1:
                            ins = dve.tensor_scalar((gain1, gain2)[k][:, c, :], src, 1.0,
                                                    ln_w[:, k, c:c + 1], ALU.add, ALU.mult)
                        elif k == 0:
                            ins = dve.tensor_scalar(gain0[:, c, :], src, bias, 1.0, ALU.add,
                                                    ALU.add)
                        else:
                            ins = dve.tensor_scalar(bias0[:, c, :], src, bias, None, ALU.add)
                        ins.then_inc(gains_made, 1)
                if layer == 1:
                    dve.wait_ge(gains_made, 4 * CH)

            def weight_lows(step):
                for piece in PIECES_AT.get(step, ()):
                    dve.wait_ge(raw_high, piece + 1)
                    for (src, dst), (_, hi) in zip(split_views(piece, 1), split_views(piece, 0)):
                        ins = dve.scalar_tensor_tensor(dst, src, WS, hi, ALU.mult, ALU.subtract)
                    ins.then_inc(raw_split, 1)

            def gates(n, pairs):
                for p in pairs:
                    need(dve, tanh_done, count(n, PAIRS, p + 1))
                    dve.scalar_tensor_tensor(silu[:], silu[:], 1.0, gbank[:], ALU.add,
                                             ALU.mult).then_inc(gated, 1)

            def inners(n, pairs):
                for p in pairs:
                    need(dve, u_full, count(n, PAIRS, p + 1))
                    need(dve, gated, count(n, PAIRS, p + 1))
                    if p > 0:
                        need(dve, inner_high, count(n, PAIRS, p))
                        need(dve, inner_low, count(n, PAIRS, p))
                    dve.scalar_tensor_tensor(inner[:], ubank[:], 0.5 * HS / (WS * WS), silu[:],
                                             ALU.mult, ALU.mult).then_inc(inner_ready, 1)

            def sums(n, tiles):
                for t in tiles:
                    need(dve, res_copied, count(n, 16, 16))
                    need(dve, d_full, count(n, TILES, t + 1))
                    dve.scalar_tensor_tensor(x_res[:, t, :], (gbank, ubank)[t][:],
                                             1.0 / (WS * HS), x_res[:, t, :], ALU.mult,
                                             ALU.add).then_inc(d_read, 1)

            steps = [0]

            def step(ins):
                steps[0] += 1
                ins.then_inc(angle_step, 1)
                dve.wait_ge(angle_step, steps[0])

            tiles = SEQS * TILES // 2
            dve.wait_ge(pos_in, 32)
            step(dve.tensor_copy(posf, pos))
            for half in range(2):
                if half == 1:
                    dve.wait_ge(const_in, 32)
                    ln_stats((None, 0))
                    ln_apply((None, 0))
                step(dve.tensor_tensor(
                    angle.rearrange("p (t f) -> p t f", t=tiles),
                    posf[:, half * tiles:(half + 1) * tiles].unsqueeze(2).broadcast_to(
                        [P, tiles, HD1 // 2]),
                    freq.unsqueeze(1).broadcast_to([P, tiles, HD1 // 2]), ALU.mult))
                for c in range(2):
                    if half == 1 and c == 1:
                        weight_lows("first")
                    t_c = turns[:, c * 512:(c + 1) * 512]
                    r_c = reduced[:, c * 512:(c + 1) * 512]
                    step(dve.tensor_scalar(t_c, angle, 1.0 / (2 * np.pi), 0.25 * (1 - c), ALU.mult,
                                           ALU.add))
                    step(dve.tensor_scalar(t_c, t_c, ROUND, None, ALU.add))
                    step(dve.tensor_scalar(t_c, t_c, -ROUND, None, ALU.add))
                    step(dve.scalar_tensor_tensor(r_c, t_c, -TWO_PI_1, angle, ALU.mult, ALU.add))
                    step(dve.scalar_tensor_tensor(r_c, t_c, -TWO_PI_2, r_c, ALU.mult, ALU.add))
                    step(dve.scalar_tensor_tensor(r_c, t_c, -TWO_PI_3, r_c, ALU.mult, ALU.add))
                    if c == 0:
                        step(dve.tensor_scalar(r_c, r_c, float(np.pi / 2), None, ALU.add))
                dve.tensor_scalar(reduced, reduced, PI_IN, -PI_IN, ALU.min, ALU.max).then_inc(
                    angle_ready, 1)
                dve.wait_ge(sines, half + 1)
                if half == 1:
                    dve.wait_ge(table_out, 16)
                tab = table.rearrange("p (t n) -> p t n", t=tiles)
                f = HD1 // 2
                for at, c, sign in ((0, 0, 1.0), (f, 1, -1.0), (2 * f, 1, 1.0)):
                    ins = dve.tensor_scalar(
                        tab[:, :, at:at + f],
                        reduced[:, c * 512:(c + 1) * 512].rearrange("p (t f) -> p t f", t=tiles),
                        sign / WS, None, ALU.mult)
                ins.then_inc(table_made, 1)
            gains(0)
            dve.sem_inc(d_read, TILES)
            layer0((None, 0), None)
            layer1((None, 0), None)
            with dve.Fori(0, SEQS - 1) as i:
                layer0((i, 1), (i, 0))
                layer1((i, 1), (i, 0))
            for p in range(PAIRS):
                gates((None, SEQS - 1), [p])
                inners((None, SEQS - 1), [p])
            sums((None, SEQS - 1), range(TILES))

        @block.tensor
        def _(pe):
            def product(out_ap, left, right, start=True, stop=True):
                pe.matmul(out_ap, left[0], right[0], start=start, stop=False)
                pe.matmul(out_ap, left[0], right[1], start=False, stop=False)
                return pe.matmul(out_ap, left[1], right[0], start=False, stop=stop)

            def cut(pair, *at):
                return pair[0][at], pair[1][at]

            def events():
                return {"lat_low": lat_low, "rope_terms": rope_terms, "near_low": near_low,
                        "terms_made": terms_made, "mid_ready": mid_ready}

            def score_bank(n, use):
                m, last = before(n, use, S_USES)
                name, per, k = S_READ[last]
                need(pe, events()[name], count(m, per, k))
                return score[use % 2]

            def trans_bank(n, use):
                m, last = before(n, use, T_USES)
                need(pe, t_free, count(m, T_USES, last + 1))
                return trans[use % 2]

            def fill(n, f):
                for b in range(2):
                    bank_ = trans_bank(n, T_FILL[f] + b)
                    for t in range(TILES):
                        if b == 0:
                            if f in (1, 3):
                                need(pe, weighted, count(n, 4, f - 1 + t + 1))
                            elif f == 0:
                                need(pe, ln_ready, count(n, 2, t + 1))
                            else:
                                need(pe, work_ready, count(n, 4, f - 2 + t + 1))
                        src = work if f else normed
                        for c in (2 * b, 2 * b + 1):
                            ins = pe.transpose(bank_[:, (c % 2) * TOK + t * P:][:, 0:P],
                                               src[:, t, c * P:(c + 1) * P], ident[:])
                    ins.then_inc(t_full, 1)

            def token_major(out_ap, src, t, w, cols):
                for c in range(CH):
                    ins = product(out_ap, cut(src, slice(None), c, slice(t * P, (t + 1) * P)),
                                  cut(w, slice(None), c, slice(0, cols)), c == 0, c == CH - 1)
                return ins

            def queries(n, layer, t, w):
                if layer == 0:
                    need(pe, weighted, count((n[0], n[1] - 1), 4, 2 + t + 1))
                else:
                    need(pe, weighted, count(n, 4, t + 1))
                token_major(ybank[t][:], act_t, t, w, D).then_inc(y_full, 1)

            def stacks(n, use, k, again, rows, at, heads):
                bank_ = trans_bank(n, use)[0:rows].bitcast(F16)
                need(pe, stack_low, count(n, 6, k))
                if again:
                    need(pe, stack_again, count(n, 4, again))
                for m in range(heads):
                    ins = pe.transpose(bank_[:, m * P:(m + 1) * P],
                                       stack[:, at + m * rows:at + (m + 1) * rows], ident16[:])
                ins.then_inc(t_full, 1)

            placed = [{0: T_Q0 + 1, 1: T_Q0 + 3, 7: T_Q0 + 4}, {0: T_Q1 + 1, 1: T_Q1 + 2}]

            def unit_scores(n, layer, u):
                if u in placed[layer]:
                    need(pe, t_free, count(n, T_USES, placed[layer][u]))
                bank_ = score_bank(n, (S_UNIT0 if layer == 0 else S_UNIT1) + u)
                for h, t, at, wid in unit_heads(layer, u):
                    q = q_t[0:(ROWS0, P)[layer], h, t * P:(t + 1) * P]
                    if layer == 0:
                        first = 0 if t else P + WINDOW
                        ins = pe.matmul(bank_[:, at:at + wid], q,
                                        k0_t[:, h // (H0 // KV0), first:first + wid], start=True,
                                        stop=True)
                    else:
                        pe.matmul(bank_[:, at:at + wid], q, k1_t[:, 0, :], start=True, stop=False)
                        ins = pe.matmul(bank_[:, at:at + wid], q, k1_t[:, 1, :], start=False,
                                        stop=True)
                ins.then_inc(s_full, 1)

            def unit_transposes(n, layer, u):
                need(pe, terms_made, count(n, UNITS, layer * UNITS0 + u + 1))
                bank_ = trans_bank(n, (T_UNIT0 if layer == 0 else T_UNIT1) + u)
                for b in range(4):
                    ins = pe.transpose(bank_[:, b * P:(b + 1) * P],
                                       prob[:, u % 2, b * P:(b + 1) * P], ident[:])
                ins.then_inc(t_full, 1)

            def unit_values(n, layer, u):
                need(pe, t_free, count(n, T_USES, (T_UNIT0 if layer == 0 else T_UNIT1) + u + 1))
                for h, t, at, wid in unit_heads(layer, u):
                    if layer == 0:
                        if h == 0:
                            need(pe, rope_terms, count(n, 6, 1 + t + 1))
                        g = h // (H0 // KV0)
                        out_ap = ybank[t][:, h * HD0:(h + 1) * HD0]
                        blocks = [(at, P, 0)] if t == 0 else [(at, P, 1), (at + P, K_NEAR, 2)]
                        for m, (col, rows, tile) in enumerate(blocks):
                            ins = product(
                                out_ap, cut(prob_t, slice(0, rows), u % 2, slice(col, col + P)),
                                cut(v0, slice(0, rows), tile, slice(g * HD0, (g + 1) * HD0)),
                                m == 0, m == len(blocks) - 1)
                    else:
                        if h == 0:
                            need(pe, rope_terms, count(n, 6, 4 + t + 1))
                        out_ap = ybank[t][:, h * HD1:(h + 1) * HD1]
                        for m in range(TILES):
                            ins = product(
                                out_ap,
                                cut(prob_t, slice(None), u % 2, slice(at + m * P, at + m * P + P)),
                                cut(v1, slice(None), m, slice(None)), m == 0, m == TILES - 1)
                ins.then_inc(pv_done, 1)

            def units(n, mlp, layer):
                total = UNITS0 if layer == 0 else UNITS1
                between(mlp, f"scores{layer}")
                unit_scores(n, layer, 0)
                unit_scores(n, layer, 1)
                for u in range(total):
                    between(mlp, f"unit{layer}_{u}")
                    if u + 2 < total:
                        unit_scores(n, layer, u + 2)
                    unit_transposes(n, layer, u)
                    if u > 0:
                        unit_values(n, layer, u - 1)
                unit_values(n, layer, total - 1)

            def project(n, layer, w):
                for t in range(TILES):
                    bank_ = score_bank(n, (S_OUT0 if layer == 0 else S_OUT1) + t)
                    if t == 0:
                        need(pe, t_free, count(n, T_USES, T_FILL[1 if layer == 0 else 3] + 2))
                    token_major(bank_[:], act_t, t, w, D).then_inc(s_full, 1)

            def layer0(n, mlp):
                between(mlp, "fill0")
                fill(n, 0)
                between(mlp, "latent")
                bank_ = score_bank(n, S_LAT)
                for c in range(CH):
                    if c % 2 == 0:
                        need(pe, t_free, count(n, T_USES, T_FILL[0] + c // 2 + 1))
                    ins = product(bank_[:, 0:TOK], cut(wkd, slice(None), c, slice(None)),
                                  cut(act_t, slice(None), c, slice(None)), c == 0, c == CH - 1)
                ins.then_inc(s_full, 1)
                between(mlp, "query0")
                queries(n, 0, 0, wq0)
                between(mlp, "kv")
                bank_ = score_bank(n, S_KV)
                need(pe, lat_low, count(n, 1, 1))
                for t in range(TILES):
                    ins = product(bank_[:, t * TOK:(t + 1) * TOK],
                                  cut(lat, slice(None), slice(WINDOW + t * P, WINDOW + t * P + P)),
                                  cut(wkv0, slice(None), 0, slice(None)))
                ins.then_inc(s_full, 1)
                bank_ = score_bank(n, S_NEAR)
                product(bank_[0:K_NEAR, 0:P], cut(lat, slice(None), slice(0, K_NEAR)),
                        cut(wkv0, slice(None), 0, slice(P, 2 * P))).then_inc(s_full, 1)
                between(mlp, "query1")
                queries(n, 0, 1, wq0)
                between(mlp, "keys")
                stacks(n, T_K0, 1, 1, ROWS0, 0, TILES * KV0)
                for t in range(TILES):
                    between(mlp, f"stack{t}")
                    for b in range(2):
                        stacks(n, T_Q0 + 2 * t + b, 2 + t, 2 + t, ROWS0, 8 * b * ROWS0, 8)
                units(n, mlp, 0)
                between(mlp, "fill1")
                fill(n, 1)
                between(mlp, "out0")
                project(n, 0, wo0)

            def layer1(n, mlp):
                between(mlp, "fill2")
                fill(n, 2)
                between(mlp, "kv1")
                bank_ = score_bank(n, S_KV1)
                need(pe, t_free, count(n, T_USES, T_FILL[2] + 2))
                for t in range(TILES):
                    ins = token_major(bank_[:, t * P:(t + 1) * P], act_t, t, wkv1, P)
                ins.then_inc(s_full, 1)
                for t in range(TILES):
                    between(mlp, f"query{2 + t}")
                    queries(n, 1, t, wq1)
                between(mlp, "keys1")
                stacks(n, T_K1, 4, 4, P, 0, 2 * TILES)
                for t, at in enumerate((1024, 0)):
                    between(mlp, f"stack{2 + t}")
                    stacks(n, T_Q1 + t, 5 + t, 0, P, at, H1)
                units(n, mlp, 1)
                between(mlp, "fill3")
                fill(n, 3)
                between(mlp, "out1")
                project(n, 1, wo1)
                between(mlp, "fill4")
                fill(n, 4)
                between(mlp, "end")

            def mlp_part(n, part):
                if part < 4 * PAIRS:
                    p, kind, m = part // 4, part // 2 % 2, part % 2
                    w, bank_, full, read = ((wg, gbank, g_full, gated),
                                            (wu, ubank, u_full, inner_ready))[kind]
                    if part == 0:
                        need(pe, t_free, count(n, T_USES, T_USES))
                    if m == 0:
                        if p > 0:
                            need(pe, read, count(n, PAIRS, p))
                        else:
                            need(pe, d_read, count(n, TILES, 1 + kind))
                    f = 2 * p + m
                    for c in range(CH):
                        ins = product(bank_[:, m * TOK:(m + 1) * TOK],
                                      cut(w, slice(None), c, slice(f * P, (f + 1) * P)),
                                      cut(mlp_t, slice(None), c, slice(None)), c == 0, c == CH - 1)
                    if m == 1:
                        ins.then_inc(full, 1)
                    return
                t, j = divmod(part - 4 * PAIRS, PAIRS)
                if t == 0:
                    if j == 0:
                        need(pe, gated, count(n, PAIRS, PAIRS))
                    need(pe, inner_high, count(n, PAIRS, j + 1))
                    need(pe, inner_low, count(n, PAIRS, j + 1))
                elif j == 0:
                    need(pe, inner_ready, count(n, PAIRS, PAIRS))
                cols = slice(t * P, (t + 1) * P)
                for f in (2 * j, 2 * j + 1):
                    ins = product((gbank, ubank)[t][:],
                                  (inner_t[:, 0, f, cols], inner_t[:, 1, f, cols]),
                                  cut(wd, slice(None), f, slice(None)), f == 0, f == FCH - 1)
                if j == PAIRS - 1:
                    ins.then_inc(d_full, 1)

            def between(mlp, step):
                if mlp is not None:
                    for part in parts_at(step):
                        mlp_part(mlp, part)
                    return
                if step in CONDITION_AT:
                    conditioning(CONDITION_AT[step])
                if step in WEIGHTS_FOR:
                    split_wait(pe, WEIGHTS_FOR[step])

            def conditioning(k):
                pe.wait_ge(*landed[raws[k]])
                slot = stage[:, raws[k] % 2, :].rearrange("p (c n) -> p c n", c=CH)
                for j in range(CH):
                    for c in range(CH):
                        ins = pe.matmul(mod[:, k * CH + j, :], slot[:, c, j * P:(j + 1) * P],
                                        cond[:, c, :], start=c == 0, stop=c == CH - 1)
                ins.then_inc(cond_used, 1)

            pe.wait_ge(cond_in, 64)
            conditioning(0)
            conditioning(1)
            pe.wait_ge(ident_made, 2)
            layer0((None, 0), None)
            layer1((None, 0), None)
            with pe.Fori(0, SEQS - 1) as i:
                layer0((i, 1), (i, 0))
                layer1((i, 1), (i, 0))
            for part in range(PARTS):
                mlp_part((None, SEQS - 1), part)


def key_mask():
    q = np.arange(P)[:, None]
    own = np.arange(P)[None, :]
    own_ok = (np.abs(q - own) <= WINDOW) | (own % GLOBAL == 0)
    near = np.arange(P - WINDOW, P)[None, :]
    near_ok = (q + P - near <= WINDOW) | (near % GLOBAL == 0)
    ok = np.concatenate([own_ok, near_ok, np.ones((P, 1), bool)], axis=1)
    return np.where(ok, 0.0, NEG).astype(np.float32)


def frequencies(width):
    f = np.float32(1.0) / np.float32(10000.0) ** (np.arange(0, width, 2, dtype=np.float32)
                                                  / np.float32(width))
    return f.astype(np.float32)


def rope_table0():
    angle = np.arange(TOK, dtype=np.float32)[:, None] * frequencies(HD0)[None, :]
    cos, sin = np.cos(angle.astype(np.float64)), np.sin(angle.astype(np.float64))
    one = np.stack([np.concatenate([cos, cos], 1), np.concatenate([-sin, sin], 1)], 1)
    both = np.stack([one * (-(HD0 ** -0.5) / WS), one / WS])
    both = both.reshape(2, TILES, P, 2, HD0).transpose(2, 0, 1, 3, 4)
    return np.ascontiguousarray(both.reshape(P, -1).astype(np.float32))


def kernel(**inputs):
    import concourse.bacc as bacc
    from concourse.bass_utils import run_bass_kernel_spmd

    def get(name):
        return np.asarray(inputs[name])

    def turned(name):
        return np.ascontiguousarray(get(name).T)

    def by_feature(v):
        return np.ascontiguousarray(v.reshape(-1, P).T)

    arrays = {
        "x": np.ascontiguousarray(get("x")),
        "cond_t": turned("cond_2048"),
        "pos_t": np.ascontiguousarray(get("pos_BxS").reshape(SEQS * TILES, P).T),
        "w_ada_t": turned("L0_cond_W_ada"), "b_ada_t": by_feature(get("L0_cond_b_ada")),
        "wq0_t": turned("L0_cond_Wq"), "wkd_t": turned("L0_cond_Wkd"),
        "wku_t": turned("L0_cond_Wku"), "wvu_t": turned("L0_cond_Wvu"),
        "wo0_t": turned("L0_cond_Wo"),
        "ln1_w": by_feature(get("L1_cond_ln1_w")), "tw1_t": turned("L1_cond_ln1_tw"),
        "ln2_w": by_feature(get("L1_cond_ln2_w")), "tw2_t": turned("L1_cond_ln2_tw"),
        "wq1_t": turned("L1_cond_Wq"), "wk1_t": turned("L1_cond_Wk"),
        "wv1_t": turned("L1_cond_Wv"), "wo1_t": turned("L1_cond_Wo"),
        "wg_t": turned("L1_cond_Wg"), "wu_t": turned("L1_cond_Wu"), "wd_t": turned("L1_cond_Wd"),
        "mask_c": key_mask(), "rope0_c": rope_table0(),
        "freq_c": np.ascontiguousarray(np.broadcast_to(frequencies(HD1), (P, HD1 // 2))),
    }
    nc = bacc.Bacc("TRN2", target_bir_lowering=False, num_devices=1)
    args = {name: nc.dram_tensor(name + "_dram", a.shape, mybir.dt.from_np(a.dtype),
                                 kind="ExternalInput").ap() for name, a in arrays.items()}
    args["rope1"] = nc.dram_tensor("rope1_dram", (SEQS * TILES, P, TAB), F32, kind="Internal").ap()
    args["out"] = nc.dram_tensor("out_dram", (SEQS, TOK, D), F32, kind="ExternalOutput").ap()
    build(nc, **args)
    result = run_bass_kernel_spmd(nc, [{name + "_dram": a for name, a in arrays.items()}],
                                  core_ids=[0])
    return result.results[0]["out_dram"]
```
